# Optimizing a Trainium2 kernel written in Bass

```python
import numpy as np
import jax
import jax.numpy as jnp

def _softmax(x, axis=-1):
    return jax.nn.softmax(x, axis=axis)

def _gelu(x):
    return jax.nn.gelu(x, approximate=True)

def _silu(x):
    return jax.nn.silu(x)

def _sigmoid(x):
    return jax.nn.sigmoid(x)

def _layernorm(x, axis=-1, eps=1e-05):
    m = jnp.mean(x, axis=axis, keepdims=True)
    v = jnp.var(x, axis=axis, keepdims=True)
    return (x - m) / jnp.sqrt(v + eps)

def _scatter_add(tgt, idx, src, axis=0):
    return tgt.at[idx].add(src)

def _segment_sum(src, seg, n):
    return jax.ops.segment_sum(src, seg, n)
kernel_name = 'mk_pixart_resid_d2_seqx_r8_166433'

def setup_inputs(seed: int=0):
    np.random.seed(seed)
    _w = jnp.asarray

    def _rec_inputs():
        import jax
        import jax.numpy as jnp
        _rk = jax.random.key(seed)
        x = 7.22e-05 + 1 * jax.random.normal(jax.random.fold_in(_rk, 1), (64, 64, 128), jnp.float32)
        _lenS = 64 - jax.random.randint(jax.random.fold_in(_rk, 7), (64,), 0, max(1, 64 // 4) + 1, jnp.int32)
        _lenS2 = 64 - jax.random.randint(jax.random.fold_in(_rk, 8), (64,), 0, max(1, 64 // 4) + 1, jnp.int32)
        cond_1024 = -0.00493535 + 1.00056 * jax.random.normal(jax.random.fold_in(_rk, 11), (64, 128), jnp.float32)
        _ctx_1024P = jax.random.normal(jax.random.fold_in(_rk, 12), (64, 16, 128), jnp.float32)
        _ctx_1024c = jax.random.dirichlet(jax.random.fold_in(_rk, 512), 0.3 * jnp.ones((16,), jnp.float32), (64, 64))
        _ctx_1024t = jnp.einsum('bsk,bkd->bsd', _ctx_1024c, _ctx_1024P)
        _ctx_1024t = _ctx_1024t * jax.lax.rsqrt(jnp.mean(jnp.square(_ctx_1024t)) + 1e-12) * 0.953939
        ctx_1024 = 0.000121155 + 1.00018 * (_ctx_1024t + 0.3 * jax.random.normal(jax.random.fold_in(_rk, 612), (64, 64, 128), jnp.float32))
        return (x, cond_1024, ctx_1024)
    x, cond_1024, ctx_1024 = _rec_inputs()

    def _L0_xcond_setup():
        import jax, jax.numpy as jnp
        import numpy as np
        B, T, H, L = (64, 128, 128, 64)
        key = jax.random.key(seed)
        ks = jax.random.split(key, 12)
        s_attn = 1.0 / np.sqrt(2 * H)
        s_h = 1.0 / np.sqrt(H)
        return {'decode_input': jax.random.normal(ks[0], (B, T, H), jnp.float32), 'decode_hidden': jax.random.normal(ks[1], (B, H), jnp.float32), 'encode_outputs': jax.random.normal(ks[2], (B, L, H), jnp.float32), 'W_attn': jax.random.uniform(ks[3], (L, 2 * H), jnp.float32, -s_attn, s_attn), 'b_attn': jax.random.uniform(ks[4], (L,), jnp.float32, -s_attn, s_attn), 'W_comb': jax.random.uniform(ks[5], (H, 2 * H), jnp.float32, -s_attn, s_attn), 'b_comb': jax.random.uniform(ks[6], (H,), jnp.float32, -s_attn, s_attn), 'W_ih': jax.random.uniform(ks[7], (H, H), jnp.float32, -s_h, s_h), 'b_ih': jax.random.uniform(ks[8], (H,), jnp.float32, -s_h, s_h), 'W_hh': jax.random.uniform(ks[9], (H, H), jnp.float32, -s_h, s_h), 'b_hh': jax.random.uniform(ks[10], (H,), jnp.float32, -s_h, s_h), 'W_out': jax.random.uniform(ks[11], (H, H), jnp.float32, -s_h, s_h), 'b_out': jnp.zeros((H,), jnp.float32)}
    _L0_xcond_all = _L0_xcond_setup()
    _L0_xcond_in = {k: v for k, v in _L0_xcond_all.items() if k in ('W_attn', 'b_attn', 'W_comb', 'b_comb', 'W_ih', 'b_ih', 'W_hh', 'b_hh', 'W_out', 'b_out')}
    del _L0_xcond_all

    def _L0_ffn_setup():
        import jax, jax.numpy as jnp
        import numpy as np
        E = 16
        K = 2
        LOAD = 1.0

        def _dispatch(xb, pb, cap):
            T, C = xb.shape
            top_k_probs, ei = jax.lax.top_k(pb, K)
            flat = ei.swapaxes(0, 1).ravel()
            one_hot = jax.nn.one_hot(flat, E, dtype=jnp.int32)
            pos = jnp.cumsum(one_hot, axis=0) * one_hot
            pos = pos.reshape(K, T, E).swapaxes(0, 1)
            pos = jnp.max(pos, axis=-1) - 1
            ei2 = flat.reshape(K, T).swapaxes(0, 1)
            xr = jnp.repeat(xb, K, axis=0)
            buf = jnp.zeros((E, cap, C), xb.dtype)
            buf = buf.at[ei2.ravel(), pos.ravel()].set(xr, mode='drop')
            return (top_k_probs, pos, ei2, buf)

        def _collect(eo_b, ei_b, pos_b, tk_b):
            out = eo_b[ei_b, pos_b]
            return jnp.sum(tk_b[..., None] * out, axis=1)
        key = jax.random.key(seed)
        k1, k2, k3, k4, k5 = jax.random.split(key, 5)
        B, T, C, H = (8, 512, 128, 64)
        n_layer = 12
        x = jax.random.normal(k1, (B, T, C), dtype=jnp.float32)
        w_router = jax.random.normal(k2, (C, E), dtype=jnp.float32) * 0.02
        w_fc = jax.random.normal(k3, (E, C, H), dtype=jnp.float32) * 0.02
        w_gate = jax.random.normal(k4, (E, C, H), dtype=jnp.float32) * 0.02
        w_proj = jax.random.normal(k5, (E, H, C), dtype=jnp.float32) * (0.02 * (2 * n_layer) ** (-0.5))
        return {'x': x, 'w_router': w_router, 'w_fc': w_fc, 'w_gate': w_gate, 'w_proj': w_proj}
    _L0_ffn_all = _L0_ffn_setup()
    _L0_ffn_in = {k: v for k, v in _L0_ffn_all.items() if k in ('w_router', 'w_fc', 'w_gate', 'w_proj')}
    del _L0_ffn_all

    def _L1_xcond_setup():
        import jax, jax.numpy as jnp
        import numpy as np
        B, N, K, D, T = (16, 512, 16, 128, 3)
        EPS_ATTN = 1e-08
        LN_EPS = 1e-05

        def _ln(x, g, b):
            mu = jnp.mean(x, axis=-1, keepdims=True)
            var = jnp.mean(jnp.square(x - mu), axis=-1, keepdims=True)
            return (x - mu) * jax.lax.rsqrt(var + LN_EPS) * g + b
        key = jax.random.key(seed)
        ks = jax.random.split(key, 16)
        w = lambda k, i, o: jax.random.normal(k, (i, o), jnp.float32) * 0.02
        inp = {'x_cls': jax.random.normal(ks[0], (B, D), jnp.float32), 'x': jax.random.normal(ks[1], (B, N, D), jnp.float32), 'noise': jax.random.normal(ks[2], (B, K, D), jnp.float32), 'q_mu': jax.random.normal(ks[3], (1, 1, D), jnp.float32), 'q_logsig': jax.random.normal(ks[4], (1, 1, D), jnp.float32) * 0.02, 'lnkv_g': jnp.ones((D,), jnp.float32), 'lnkv_b': jnp.zeros((D,), jnp.float32), 'lnq_g': jnp.ones((D,), jnp.float32), 'lnq_b': jnp.zeros((D,), jnp.float32), 'lnm_g': jnp.ones((D,), jnp.float32), 'lnm_b': jnp.zeros((D,), jnp.float32), 'lnp_g': jnp.ones((D,), jnp.float32), 'lnp_b': jnp.zeros((D,), jnp.float32), 'wk': w(ks[5], D, D), 'bk': jnp.zeros((D,), jnp.float32), 'wv': w(ks[6], D, D), 'bv': jnp.zeros((D,), jnp.float32), 'wq': w(ks[7], D, D), 'bq': jnp.zeros((D,), jnp.float32), 'wu': w(ks[8], D, D), 'bu': jnp.zeros((D,), jnp.float32), 'w1': w(ks[9], D, D), 'b1': jnp.zeros((D,), jnp.float32), 'w2': w(ks[10], D, D), 'b2': jnp.zeros((D,), jnp.float32)}
        return inp
    _L1_xcond_all = _L1_xcond_setup()
    _L1_xcond_in = {k: v for k, v in _L1_xcond_all.items() if k in ('q_mu', 'q_logsig', 'lnkv_g', 'lnkv_b', 'lnq_g', 'lnq_b', 'lnm_g', 'lnm_b', 'lnp_g', 'lnp_b', 'wk', 'bk', 'wv', 'bv', 'wq', 'bq', 'wu', 'bu', 'w1', 'b1', 'w2', 'b2')}
    del _L1_xcond_all

    def _L1_ffn_setup():
        import jax, jax.numpy as jnp
        import numpy as np
        B, S, D, F, E, K = (4, 512, 128, 256, 8, 2)
        key = jax.random.key(seed)
        ks = jax.random.split(key, 5)
        s = lambda n: 1.0 / np.sqrt(n).astype(np.float32)
        return {'hidden_states': jax.random.normal(ks[0], (B, S, D), jnp.float32), 'router_w': jax.random.normal(ks[1], (E, D), jnp.float32) * s(D), 'w_gate': jax.random.normal(ks[2], (E, F, D), jnp.float32) * s(D), 'w_up': jax.random.normal(ks[3], (E, F, D), jnp.float32) * s(D), 'w_down': jax.random.normal(ks[4], (E, D, F), jnp.float32) * s(F)}
    _L1_ffn_all = _L1_ffn_setup()
    _L1_ffn_in = {k: v for k, v in _L1_ffn_all.items() if k in ('router_w', 'w_gate', 'w_up', 'w_down')}
    del _L1_ffn_all
    return {'x': x, 'cond_1024': cond_1024, 'ctx_1024': ctx_1024, 'L0_xcond_W_attn': _L0_xcond_in['W_attn'], 'L0_xcond_b_attn': _L0_xcond_in['b_attn'], 'L0_xcond_W_comb': _L0_xcond_in['W_comb'], 'L0_xcond_b_comb': _L0_xcond_in['b_comb'], 'L0_xcond_W_ih': _L0_xcond_in['W_ih'], 'L0_xcond_b_ih': _L0_xcond_in['b_ih'], 'L0_xcond_W_hh': _L0_xcond_in['W_hh'], 'L0_xcond_b_hh': _L0_xcond_in['b_hh'], 'L0_xcond_W_out': _L0_xcond_in['W_out'], 'L0_xcond_b_out': _L0_xcond_in['b_out'], 'L0_ffn_w_router': _L0_ffn_in['w_router'], 'L0_ffn_w_fc': _L0_ffn_in['w_fc'], 'L0_ffn_w_gate': _L0_ffn_in['w_gate'], 'L0_ffn_w_proj': _L0_ffn_in['w_proj'], 'L1_xcond_q_mu': _L1_xcond_in['q_mu'], 'L1_xcond_q_logsig': _L1_xcond_in['q_logsig'], 'L1_xcond_lnkv_g': _L1_xcond_in['lnkv_g'], 'L1_xcond_lnkv_b': _L1_xcond_in['lnkv_b'], 'L1_xcond_lnq_g': _L1_xcond_in['lnq_g'], 'L1_xcond_lnq_b': _L1_xcond_in['lnq_b'], 'L1_xcond_lnm_g': _L1_xcond_in['lnm_g'], 'L1_xcond_lnm_b': _L1_xcond_in['lnm_b'], 'L1_xcond_lnp_g': _L1_xcond_in['lnp_g'], 'L1_xcond_lnp_b': _L1_xcond_in['lnp_b'], 'L1_xcond_wk': _L1_xcond_in['wk'], 'L1_xcond_bk': _L1_xcond_in['bk'], 'L1_xcond_wv': _L1_xcond_in['wv'], 'L1_xcond_bv': _L1_xcond_in['bv'], 'L1_xcond_wq': _L1_xcond_in['wq'], 'L1_xcond_bq': _L1_xcond_in['bq'], 'L1_xcond_wu': _L1_xcond_in['wu'], 'L1_xcond_bu': _L1_xcond_in['bu'], 'L1_xcond_w1': _L1_xcond_in['w1'], 'L1_xcond_b1': _L1_xcond_in['b1'], 'L1_xcond_w2': _L1_xcond_in['w2'], 'L1_xcond_b2': _L1_xcond_in['b2'], 'L1_ffn_router_w': _L1_ffn_in['router_w'], 'L1_ffn_w_gate': _L1_ffn_in['w_gate'], 'L1_ffn_w_up': _L1_ffn_in['w_up'], 'L1_ffn_w_down': _L1_ffn_in['w_down']}

def reference(x, cond_1024, ctx_1024, L0_xcond_W_attn, L0_xcond_b_attn, L0_xcond_W_comb, L0_xcond_b_comb, L0_xcond_W_ih, L0_xcond_b_ih, L0_xcond_W_hh, L0_xcond_b_hh, L0_xcond_W_out, L0_xcond_b_out, L0_ffn_w_router, L0_ffn_w_fc, L0_ffn_w_gate, L0_ffn_w_proj, L1_xcond_q_mu, L1_xcond_q_logsig, L1_xcond_lnkv_g, L1_xcond_lnkv_b, L1_xcond_lnq_g, L1_xcond_lnq_b, L1_xcond_lnm_g, L1_xcond_lnm_b, L1_xcond_lnp_g, L1_xcond_lnp_b, L1_xcond_wk, L1_xcond_bk, L1_xcond_wv, L1_xcond_bv, L1_xcond_wq, L1_xcond_bq, L1_xcond_wu, L1_xcond_bu, L1_xcond_w1, L1_xcond_b1, L1_xcond_w2, L1_xcond_b2, L1_ffn_router_w, L1_ffn_w_gate, L1_ffn_w_up, L1_ffn_w_down):
    import jax
    import jax.numpy as jnp

    def _L0_xcond_ref(decode_input, decode_hidden, encode_outputs, W_attn, b_attn, W_comb, b_comb, W_ih, b_ih, W_hh, b_hh, W_out, b_out):
        import jax, jax.numpy as jnp
        import numpy as np
        B, T, H, L = (64, 128, 128, 64)

        def per_sample(xs, h0, enc):

            def step(carry, x):
                h, stopped = carry
                stop = jnp.logical_or(stopped, jnp.mean(x) == 0)
                logits = jnp.concatenate([x, h]) @ W_attn.T + b_attn
                aw = jax.nn.softmax(logits)
                applied = aw @ enc
                comb = jax.nn.relu(jnp.concatenate([x, applied]) @ W_comb.T + b_comb)
                h_new = jnp.tanh(comb @ W_ih.T + b_ih + h @ W_hh.T + b_hh)
                out = h_new @ W_out.T + b_out
                out = jnp.where(stop, jnp.zeros_like(out), out)
                h = jnp.where(stop, h, h_new)
                return ((h, stop), out)
            (_, _), outs = jax.lax.scan(step, (h0, jnp.asarray(False)), xs)
            return outs
        return jax.vmap(per_sample)(decode_input, decode_hidden, encode_outputs)

    def _L0_ffn_ref(x, w_router, w_fc, w_gate, w_proj):
        import jax, jax.numpy as jnp
        import numpy as np
        E = 16
        K = 2
        LOAD = 1.0

        def _dispatch(xb, pb, cap):
            T, C = xb.shape
            top_k_probs, ei = jax.lax.top_k(pb, K)
            flat = ei.swapaxes(0, 1).ravel()
            one_hot = jax.nn.one_hot(flat, E, dtype=jnp.int32)
            pos = jnp.cumsum(one_hot, axis=0) * one_hot
            pos = pos.reshape(K, T, E).swapaxes(0, 1)
            pos = jnp.max(pos, axis=-1) - 1
            ei2 = flat.reshape(K, T).swapaxes(0, 1)
            xr = jnp.repeat(xb, K, axis=0)
            buf = jnp.zeros((E, cap, C), xb.dtype)
            buf = buf.at[ei2.ravel(), pos.ravel()].set(xr, mode='drop')
            return (top_k_probs, pos, ei2, buf)

        def _collect(eo_b, ei_b, pos_b, tk_b):
            out = eo_b[ei_b, pos_b]
            return jnp.sum(tk_b[..., None] * out, axis=1)
        B, T, C = x.shape
        cap = int(LOAD * K * max(1, T / E))
        g = jnp.einsum('btc,ce->bte', x, w_router)
        gate_probs = jax.nn.softmax(g, axis=-1)
        top_k_probs, positions, indices, expert_inputs = jax.vmap(lambda xb, pb: _dispatch(xb, pb, cap))(x, gate_probs)
        expert_inputs = jnp.swapaxes(expert_inputs, 0, 1).reshape(E, B * cap, C)
        gg = jnp.einsum('enc,ech->enh', expert_inputs, w_gate)
        h = jnp.einsum('enc,ech->enh', expert_inputs, w_fc)
        h = jax.nn.silu(gg) * h
        o = jnp.einsum('enh,ehc->enc', h, w_proj)
        expert_outputs = jnp.swapaxes(o.reshape(E, B, cap, C), 0, 1)
        y = jax.vmap(_collect)(expert_outputs, indices, positions, top_k_probs)
        return y

    def _L1_xcond_ref(x_cls, x, noise, q_mu, q_logsig, lnkv_g, lnkv_b, lnq_g, lnq_b, lnm_g, lnm_b, lnp_g, lnp_b, wk, bk, wv, bv, wq, bq, wu, bu, w1, b1, w2, b2):
        import jax, jax.numpy as jnp
        import numpy as np
        B, N, K, D, T = (16, 512, 16, 128, 3)
        EPS_ATTN = 1e-08
        LN_EPS = 1e-05

        def _ln(x, g, b):
            mu = jnp.mean(x, axis=-1, keepdims=True)
            var = jnp.mean(jnp.square(x - mu), axis=-1, keepdims=True)
            return (x - mu) * jax.lax.rsqrt(var + LN_EPS) * g + b
        scale = D ** (-0.5)
        x_in = _ln(x, lnkv_g, lnkv_b)
        k = x_in @ wk + bk
        v = x_in @ wv + bv
        slots = q_mu + jnp.exp(q_logsig) * noise
        for _ in range(T):
            prev = slots
            q = _ln(slots, lnq_g, lnq_b) @ wq + bq
            logits = jnp.einsum('bnd,bkd->bnk', k, q) / scale
            attn = jax.nn.softmax(logits, axis=-1) + EPS_ATTN
            attn = attn / jnp.sum(attn, axis=1, keepdims=True)
            upd = jnp.einsum('bnk,bnd->bkd', attn, v)
            slots = upd @ wu + bu + prev
            h = _ln(slots, lnm_g, lnm_b) @ w1 + b1
            slots = jax.nn.gelu(h, approximate=False) @ w2 + b2 + slots
            slots = _ln(slots + x_cls[:, None, :], lnp_g, lnp_b)
        return slots

    def _L1_ffn_ref(hidden_states, router_w, w_gate, w_up, w_down):
        import jax, jax.numpy as jnp
        import numpy as np
        B, S, D, F, E, K = (4, 512, 128, 256, 8, 2)
        b, s, d = hidden_states.shape
        e = router_w.shape[0]
        x = hidden_states.reshape(-1, d)
        logits = x @ router_w.T
        scores = jax.nn.softmax(logits.astype(jnp.float32), axis=-1)
        topk_w, topk_idx = jax.lax.top_k(scores, K)
        topk_w = topk_w / jnp.sum(topk_w, axis=-1, keepdims=True)
        cw = jnp.sum(jax.nn.one_hot(topk_idx, e, dtype=topk_w.dtype) * topk_w[..., None], axis=1)
        cw = cw.astype(x.dtype)

        def per_expert(acc, wts):
            wg, wu, wd, cwe = wts
            h = jax.nn.silu(x @ wg.T) * (x @ wu.T)
            return (acc + cwe[:, None] * (h @ wd.T), None)
        out, _ = jax.lax.scan(per_expert, jnp.zeros_like(x), (w_gate, w_up, w_down, cw.T))
        return out.reshape(b, s, d)
    x = x + _L0_xcond_ref(_layernorm(x, axis=-1), cond_1024, ctx_1024, L0_xcond_W_attn, L0_xcond_b_attn, L0_xcond_W_comb, L0_xcond_b_comb, L0_xcond_W_ih, L0_xcond_b_ih, L0_xcond_W_hh, L0_xcond_b_hh, L0_xcond_W_out, L0_xcond_b_out)
    x = x + _L0_ffn_ref(_layernorm(x, axis=-1), L0_ffn_w_router, L0_ffn_w_fc, L0_ffn_w_gate, L0_ffn_w_proj)
    x = x + _L1_xcond_ref(cond_1024, ctx_1024, _layernorm(x, axis=-1), L1_xcond_q_mu, L1_xcond_q_logsig, L1_xcond_lnkv_g, L1_xcond_lnkv_b, L1_xcond_lnq_g, L1_xcond_lnq_b, L1_xcond_lnm_g, L1_xcond_lnm_b, L1_xcond_lnp_g, L1_xcond_lnp_b, L1_xcond_wk, L1_xcond_bk, L1_xcond_wv, L1_xcond_bv, L1_xcond_wq, L1_xcond_bq, L1_xcond_wu, L1_xcond_bu, L1_xcond_w1, L1_xcond_b1, L1_xcond_w2, L1_xcond_b2)
    x = x + _L1_ffn_ref(_layernorm(x, axis=-1), L1_ffn_router_w, L1_ffn_w_gate, L1_ffn_w_up, L1_ffn_w_down)
    return x

_drawn_inputs = setup_inputs


def setup_inputs(seed=0):
    import zlib

    import numpy as np

    out = dict(_drawn_inputs(seed))
    spreads = {'L0_xcond_b_out': (0.0, 0.1),
     'L1_xcond_lnkv_g': (1.0, 0.6),
     'L1_xcond_lnkv_b': (0.0, 0.556),
     'L1_xcond_lnq_g': (1.0, 0.6),
     'L1_xcond_lnq_b': (0.0, 2.0),
     'L1_xcond_lnm_g': (1.0, 0.6),
     'L1_xcond_lnm_b': (0.0, 1.63),
     'L1_xcond_lnp_g': (1.0, 0.2),
     'L1_xcond_lnp_b': (0.0, 0.1),
     'L1_xcond_bk': (0.0, 0.445),
     'L1_xcond_bv': (0.0, 0.1),
     'L1_xcond_bq': (0.0, 2.0),
     'L1_xcond_bu': (0.0, 0.1),
     'L1_xcond_b1': (0.0, 0.456),
     'L1_xcond_b2': (0.0, 0.1)}
    factors = {'L0_xcond_W_attn': 8.0,
     'L0_xcond_b_attn': 50.377,
     'L0_xcond_b_comb': 7.51,
     'L0_xcond_b_ih': 4.236,
     'L0_xcond_b_hh': 4.054,
     'L0_ffn_w_router': 8.0,
     'L0_ffn_w_fc': 8.0,
     'L0_ffn_w_gate': 8.0,
     'L0_ffn_w_proj': 8.0,
     'L1_xcond_q_logsig': 6.278}
    for name, (base, spread) in spreads.items():
        noise = np.random.default_rng([zlib.crc32(name.encode()), seed]).standard_normal(out[name].shape)
        drawn = base * np.exp(spread * noise) if base else spread * noise
        out[name] = jnp.asarray(drawn.astype(out[name].dtype))
    for name, factor in factors.items():
        out[name] = (out[name] * factor).astype(out[name].dtype)
    return out
```

```python
from contextlib import ExitStack

import concourse.bass as bass
from concourse import mybir

F32 = mybir.dt.float32
BF16 = mybir.dt.bfloat16
F16 = mybir.dt.float16
U32 = mybir.dt.uint32
ALU = mybir.AluOpType
ACT = mybir.ActivationFunctionType
AX_X = mybir.AxisListType.X

NB, NS, C = 64, 64, 128
P = 128
NT = NB * NS // P
TPG = 4
NG = NT // TPG
BG = NB // 2
E0, H0, CAP = 16, 64, 8
E1, F1 = 8, 256
FC = F1 // P
NSLOT = E0 * CAP
EPS = 1e-5
EPS_ATTN = 1e-8
ITERS = 3
VAR_AT = 50
HIGH12 = 0xFFFFF000

SQ = ["WcxT", "WcaT", "WihT", "WhhT", "WoT", "wk", "wvT", "wu", "wq", "w1", "w2"]
COLS = ["b_comb", "b_ih", "b_hh", "kv_g", "kv_b", "q_g", "q_b", "m_g", "m_b", "bk", "bq", "bv", "b1"]
ROWS = ["b_out", "q_mu", "q_logsig", "p_g", "p_b", "b2", "bu"]


def wait_apart(eng, sem, value):
    if not isinstance(value, int):
        value = eng.to_reg(value)
        eng.wait_ge(ALWAYS[0], 1)
    eng.wait_ge(sem, value)


ALWAYS = []


class Chain:

    def __init__(self, eng, sem):
        self.eng, self.sem, self.done, self.n, self.at = eng, sem, 0, 0, 0

    def do(self, ins):
        ins.then_inc(self.sem, 1)
        self.n += 1
        return ins

    def sync(self):
        self.eng.wait_ge(self.sem, self.at + self.n if isinstance(self.at, int) else self.at + self.n)

    def sync_apart(self):
        wait_apart(self.eng, self.sem, self.at + self.n)

    def __call__(self, ins):
        self.do(ins)
        self.sync()

    def loop(self, turn, per_turn):
        self.outer = (self.at, self.n)
        base = self.n + (self.at if isinstance(self.at, int) else 0)
        self.at = turn * per_turn + base if isinstance(self.at, int) else self.at + turn * per_turn + self.n
        self.n = 0

    def end(self, turns, per_turn):
        assert self.n == per_turn, (self.n, per_turn)
        self.at, n = self.outer
        self.n = n + turns * per_turn


def program(nc, d, out):
    ctx = ExitStack()
    with ctx:
        def sb(name, shape, dt=F32):
            return ctx.enter_context(nc.sbuf_tensor(name, shape, dt))

        def sem(name):
            return ctx.enter_context(nc.semaphore(name))

        bank = [ctx.enter_context(nc.psum_tensor(f"bank{i}", [P, 512], F32)) for i in range(8)]

        X = sb("X", [P, NT, C])
        R1 = sb("R1", [P, NT * C])
        R23 = sb("R23", [P, 2 * NT * C])
        R45 = sb("R45", [P, 2 * NT * C])
        R6 = sb("R6", [P, NT * C])
        R7 = sb("R7", [P, NT * C + NT])
        W1B = sb("W1B", [P, E1 * 2 * F1 + E1 * FC * C])
        cen = R1[:, :].rearrange("p (j c) -> p j c", j=NT)
        xhat = R23[:, 0:NT * C].rearrange("p (j c) -> p j c", j=NT)
        cenh = R23[:, NT * C:].rearrange("p (j c) -> p j c", j=NT)
        xhT = R45[:, 0:NT * C].rearrange("p (t b) -> p t b", t=NS)
        EWf = R45[:, NT * C:].rearrange("p (j c) -> p j c", j=NT)
        XL = R45[0:NB, NT * C:].rearrange("p (t l) -> p t l", t=NS)
        XC = R7[:, 0:NT * C].rearrange("p (t b) -> p t b", t=NS)
        EWp = [W1B[:, i * NT * C // 2:(i + 1) * NT * C // 2].bitcast(BF16).rearrange("p (j c) -> p j c", j=NT)
               for i in range(3)]
        HT = R6[:, :].rearrange("p (b t) -> p b t", t=NS)
        ctxT = R7[:, 0:NT * C]
        sq = R45[:, 0:NT * C].rearrange("p (j c) -> p j c", j=NT)
        BT = R23[:, :].rearrange("p (e b s) -> p e b s", e=E0, b=NB)
        OT = R45[:, :].rearrange("p (e b s) -> p e b s", e=E0, b=NB)
        kT = R1[:, :]
        V = R7[:, :].rearrange("p (j c) -> p j c", j=NT)
        slots = R23[:, 0:NT * C].rearrange("p (j c) -> p j c", j=NT)
        condb = R23[:, NT * C:].rearrange("p (j c) -> p j c", j=NT)
        ctxk = R6[:, :].rearrange("p (j c) -> p j c", j=NT)
        zTa = R1[:, :]
        wgu = W1B[:, 0:E1 * 2 * F1].rearrange("p (e f) -> p e f", e=E1)
        wdn = W1B[:, E1 * 2 * F1:].rearrange("p (e c) -> p e c", e=E1 * FC)

        wgf = W1B[:, 0:E0 * 2 * H0].rearrange("p (e f) -> p e f", e=E0)
        wpj = W1B[:, E0 * 2 * H0:E0 * 2 * H0 + E0 // 2 * C].rearrange("p (e c) -> p e c", e=E0 // 2)
        wsq = sb("wsq", [P, len(SQ), C])
        wat = sb("wat", [P, 2, NS])
        wr0 = sb("wr0", [P, E0])
        wr1 = sb("wr1", [P, E1])
        cols = sb("cols", [P, len(COLS)])
        rows = sb("rows", [P, len(ROWS), C])
        battn = sb("battn", [NB, NS])
        h0T = sb("h0T", [P, NB])
        W = {n: wsq[:, i, :] for i, n in enumerate(SQ)}
        COL = {n: cols[:, i:i + 1] for i, n in enumerate(COLS)}
        ROW = {n: rows[:, i, :] for i, n in enumerate(ROWS)}

        ident = sb("ident", [P, P])
        tri = sb("tri", [P, P])
        blk = sb("blk", [P, P])
        ones = sb("ones", [P, P])
        iota = sb("iota", [P, NSLOT])
        iotaE = sb("iotaE", [P, E0])
        mhalf = sb("mhalf", [P, TPG])
        parity = sb("parity", [NB, 2, NS])
        b_h = sb("b_h", [P, 1])
        wvu = sb("wvu", [P, C])
        bvu = sb("bvu", [1, C])
        qsig = sb("qsig", [P, C])

        a16 = sb("a16", [P, NT, 16])
        a8 = sb("a8", [P, NT, 8])
        a4 = sb("a4", [P, NT, 4])
        a2 = sb("a2", [P, NT, 2])
        acc4 = sb("acc4", [P, NT, 4])
        tok = sb("tok", [P, 20, NT])
        (mean, var, std, rstd, rh, rl, rlo, ta, tb, tc, td, te, tf, stopped, keep, inv, sh, sl) = (
            tok[:, i, :] for i in range(18))
        cl = sb("cl", [P, C])
        er = sb("er", [P, C])
        pr = sb("pr", [P, C])

        h = [sb(f"h{g}", [P, BG]) for g in range(2)]
        comb = [sb(f"comb{g}", [P, BG]) for g in range(2)]
        awb = [sb(f"awb{g}", [P, BG, 2], F16) for g in range(2)]
        logit, expd, spread, nmax, esum, rsum = (
            [t[g * BG:(g + 1) * BG] for g in range(2)] for t in (
                sb("logit", [NB, NS]), sb("expd", [NB, NS]), sb("spread", [NB, 2, NS]),
                sb("nmax", [NB, 1]), sb("esum", [NB, 1]), sb("rsum", [NB, 1])))

        ring = [[sb(f"ring{i}{u}", [P, 512]) for u in range(2)] for i in range(5)]
        vst = [sb(f"vst{u}", [P, TPG, C + 1]) for u in range(2)]
        zero4 = sb("zero4", [P, TPG])
        bn6, mv, ve, rs, nm = (
            [[sb(f"{n}{w}{u}", [P, TPG] + more) for u in range(2)] for w in range(2)]
            for n, more in (("bn6", [6]), ("mv", [2]), ("ve", []), ("rs", []), ("nm", [])))
        ta4, tb4, tc4 = ([sb(f"{n}{u}", [P, TPG]) for u in range(2)] for n in ("attn_top", "attn_inv", "upd_inv"))
        mx = [sb(f"mx{u}", [P, TPG]) for u in range(2)]
        sm = [sb(f"sm{u}", [P, TPG]) for u in range(2)]
        rsa = sb("rsa", [P, NT])
        nma = sb("nma", [P, NT])

        lg, pb, oh1, oh2, tmpE = (R7[:, i * NT * E0:(i + 1) * NT * E0].rearrange("p (j e) -> p j e", e=E0)
                                  for i in range(5))
        cw = R7[:, 5 * NT * E0:5 * NT * E0 + NT * E1].rearrange("p (j e) -> p j e", e=E1)
        rt = sb("rt", [P, 12, NT])
        (m1, m2, i1, i2, sd1, sd2, sc1, sc2, ra, rb, rc, rd) = (rt[:, i, :] for i in range(12))

        s_x, s_ctx, s_w, s_l0, s_l1, s_cond, s_ctxk, s_out = (
            sem(n) for n in ("x_loaded", "ctx_loaded", "weights_loaded", "l0_loaded", "l1_loaded",
                             "cond_loaded", "ctxk_loaded", "out_stored"))
        s_phase = sem("phase_ended")
        s_dve, s_pool, s_act, s_pe = (sem(n) for n in ("dve_own", "pool_own", "act_own", "pe_own"))
        s_const = sem("consts_ready")
        ALWAYS[:] = [s_const]
        names = {}

        def S(name):
            if name not in names:
                names[name] = sem(name)
            return names[name]

        def ds(start, size):
            return slice(start, start + size) if isinstance(start, int) else bass.ds(start, size)

        def one(buf, j):
            return buf[:, j, :] if isinstance(j, int) else buf[:, bass.ds(j, 1), :].rearrange("p a c -> p (a c)")

        def bc(ap, n):
            return ap.unsqueeze(2).to_broadcast([ap.shape[0], ap.shape[1], n])

        def phase_end(eng, k):
            eng.drain().then_inc(s_phase, 1)
            eng.wait_ge(s_phase, 4 * k)

        block = ctx.enter_context(nc.Block())
        LAST = 17
        SCALE = C ** 0.5

        def outs(u, i):
            return R1[:, (2 * u + i) * 512:(2 * u + i + 1) * 512]

        def upd_ps(q):
            return bank[6 + q // 2][:, q % 2 * (C + 1):(q % 2 + 1) * (C + 1)]

        def prime(eng, *counts, lead=2):
            for name in counts:
                eng.drain().then_inc(S(name), lead)

        def after(eng, name, k, lead=2):
            wait_apart(eng, S(name), k + 1 + lead)

        def steps(eng, own, stages, marks, peel=2):
            def step(n):
                for fn, lag in stages:
                    if 0 <= n - lag < NG:
                        fn(n - lag, (n - lag) % 2)
            for n in range(peel):
                step(n)
            first = peel // 2
            with eng.Fori(first, NG // 2) as t:
                own.loop(t - first, marks)
                for u in range(2):
                    for fn, lag in stages:
                        fn(t * 2 + (u - lag), (u - lag) % 2)
                own.end(NG // 2 - first, marks)
            for n in range(NG, NG + peel):
                step(n)

        def group(buf, n):
            return buf[:, ds(n * TPG, TPG)]

        def tile4(i, u):
            return ring[i][u][:].rearrange("p (q c) -> p q c", q=TPG)

        def bank4(i):
            return bank[i][:].rearrange("p (q c) -> p q c", q=TPG)

        def beside(row, n=TPG):
            return row.unsqueeze(1).to_broadcast([P, n, row.shape[1]])

        def ln_stats(dve, own, mark, w, k, n, u, src):
            for q in range(TPG):
                own.do(dve.bn_stats(bn6[w][u][:, q], one(src, n * TPG + q)))
            own.sync_apart()
            after(dve, mark + "_rstd", k - 2)
            for q in range(TPG):
                last = dve.bn_aggr(mv[w][u][:, q], bn6[w][u][:, q])
            last.then_inc(S(mark + "_stats"), 1)

        def ln_rstd(pool, own, mark, w, k, n, u):
            after(pool, mark + "_stats", k)
            own(pool.tensor_scalar(ve[w][u][:], mv[w][u][:, :, 1], EPS, None, ALU.add))
            own(pool.tensor_tensor(rs[w][u][:], ve[w][u][:], mhalf[:], ALU.pow))
            own(pool.tensor_tensor(nm[w][u][:], mv[w][u][:, :, 0], rs[w][u][:], ALU.mult))
            own(pool.tensor_copy(group(rsa, n), rs[w][u][:]))
            pool.tensor_tensor(group(nma, n), zero4[:], nm[w][u][:], ALU.subtract).then_inc(S(mark + "_rstd"), 1)

        def ln_scale(act, mark, k, n, u, src, dst):
            after(act, mark + "_rstd", k)
            after(act, mark + "_turned", k - 2)
            for q in range(TPG):
                j = n * TPG + q
                last = act.activation(dst[:, q * C:(q + 1) * C], one(src, j), ACT.Identity,
                                      bias=nma[:, ds(j, 1)], scale=rsa[:, ds(j, 1)])
            last.then_inc(S(mark + "_z"), 1)

        def ln_turn(pe, mark, k, n, u, src, ps):
            after(pe, mark + "_z", k)
            after(pe, mark + "_zT", k - 2)
            for q in range(TPG):
                last = pe.transpose(ps[:, q * C:(q + 1) * C], src[:, q * C:(q + 1) * C], ident[:])
            last.then_inc(S(mark + "_turned"), 1)

        def pool_rest(pool, own):
            prime(pool, "a_rstd", "hidden_staged")

            def stage_hidden(n, u):
                after(pool, "y", n - 2)
                pool.tensor_copy(ring[0][u][:].rearrange("p (b t) -> p b t", t=NS), HT[:, ds(n * 8, 8), :])\
                    .then_inc(S("hidden_staged"), 1)
            steps(pool, own, [(stage_hidden, 0), (lambda n, u: ln_rstd(pool, own, "a", 0, n, n, u), 1)], 8)
            phase_end(pool, 3)
            phase_end(pool, 4)
            phase_end(pool, 5)
            phase_end(pool, 6)

            prime(pool, "outs_staged")

            def stage_outs(n, u):
                after(pool, "outs_turned", n - 2)
                for i in range(2):
                    last = pool.tensor_copy(ring[3 + i][u][:].rearrange("p (b e s) -> p e b s", b=4, e=E0),
                                            OT[:, :, ds(n * 8 + 4 * i, 4), :])
                last.then_inc(S("outs_staged"), 1)
            steps(pool, own, [(stage_outs, 0)], 0)
            phase_end(pool, 7)

            prime(pool, "kv_rstd")
            steps(pool, own, [(lambda n, u: ln_rstd(pool, own, "kv", 0, n, n, u), 0)], 8)
            own(pool.memset(V[:, :, C:C + 1], 1.0))
            phase_end(pool, 8)

            prime(pool, "noise_rstd")
            pool.wait_ge(s_cond, 16)

            def condition(n, u):
                pool.tensor_tensor(group(condb, n), group(condb, n), beside(ROW["b2"]), ALU.add)
            steps(pool, own, [(lambda n, u: ln_rstd(pool, own, "noise", 0, n, n, u), 0), (condition, 0)], 8)
            phase_end(pool, 9)

            prime(pool, "q_rstd", "k_staged", "v_staged", "m_rstd", "p_rstd", "sums_staged")
            for it in range(ITERS):
                def k_of(n, it=it):
                    return n + it * NG

                def stage_k(n, u):
                    after(pool, "attn_logits", k_of(n - 2))
                    pool.tensor_copy(ring[3][u][:], kT[:, ds(n * 512, 512)]).then_inc(S("k_staged"), 1)

                def stage_v(n, u):
                    after(pool, "updated", k_of(n - 2))
                    pool.tensor_copy(vst[u][:], group(V, n)).then_inc(S("v_staged"), 1)
                steps(pool, own, [(lambda n, u: ln_rstd(pool, own, "q", 0, k_of(n), n, u), 0), (stage_k, 1),
                                  (stage_v, 2)], 8, peel=4)
                phase_end(pool, 10 + 2 * it)

                def stage_sums(n, u):
                    after(pool, "mlp_added", k_of(n - 2))
                    pool.tensor_tensor(tile4(3, u), group(slots, n), group(condb, n), ALU.add)\
                        .then_inc(S("sums_staged"), 1)
                steps(pool, own, [(lambda n, u: ln_rstd(pool, own, "m", 0, k_of(n), n, u), 0), (stage_sums, 1),
                                  (lambda n, u: ln_rstd(pool, own, "p", 1, k_of(n), n, u), 3)], 16, peel=4)
                phase_end(pool, 11 + 2 * it)

            prime(pool, "f_rstd", "zT_kept")

            def keep_zT(n, u):
                after(pool, "f_zT", n)
                pool.tensor_copy(zTa[:, ds(n * 512, 512)], ring[2][u][:]).then_inc(S("zT_kept"), 1)
            steps(pool, own, [(lambda n, u: ln_rstd(pool, own, "f", 0, n, n, u), 0), (keep_zT, 1)], 8)
            phase_end(pool, 16)
            phase_end(pool, 17)

        def route(dve, own, e, pos):
            tt, tsc, stt = dve.tensor_tensor, dve.tensor_scalar, dve.scalar_tensor_tensor
            L, pr_, h1_, h2_, t_ = (b[:, :, 0:e] for b in (lg, pb, oh1, oh2, tmpE))
            idx = iotaE[:, 0:e].unsqueeze(1).to_broadcast([P, NT, e])
            own(dve.tensor_reduce(ra, L, AX_X, ALU.max))
            tt(pr_, L, bc(ra, e), ALU.subtract).then_inc(S("route_shifted"), 1)
            dve.wait_ge(S("route_exp"), 1 if pos else 2)
            own(dve.tensor_reduce(rb, pr_, AX_X, ALU.add))
            own(dve.reciprocal(rc, rb))
            own(tt(pr_, pr_, bc(rc, e), ALU.mult))
            for m, i, oh, src in ((m1, i1, h1_, pr_), (m2, i2, h2_, t_)):
                own(dve.tensor_reduce(m, src, AX_X, ALU.max))
                own(tt(oh, src, bc(m, e), ALU.is_equal))
                own(tt(oh, oh, idx, ALU.mult))
                own(dve.tensor_reduce(i, oh, AX_X, ALU.min))
                own(tt(oh, idx, bc(i, e), ALU.is_equal))
                if m is m1:
                    own(stt(t_, oh, -4.0, pr_, ALU.mult, ALU.add))

        def dve_rest(dve, own):
            tt, tsc, stt = dve.tensor_tensor, dve.tensor_scalar, dve.scalar_tensor_tensor
            prime(dve, "a_stats", "logits_kept")

            def add_output(n, u):
                after(dve, "y", n)
                for q in range(TPG):
                    j = n * TPG + q
                    own.do(stt(one(X, j), bank[u][:, q * C:(q + 1) * C], keep[:, ds(j, 1)], one(X, j),
                               ALU.mult, ALU.add))
                own.sync_apart()
                ln_stats(dve, own, "a", 0, n, n, u, X)

            def keep_logits(k, n, u, e):
                after(dve, "router", k)
                dve.tensor_copy(group(lg, n)[:, :, 0:e], bank[4 + u][:, 0:TPG * e].rearrange("p (q e) -> p q e", e=e))\
                    .then_inc(S("logits_kept"), 1)
            steps(dve, own, [(add_output, 0), (lambda n, u: keep_logits(n, n, u, E0), 2)], 16)
            phase_end(dve, 3)

            route(dve, own, E0, True)
            dve.nop().then_inc(S("picked"), 1)
            for k, (oh, i, sd, sc) in enumerate(((oh1, i1, sd1, sc1), (oh2, i2, sd2, sc2))):
                ps = bank[k][:].rearrange("p (j e) -> p j e", e=E0)
                dve.wait_ge(S("counted"), k + 1)
                own(tt(tmpE, ps, oh, ALU.mult))
                own(dve.tensor_reduce(ra, tmpE, AX_X, ALU.add))
                own(tsc(ra, ra, -1.0, None, ALU.add))
                own.do(tsc(rb, ra, float(CAP), None, ALU.is_lt))
                own(tsc(rc, ra, float(CAP - 1), None, ALU.min))
                own(stt(sc, i, float(CAP), rc, ALU.mult, ALU.add))
                own(tsc(sc, sc, 100.0 * CAP, None, ALU.add))
                own(stt(sd, sc, 1.0, rb, ALU.add, ALU.mult))
                own(tsc(sd, sd, -1.0, None, ALU.add))
            phase_end(dve, 4)

            prime(dve, "places", "placed_hi")

            def places(n, u):
                after(dve, "dispatched", n - 2)
                for q in range(TPG):
                    j = n * TPG + q
                    own.do(tsc(ring[2][u][:, q * C:(q + 1) * C], iota[:], sd1[:, ds(j, 1)], None, ALU.is_equal))
                own.sync()
                for q in range(TPG):
                    j = n * TPG + q
                    cs = slice(q * C, (q + 1) * C)
                    last = stt(ring[1][u][:, cs], iota[:], sd2[:, ds(j, 1)], ring[2][u][:, cs], ALU.is_equal, ALU.add)
                last.then_inc(S("places"), 1)

            def keep_hi(n, u):
                after(dve, "dispatched", n)
                dve.tensor_copy(BT[:, :, ds(n * 8 + 4, 4), :],
                                bank[2 * u + 1][:].rearrange("p (b e s) -> p e b s", b=4, e=E0))\
                    .then_inc(S("placed_hi"), 1)
            steps(dve, own, [(places, 0), (keep_hi, 1)], 8)
            phase_end(dve, 5)

            for p in range(E0 // 2):
                u = p % 2
                dve.wait_ge(S("fc"), p + 1)
                dve.wait_ge(S("silu"), p + 1)
                if p >= 2:
                    dve.wait_ge(S("down"), 2 * (p - 1))
                tt(ring[1][u][:], ring[0][u][:], bank[2 + u][:], ALU.mult).then_inc(S("gated"), 1)
                dve.wait_ge(S("down"), 2 * p + 1)
                dve.tensor_copy(OT[:, 2 * p], bank[4 + 2 * u][:].rearrange("p (b s) -> p b s", s=CAP))\
                    .then_inc(S("out_even"), 1)
            phase_end(dve, 6)

            prime(dve, "weights", "outs_hi", "x_added")

            def weights(n, u):
                after(dve, "weights_turned", n - 2)
                for q in range(TPG):
                    j = n * TPG + q
                    cs = slice(q * C, (q + 1) * C)
                    own.do(tsc(ring[0][u][:, cs], iota[:], sc1[:, ds(j, 1)], m1[:, ds(j, 1)], ALU.is_equal, ALU.mult))
                    own.do(tsc(ring[1][u][:, cs], iota[:], sc2[:, ds(j, 1)], m2[:, ds(j, 1)], ALU.is_equal, ALU.mult))
                own.sync()
                tt(ring[0][u][:], ring[0][u][:], ring[1][u][:], ALU.add).then_inc(S("weights"), 1)

            def outs_hi(n, u):
                after(dve, "outs_turned", n)
                after(dve, "collected", n - 2)
                dve.tensor_copy(outs(u, 1), bank[4 + u][:]).then_inc(S("outs_hi"), 1)

            def add_collected(n, u):
                after(dve, "collected", n)
                tt(group(X, n), group(X, n), bank4(6 + u), ALU.add).then_inc(S("x_added"), 1)
            steps(dve, own, [(weights, 0), (outs_hi, 1), (add_collected, 2)], 16)
            phase_end(dve, 7)

            prime(dve, "kv_stats", "v_kept")
            for i, (sem_, dst, bk) in enumerate((("wvu", wvu[:], bank[6][:, 0:C]), ("bvu", bvu[:], bank[7][0:1, 0:C]))):
                dve.wait_ge(S("folded"), i + 1)
                if i == 0:
                    dve.tensor_copy(dst, bk).then_inc(S("folded_kept"), 1)
                else:
                    tt(dst, bk, ROW["bu"][0:1, :], ALU.add).then_inc(S("folded_kept"), 1)
            dve.wait_ge(s_ctxk, 16)

            def keep_v(n, u):
                after(dve, "v", n)
                dve.tensor_copy(group(V, n)[:, :, 0:C], bank4(4 + u)).then_inc(S("v_kept"), 1)
            steps(dve, own, [(lambda n, u: ln_stats(dve, own, "kv", 0, n, n, u, ctxk), 0), (keep_v, 2)], 8)
            phase_end(dve, 8)

            prime(dve, "noise_stats", "noise_turned")

            def begin_slots(n, u):
                after(dve, "noise_z", n)
                own(tt(tile4(0, u), tile4(0, u), beside(qsig[:]), ALU.mult))
                tt(group(slots, n), tile4(0, u), beside(ROW["q_mu"]), ALU.add).then_inc(S("noise_turned"), 1)
            steps(dve, own, [(lambda n, u: ln_stats(dve, own, "noise", 0, n, n, u, X), 0), (begin_slots, 1)], 10)
            phase_end(dve, 9)

            prime(dve, "q_stats", "attn_max", "attn", "updated_kept", "m_stats", "mlp_added", "p_stats", "p_turned")
            for it in range(ITERS):
                def k_of(n, it=it):
                    return n + it * NG

                def attn_max(n, u):
                    after(dve, "attn_logits", k_of(n))
                    own(dve.tensor_reduce(ta4[u][:], bank[4 + u][:, 0:TPG * NS].rearrange("p (q s) -> p q s", s=NS),
                                          AX_X, ALU.max))
                    tsc(mx[u][:], ta4[u][:], -SCALE, None, ALU.mult).then_inc(S("attn_max"), 1)

                def attn(n, u):
                    after(dve, "attn_exp", k_of(n))
                    own(dve.reciprocal(tb4[u][:], sm[u][:]))
                    for q in range(TPG):
                        cs = slice(q * NS, (q + 1) * NS)
                        last = tsc(ring[4][u][:, cs], ring[4][u][:, cs], tb4[u][:, q:q + 1], EPS_ATTN, ALU.mult, ALU.add)
                    last.then_inc(S("attn"), 1)

                def update(n, u):
                    after(dve, "updated", k_of(n))
                    for q in range(TPG):
                        own.do(dve.reciprocal(tc4[u][:, q:q + 1], upd_ps(q)[:, C:C + 1]))
                    own.sync()
                    for q in range(TPG):
                        s_ = one(slots, n * TPG + q)
                        last = own.do(stt(s_, upd_ps(q)[:, 0:C], tc4[u][:, q:q + 1], s_, ALU.mult, ALU.add))
                    own.sync()
                    dve.nop().then_inc(S("updated_kept"), 1)
                steps(dve, own, [(lambda n, u: ln_stats(dve, own, "q", 0, k_of(n), n, u, slots), 0),
                                 (update, 4), (attn, 3), (attn_max, 2)], 28, peel=4)
                phase_end(dve, 10 + 2 * it)

                def add_mlp(n, u):
                    after(dve, "mlp", k_of(n))
                    after(dve, "sums_staged", k_of(n))
                    tt(group(slots, n), bank4(4 + u), tile4(3, u), ALU.add).then_inc(S("mlp_added"), 1)
                    after(dve, "mlp_added", k_of(n))
                    ln_stats(dve, own, "p", 1, k_of(n), n, u, slots)

                def affine(n, u):
                    after(dve, "p_z", k_of(n))
                    own(tt(tile4(4, u), tile4(4, u), beside(ROW["p_g"]), ALU.mult))
                    tt(group(slots, n), tile4(4, u), beside(ROW["p_b"]), ALU.add).then_inc(S("p_turned"), 1)
                steps(dve, own, [(lambda n, u: ln_stats(dve, own, "m", 0, k_of(n), n, u, slots), 0),
                                 (add_mlp, 3), (affine, 4)], 18, peel=4)
                phase_end(dve, 11 + 2 * it)

            prime(dve, "f_stats")

            def add_slots(n, u):
                own.do(tt(group(X, n), group(X, n), group(slots, n), ALU.add))
                own.sync_apart()
                ln_stats(dve, own, "f", 0, n, n, u, X)

            steps(dve, own, [(add_slots, 0), (lambda n, u: keep_logits(n + NG, n, u, E1), 2)], 10)
            dve.wait_ge(S("logits_kept"), 2 + 2 * NG)
            route(dve, own, E1, False)
            own(tt(ra, m1, m2, ALU.add))
            own(dve.reciprocal(rb, ra))
            own.do(tt(m1, m1, rb, ALU.mult))
            own(tt(m2, m2, rb, ALU.mult))
            own.do(tt(oh1[:, :, 0:E1], oh1[:, :, 0:E1], bc(m1, E1), ALU.mult))
            own(tt(oh2[:, :, 0:E1], oh2[:, :, 0:E1], bc(m2, E1), ALU.mult))
            own(tt(cw, oh1[:, :, 0:E1], oh2[:, :, 0:E1], ALU.add))
            phase_end(dve, 16)

            prime(dve, "y_added")
            prime(dve, "prod", lead=2 * FC)
            units = E1 * FC

            def add_expert(n, e):
                after(dve, "ffn_y", n * E1 + e)
                own.sync()
                for q in range(TPG):
                    j = n * TPG + q
                    own.do(stt(one(X, j), bank[6 + e % 2][:, q * C:(q + 1) * C], one(cw, j)[:, e:e + 1], one(X, j),
                               ALU.mult, ALU.add))
                own.sync()
                dve.nop().then_inc(S("y_added"), 1)
            with dve.Fori(0, NG) as n:
                own.loop(n, E1 * TPG)
                for e in range(E1):
                    for f in range(FC):
                        k = e * FC + f
                        after(dve, "ffn_up", n * units + k)
                        after(dve, "ffn_silu", n * units + k)
                        after(dve, "ffn_y", n * E1 + (e - 2))
                        tt(ring[2 + f][e % 2][:], ring[f][e % 2][:], bank[2 + f][:], ALU.mult).then_inc(S("prod"), 1)
                    if e > 0:
                        add_expert(n, e - 1)
                add_expert(n, E1 - 1)
                own.end(NG, E1 * TPG)
            phase_end(dve, 17)

        def act_rest(act, own):
            prime(act, "a_z", "a_zT")

            def keep_zT(mark, k, n, u, src, dst, g=None, b=None, free=None):
                after(act, mark + "_turned", k)
                after(act, free, k - 2)
                if g is None:
                    act.activation(dst, src, ACT.Copy).then_inc(S(mark + "_zT"), 1)
                else:
                    act.activation(dst, src, ACT.Identity, bias=b, scale=g).then_inc(S(mark + "_zT"), 1)
            steps(act, own, [(lambda n, u: ln_scale(act, "a", n, n, u, X, ring[1][u]), 1),
                             (lambda n, u: keep_zT("a", n, n, u, bank[2 + u][:], ring[2][u][:], free="router"), 2)], 0)
            phase_end(act, 3)
            act.wait_ge(S("route_shifted"), 1)
            act.activation(pb, pb, ACT.Exp).then_inc(S("route_exp"), 1)
            phase_end(act, 4)

            prime(act, "rows_scaled", "placed_lo")

            def scale_rows(n, u):
                after(act, "dispatched", n - 2)
                for q in range(TPG):
                    j = n * TPG + q
                    last = act.activation(ring[0][u][:, q * C:(q + 1) * C], one(X, j), ACT.Identity,
                                          bias=nma[:, ds(j, 1)], scale=rsa[:, ds(j, 1)])
                last.then_inc(S("rows_scaled"), 1)

            def keep_lo(n, u):
                after(act, "dispatched", n)
                act.activation(BT[:, :, ds(n * 8, 4), :], bank[2 * u][:].rearrange("p (b e s) -> p e b s", b=4, e=E0),
                               ACT.Copy).then_inc(S("placed_lo"), 1)
            steps(act, own, [(scale_rows, 0), (keep_lo, 1)], 0)
            act.preload_act_table(ACT.Silu)
            phase_end(act, 5)

            for p in range(E0 // 2):
                u = p % 2
                act.wait_ge(S("gate"), p + 1)
                if p >= 2:
                    act.wait_ge(S("gated"), p - 1)
                act.activation(ring[0][u][:], bank[u][:], ACT.Silu).then_inc(S("silu"), 1)
                act.wait_ge(S("down"), 2 * p + 2)
                act.activation(OT[:, 2 * p + 1], bank[5 + 2 * u][:].rearrange("p (b s) -> p b s", s=CAP), ACT.Copy)\
                    .then_inc(S("out_odd"), 1)
            phase_end(act, 6)

            prime(act, "weights_T", "outs_lo")

            def weights_T(n, u):
                after(act, "weights_turned", n)
                after(act, "collected", n - 2)
                act.activation(ring[2][u][:], bank[u][:], ACT.Copy).then_inc(S("weights_T"), 1)

            def outs_lo(n, u):
                after(act, "outs_turned", n)
                act.activation(outs(u, 0), bank[2 + u][:], ACT.Copy).then_inc(S("outs_lo"), 1)
            steps(act, own, [(weights_T, 1), (outs_lo, 1)], 0)
            act.preload_act_table(ACT.Exp)
            act.activation(qsig[:], ROW["q_logsig"], ACT.Exp)
            phase_end(act, 7)

            prime(act, "kv_z", "kv_zT", "k_kept")

            def keep_k(n, u):
                after(act, "k", n)
                act.activation(kT[:, ds(n * 512, 512)], bank[2 + u][:], ACT.Identity, bias=COL["bk"])\
                    .then_inc(S("k_kept"), 1)
            steps(act, own, [(lambda n, u: ln_scale(act, "kv", n, n, u, ctxk, ring[0][u]), 0),
                             (lambda n, u: keep_zT("kv", n, n, u, bank[u][:], ring[1][u][:], COL["kv_g"], COL["kv_b"],
                                                   free="v"), 1),
                             (keep_k, 2)], 0)
            phase_end(act, 8)

            prime(act, "noise_z")
            steps(act, own, [(lambda n, u: ln_scale(act, "noise", n, n, u, X, ring[0][u]), 0)], 0)
            phase_end(act, 9)

            prime(act, "q_z", "q_zT", "q_kept", "attn_exp", "m_z", "m_zT", "gelu", "p_z")
            for it in range(ITERS):
                def k_of(n, it=it):
                    return n + it * NG

                def keep_q(n, u):
                    after(act, "q", k_of(n))
                    after(act, "attn_logits", k_of(n - 2))
                    act.activation(ring[2][u][:], bank[2 + u][:], ACT.Identity, bias=COL["bq"]).then_inc(S("q_kept"), 1)

                def attn_exp(n, u):
                    after(act, "attn_max", k_of(n))
                    after(act, "updated", k_of(n - 2))
                    for q in range(TPG):
                        cs = slice(q * NS, (q + 1) * NS)
                        last = act.activation(ring[4][u][:, cs], bank[4 + u][:, cs], ACT.Exp, bias=mx[u][:, q:q + 1],
                                              scale=SCALE, accum_out=sm[u][:, q:q + 1])
                    last.then_inc(S("attn_exp"), 1)
                steps(act, own, [(attn_exp, 3),
                                 (lambda n, u: ln_scale(act, "q", k_of(n), n, u, slots, ring[0][u]), 0),
                                 (keep_q, 2),
                                 (lambda n, u: keep_zT("q", k_of(n), n, u, bank[u][:], ring[1][u][:], COL["q_g"],
                                                       COL["q_b"], free="q"), 1)], 0, peel=4)
                act.preload_act_table(ACT.Gelu)
                phase_end(act, 10 + 2 * it)

                def gelu(n, u):
                    after(act, "mlp_hidden", k_of(n))
                    after(act, "mlp", k_of(n - 2))
                    act.activation(ring[2][u][:], bank[2 + u][:], ACT.Gelu, bias=COL["b1"]).then_inc(S("gelu"), 1)
                steps(act, own, [(lambda n, u: ln_scale(act, "m", k_of(n), n, u, slots, ring[0][u]), 0),
                                 (gelu, 2),
                                 (lambda n, u: keep_zT("m", k_of(n), n, u, bank[u][:], ring[1][u][:], COL["m_g"],
                                                       COL["m_b"], free="mlp_hidden"), 1),
                                 (lambda n, u: ln_scale(act, "p", k_of(n), n, u, slots, ring[4][u]), 3)], 0, peel=4)
                act.preload_act_table(ACT.Exp)
                phase_end(act, 11 + 2 * it)

            prime(act, "f_z", "f_zT")

            def keep_zT_f(n, u):
                after(act, "zT_kept", n - 2)
                keep_zT("f", n, n, u, bank[u][:], ring[2][u][:], free="f_router")
            steps(act, own, [(lambda n, u: ln_scale(act, "f", n, n, u, X, ring[0][u]), 0), (keep_zT_f, 1)], 0)
            act.wait_ge(S("route_shifted"), 2)
            act.activation(pb[:, :, 0:E1], pb[:, :, 0:E1], ACT.Exp).then_inc(S("route_exp"), 1)
            act.preload_act_table(ACT.Silu)
            phase_end(act, 16)

            prime(act, "ffn_silu")
            units = E1 * FC
            with act.Fori(0, NG) as n:
                for e in range(E1):
                    for f in range(FC):
                        k = n * units + e * FC + f
                        after(act, "ffn_gate", k)
                        after(act, "prod", k - 2 * FC, 2 * FC)
                        act.activation(ring[f][e % 2][:], bank[f][:], ACT.Silu).then_inc(S("ffn_silu"), 1)
            phase_end(act, 17)

        def pe_rest(pe, own):
            mm = pe.matmul
            prime(pe, "y", "a_turned", "router")

            def hidden_out(n, u):
                after(pe, "hidden_staged", n)
                after(pe, "a_stats", n - 2)
                for q in range(TPG):
                    ps = bank[u][:, q * C:(q + 1) * C]
                    mm(ps, ring[0][u][:, q * C:(q + 1) * C], W["WoT"], start=True, stop=False)
                    last = mm(ps, ones[0:1, :], ROW["b_out"][0:1, :], start=False, stop=True)
                last.then_inc(S("y"), 1)

            def router(mark, k, n, u, w, e, zT):
                after(pe, mark + "_zT", n)
                after(pe, "logits_kept", k - 2)
                for q in range(TPG):
                    last = mm(bank[4 + u][:, q * e:(q + 1) * e], zT[:, q * C:(q + 1) * C], w[:], start=True, stop=True)
                last.then_inc(S("router"), 1)
            steps(pe, own, [(hidden_out, 0), (lambda n, u: ln_turn(pe, "a", n, n, u, ring[1][u], bank[2 + u]), 1),
                            (lambda n, u: router("a", n, n, u, wr0, E0, ring[2][u]), 2)], 0)
            phase_end(pe, 3)

            pe.wait_ge(S("picked"), 1)
            rows1, rows2 = (b.rearrange("p j e -> p (j e)") for b in (oh1, oh2))
            mm(bank[0][:], tri[:], rows1, start=True, stop=True).then_inc(S("counted"), 1)
            mm(bank[1][:], tri[:], rows2, start=True, stop=False)
            mm(bank[1][:], blk[:], rows1, start=False, stop=True).then_inc(S("counted"), 1)
            phase_end(pe, 4)

            prime(pe, "dispatched")

            def dispatch(n, u):
                after(pe, "rows_scaled", n)
                after(pe, "places", n)
                after(pe, "placed_lo", n - 2)
                after(pe, "placed_hi", n - 2)
                for q in range(TPG):
                    for b in range(2):
                        r = slice(b * NS, (b + 1) * NS)
                        last = mm(bank[2 * u + b][:, q * C:(q + 1) * C], ring[0][u][r, q * C:(q + 1) * C],
                                  ring[1][u][r, q * C:(q + 1) * C], start=True, stop=True)
                last.then_inc(S("dispatched"), 1)
            steps(pe, own, [(dispatch, 0)], 0)
            phase_end(pe, 5)

            pe.wait_ge(s_l0, 32)

            def down(p):
                u = p % 2
                pe.wait_ge(S("gated"), p + 1)
                for i, kept in ((0, "out_even"), (1, "out_odd")):
                    if p >= 2:
                        pe.wait_ge(S(kept), p - 1)
                    r = slice(i * H0, (i + 1) * H0)
                    mm(bank[4 + 2 * u + i][:], wpj[r, p, :], ring[1][u][r, :], start=True, stop=True)\
                        .then_inc(S("down"), 1)
            for p in range(E0 // 2):
                u = p % 2
                for bk, cs, name, free in ((u, slice(0, H0), "gate", "silu"), (2 + u, slice(H0, 2 * H0), "fc", "gated")):
                    if p >= 2:
                        pe.wait_ge(S(free), p - 1)
                    for i in range(2):
                        last = mm(bank[bk][i * H0:(i + 1) * H0, :], wgf[:, 2 * p + i, cs],
                                  BT[:, 2 * p + i].rearrange("p b s -> p (b s)"), start=True, stop=True)
                    last.then_inc(S(name), 1)
                if p:
                    down(p - 1)
            down(E0 // 2 - 1)
            phase_end(pe, 6)

            prime(pe, "weights_turned", "outs_turned", "collected")

            def turn_collect(n, u):
                after(pe, "weights", n)
                after(pe, "weights_T", n - 2)
                for q in range(TPG):
                    last = pe.transpose(bank[u][:, q * C:(q + 1) * C], ring[0][u][:, q * C:(q + 1) * C], ident[:])
                last.then_inc(S("weights_turned"), 1)
                after(pe, "outs_staged", n)
                after(pe, "outs_lo", n - 2)
                after(pe, "outs_hi", n - 2)
                for i in range(2):
                    for q in range(TPG):
                        last = pe.transpose(bank[2 + 2 * i + u][:, q * C:(q + 1) * C],
                                            ring[3 + i][u][:, q * C:(q + 1) * C], ident[:])
                last.then_inc(S("outs_turned"), 1)

            def collect(n, u):
                after(pe, "weights_T", n)
                after(pe, "outs_lo", n)
                after(pe, "outs_hi", n)
                after(pe, "x_added", n - 2)
                for b in range(2 * TPG):
                    q, r = b // 2, b % 2
                    last = mm(bank[6 + u][r * NS:(r + 1) * NS, q * C:(q + 1) * C], ring[2][u][:, b * NS:(b + 1) * NS],
                              outs(u, r)[:, q * C:(q + 1) * C], start=True, stop=True)
                last.then_inc(S("collected"), 1)
            steps(pe, own, [(turn_collect, 0), (collect, 1)], 0)
            phase_end(pe, 7)

            mm(bank[6][:, 0:C], W["wvT"], W["wu"], start=True, stop=True).then_inc(S("folded"), 1)
            mm(bank[7][0:1, 0:C], COL["bv"], W["wu"], start=True, stop=True).then_inc(S("folded"), 1)
            pe.wait_ge(S("folded_kept"), 2)
            prime(pe, "kv_turned", "k", "v")

            def keys_values(n, u):
                after(pe, "kv_zT", n)
                after(pe, "k_kept", n - 2)
                mm(bank[2 + u][:], W["wk"], ring[1][u][:], start=True, stop=True).then_inc(S("k"), 1)
                after(pe, "v_kept", n - 2)
                for q in range(TPG):
                    ps = bank[4 + u][:, q * C:(q + 1) * C]
                    mm(ps, ring[1][u][:, q * C:(q + 1) * C], wvu[:], start=True, stop=False)
                    last = mm(ps, ones[0:1, :], bvu[:], start=False, stop=True)
                last.then_inc(S("v"), 1)
            steps(pe, own, [(lambda n, u: ln_turn(pe, "kv", n, n, u, ring[0][u], bank[u]), 0), (keys_values, 1)], 0)
            phase_end(pe, 8)
            phase_end(pe, 9)

            prime(pe, "q_turned", "q", "attn_logits", "updated", "m_turned", "mlp_hidden", "mlp")
            for it in range(ITERS):
                def k_of(n, it=it):
                    return n + it * NG

                def queries(n, u):
                    after(pe, "q_zT", k_of(n))
                    after(pe, "q_kept", k_of(n - 2))
                    mm(bank[2 + u][:], W["wq"], ring[1][u][:], start=True, stop=True).then_inc(S("q"), 1)

                def attn_logits(n, u):
                    after(pe, "q_kept", k_of(n))
                    after(pe, "k_staged", k_of(n))
                    after(pe, "attn_exp", k_of(n - 2))
                    for b in range(2 * TPG):
                        q, r = b // 2, b % 2
                        cs = slice(b * NS, (b + 1) * NS)
                        last = mm(bank[4 + u][r * NS:(r + 1) * NS, q * NS:(q + 1) * NS], ring[3][u][:, cs],
                                  ring[2][u][:, cs], start=True, stop=True)
                    last.then_inc(S("attn_logits"), 1)

                def updates(n, u):
                    after(pe, "attn", k_of(n))
                    after(pe, "v_staged", k_of(n))
                    after(pe, "updated_kept", k_of(n - 1))
                    for b in range(2 * TPG):
                        q, r = b // 2, b % 2
                        rs_ = slice(r * NS, (r + 1) * NS)
                        last = mm(upd_ps(q)[rs_, :], ring[4][u][rs_, q * NS:(q + 1) * NS], vst[u][rs_, q, :],
                                  start=True, stop=True)
                    last.then_inc(S("updated"), 1)
                steps(pe, own, [(updates, 3), (lambda n, u: ln_turn(pe, "q", k_of(n), n, u, ring[0][u], bank[u]), 0),
                                (attn_logits, 2), (queries, 1)], 0, peel=4)
                phase_end(pe, 10 + 2 * it)

                def mlp_hidden(n, u):
                    after(pe, "m_zT", k_of(n))
                    after(pe, "gelu", k_of(n - 2))
                    mm(bank[2 + u][:], W["w1"], ring[1][u][:], start=True, stop=True).then_inc(S("mlp_hidden"), 1)

                def mlp(n, u):
                    after(pe, "gelu", k_of(n))
                    after(pe, "mlp_added", k_of(n - 2))
                    for q in range(TPG):
                        last = mm(bank[4 + u][:, q * C:(q + 1) * C], ring[2][u][:, q * C:(q + 1) * C], W["w2"],
                                  start=True, stop=True)
                    last.then_inc(S("mlp"), 1)
                steps(pe, own, [(lambda n, u: ln_turn(pe, "m", k_of(n), n, u, ring[0][u], bank[u]), 0),
                                (mlp, 2), (mlp_hidden, 1)], 0, peel=4)
                phase_end(pe, 11 + 2 * it)

            prime(pe, "f_turned", "f_router")

            def router_f(n, u):
                router("f", n + NG, n, u, wr1, E1, ring[2][u])
                pe.nop().then_inc(S("f_router"), 1)
            steps(pe, own, [(lambda n, u: ln_turn(pe, "f", n, n, u, ring[0][u], bank[u]), 0), (router_f, 1)], 0)
            phase_end(pe, 16)

            pe.wait_ge(s_l1, 32)
            prime(pe, "ffn_gate", "ffn_up", "ffn_y")
            units = E1 * FC

            def down(n, e):
                after(pe, "prod", n * units + (e * FC + FC - 1), 2 * FC)
                after(pe, "y_added", n * E1 + (e - 2))
                for q in range(TPG):
                    for f in range(FC):
                        last = mm(bank[6 + e % 2][:, q * C:(q + 1) * C], ring[2 + f][e % 2][:, q * C:(q + 1) * C],
                                  wdn[:, e * FC + f, :], start=(f == 0), stop=(f == FC - 1))
                last.then_inc(S("ffn_y"), 1)
            with pe.Fori(0, NG) as n:
                for e in range(E1):
                    for f in range(FC):
                        k = n * units + e * FC + f
                        after(pe, "ffn_silu", k - FC)
                        mm(bank[f][:], wgu[:, e, f * P:(f + 1) * P], zTa[:, ds(n * 512, 512)],
                           start=True, stop=True).then_inc(S("ffn_gate"), 1)
                        after(pe, "prod", k - FC, 2 * FC)
                        mm(bank[2 + f][:], wgu[:, e, F1 + f * P:F1 + (f + 1) * P], zTa[:, ds(n * 512, 512)],
                           start=True, stop=True).then_inc(S("ffn_up"), 1)
                    if e > 0:
                        down(n, e - 1)
                down(n, E1 - 1)
            phase_end(pe, 17)

        @block.sync
        def _(sp):
            sp.dma_start(X[:], d["x"]).then_inc(s_x, 16)
            sp.dma_start(ctxT, d["ctxT"]).then_inc(s_ctx, 16)
            for buf, name in ((wsq, "wsq"), (wat, "wat"), (cols, "cols"), (rows, "rows"), (battn, "battn"),
                              (h0T, "h0T"), (wr0, "wr0"), (wr1, "wr1")):
                sp.dma_start(buf[:], d[name]).then_inc(s_w, 16)
            sp.wait_ge(s_phase, 4 * 2)
            sp.dma_start(wgf, d["wgf"]).then_inc(s_l0, 16)
            sp.dma_start(wpj, d["wpj"]).then_inc(s_l0, 16)
            sp.wait_ge(s_phase, 4 * 3)
            sp.dma_start(ctxk, d["ctx_tok"]).then_inc(s_ctxk, 16)
            sp.wait_ge(s_phase, 4 * 6)
            sp.dma_start(condb, d["condb"]).then_inc(s_cond, 16)
            sp.wait_ge(s_l0, 32)
            sp.dma_start(wgu, d["wgu"]).then_inc(s_l1, 16)
            sp.dma_start(wdn, d["wdn"]).then_inc(s_l1, 16)
            sp.wait_ge(s_phase, 4 * LAST)
            sp.dma_start(out, X[:]).then_inc(s_out, 16)
            sp.wait_ge(s_out, 16)

        psL = [bank[g][g * BG:(g + 1) * BG, 0:NS] for g in range(2)]
        psT = [bank[2 + g][:, 0:BG] for g in range(2)]
        psC = [bank[4 + g][:, 0:2 * BG] for g in range(2)]
        psH = [bank[6 + g][:, 0:BG] for g in range(2)]

        def scan(half, attend, loop):
            def turn(t, first=False, last=False):
                attend(0, t)
                half(1, t, not first, True)
                attend(1, t)
                half(0, t + 1, True, not last)
            half(0, 0, False, True)
            turn(0, first=True)
            loop(turn)
            turn(NS - 1, last=True)
            half(1, NS, True, False)

        @block.gpsimd
        def _(pool):
            own = Chain(pool, s_pool)
            for buf in (ident, tri, blk):
                own(pool.memset(buf[:], 0.0))
            own(pool.memset(ones[:], 1.0))
            own(pool.memset(mhalf[:], -0.5))
            own(pool.memset(zero4[:], 0.0))
            own(pool.affine_select(out=ident[:], in_=ident[:], compare_op=ALU.not_equal, fill=1.0, base=0,
                                      pattern=[[-1, P]], channel_multiplier=1))
            for b in range(2):
                own(pool.memset(blk[b * NS:(b + 1) * NS, b * NS:(b + 1) * NS], 1.0))
            own(pool.iota(iota[:], [[1, NSLOT]], base=0, channel_multiplier=0,
                             allow_small_or_imprecise_dtypes=True))
            own(pool.iota(iotaE[:], [[1, E0]], base=-100, channel_multiplier=0,
                             allow_small_or_imprecise_dtypes=True))
            own(pool.affine_select(out=tri[:], in_=blk[:], compare_op=ALU.is_ge, fill=0.0, base=0,
                                   pattern=[[1, P]], channel_multiplier=-1))
            own(pool.memset(parity[:], 0.0))
            for k in range(BG):
                own(pool.affine_select(out=parity[:], in_=parity[:], compare_op=ALU.not_equal, fill=1.0,
                                       base=-2 * k, pattern=[[-1, 2], [0, NS]], channel_multiplier=1))
            pool.nop().then_inc(s_const, 1)
            for n in range(NG):
                js = slice(n * TPG, (n + 1) * TPG)
                pool.wait_ge(s_act, 2 * (n + 1))
                own(pool.tensor_tensor(EWf[:, js], EWf[:, js], EWp[0][:, js], ALU.subtract))
                own(pool.tensor_copy(EWp[1][:, js], EWf[:, js]))
                own(pool.tensor_tensor(EWp[2][:, js], EWf[:, js], EWp[1][:, js], ALU.subtract))
            pool.nop().then_inc(S("ew_split"), 1)
            phase_end(pool, 1)

            pool.wait_ge(s_w, 16 * 8)
            for g in range(2):
                pool.tensor_copy(h[g][:], h0T[:, g * BG:(g + 1) * BG]).then_inc(S(f"h_ready{g}"), 1)

            def keep_h(g, t):
                pool.wait_ge(S(f"h_ready{g}"), t + 2)
                to = HT[:, g * BG:(g + 1) * BG, ds(t, 1)].rearrange("p b a -> p (b a)")
                pool.tensor_copy(to, h[g][:]).then_inc(S(f"h_kept{g}"), 1)

            def half(g, t, end, begin):
                if end:
                    keep_h(g, t - 1)

            def loop(turn):
                with pool.Fori(1, NS - 1) as t:
                    turn(t)
            scan(half, lambda g, t: None, loop)
            phase_end(pool, 2)
            pool_rest(pool, own)

        @block.vector
        def _(dve):
            own = Chain(dve, s_dve)
            tt, tsc, stt = dve.tensor_tensor, dve.tensor_scalar, dve.scalar_tensor_tensor
            x16 = X[:].rearrange("p j (i l) -> p i j l", l=16)

            dve.wait_ge(s_x, 16)
            own(tt(a16[:], x16[:, 0], x16[:, 1], ALU.add))
            for i in range(2, 8):
                own(tt(a16[:], a16[:], x16[:, i], ALU.add))
            r4 = a16[:].rearrange("p j (r k) -> p j r k", r=4)
            r2 = a8[:].rearrange("p j (r k) -> p j r k", r=2)
            own(tt(r2, r4[:, :, 0::2, :], r4[:, :, 1::2, :], ALU.add))
            own(tt(a4[:], r2[:, :, 0, :], r2[:, :, 1, :], ALU.add))
            own(tt(a2[:], a4[:, :, 0::2], a4[:, :, 1::2], ALU.add))
            own(tt(ta, a2[:, :, 0], a2[:, :, 1], ALU.add))
            own(tsc(mean, ta, 1.0 / C, None, ALU.mult))
            own(tt(cen, X[:], bc(mean, C), ALU.subtract))
            own.do(tt(sq, cen, cen, ALU.mult))
            own(tsc(cenh.bitcast(U32), cen.bitcast(U32), HIGH12, None, ALU.bitwise_and))
            q4 = sq.rearrange("p j (k i) -> p i j k", k=4)
            own(tt(acc4[:], q4[:, 0], q4[:, 1], ALU.add))
            for i in range(2, 32):
                own(tt(acc4[:], acc4[:], q4[:, i], ALU.add))

            def sum4(dst):
                own(tt(ta, acc4[:, :, 0], acc4[:, :, 1], ALU.add))
                own(tt(tb, ta, acc4[:, :, 2], ALU.add))
                own(tt(dst, tb, acc4[:, :, 3], ALU.add))
            sum4(tc)
            own.do(tsc(var, tc, 1.0 / C, EPS, ALU.mult, ALU.add))
            own.sync()
            assert own.n == VAR_AT, own.n
            dve.wait_ge(S("root_ready"), 1)

            def split(hi, lo, a):
                own(tsc(hi.bitcast(U32), a.bitcast(U32), HIGH12, None, ALU.bitwise_and))
                own(tt(lo, a, hi, ALU.subtract))

            def product_error(ah, al, bh, bl, prod, err, t):
                own(tt(err, ah, bh, ALU.mult))
                own(tt(err, err, prod, ALU.subtract))
                for u_, v_ in ((ah, bl), (al, bh), (al, bl)):
                    own(tt(t, u_, v_, ALU.mult))
                    own(tt(err, err, t, ALU.add))
            for _ in range(2):
                own(dve.reciprocal(inv, std))
                split(sh, sl, std)
                own(tt(td, std, std, ALU.mult))
                product_error(sh, sl, sh, sl, td, te, tf)
                own(tt(ta, var, td, ALU.subtract))
                own(tt(ta, ta, te, ALU.subtract))
                own(tt(ta, ta, inv, ALU.mult))
                own(stt(std, ta, 0.5, std, ALU.mult, ALU.add))
            own(dve.reciprocal(rstd, std))
            split(sh, sl, std)
            split(rh, rl, rstd)
            own(tt(td, std, rstd, ALU.mult))
            product_error(sh, sl, rh, rl, td, te, tf)
            own(tsc(ta, td, -1.0, 1.0, ALU.mult, ALU.add))
            own(tt(ta, ta, te, ALU.subtract))
            own(tt(rlo, rstd, ta, ALU.mult))
            for j in range(0, NT, TPG):
                tt(xhat[:, j:j + TPG], cen[:, j:j + TPG], bc(rstd[:, j:j + TPG], C), ALU.mult)\
                    .then_inc(S("xhat_ready"), 1)
            dve.wait_ge(s_w, 16 * 8)
            own.do(tt(b_h[:], COL["b_ih"], COL["b_hh"], ALU.add))
            dve.wait_ge(S("ew_split"), 1)
            for n in range(NG):
                dve.wait_ge(S("xl_ready"), n + 1)
                tt(XL[:, n * 8:(n + 1) * 8, :], bank[n % 2][0:NB, :].rearrange("b (t l) -> b t l", l=NS),
                   battn[:].unsqueeze(1).to_broadcast([NB, 8, NS]), ALU.add).then_inc(S("xl_taken"), 1)
            phase_end(dve, 1)

            def exact_quotient(j):
                c, q, ch = one(cen, j), one(xhat, j), one(cenh, j)

                def col(v):
                    return v[:, ds(j, 1)]
                own(tt(cl[:], c, ch, ALU.subtract))
                own(stt(er[:], ch, col(rh), q, ALU.mult, ALU.subtract))
                own(stt(er[:], ch, col(rl), er[:], ALU.mult, ALU.add))
                own(stt(er[:], cl[:], col(rh), er[:], ALU.mult, ALU.add))
                yield
                own(stt(er[:], cl[:], col(rl), er[:], ALU.mult, ALU.add))
                own(stt(er[:], c, col(rlo), er[:], ALU.mult, ALU.add))
                own(tt(c, q, er[:], ALU.add))
                yield

            c4 = cen.rearrange("p j (k i) -> p i j k", k=4)

            def add_run(i):
                src = c4[:, i] if isinstance(i, int) else c4[:, bass.ds(i, 1)].rearrange("p a j k -> p (a j) k")
                own(tt(acc4[:], acc4[:], src, ALU.add))
                yield
                yield

            background = [iter(())]

            def half(g, t, end, begin):
                if end:
                    dve.wait_ge(S(f"attended{g}"), t)
                    own(dve.tensor_reduce(comb[g][:], psC[g].rearrange("p (b k) -> p b k", k=2), AX_X, ALU.add))
                    own(tt(comb[g][:], comb[g][:], one(XC, t - 1)[:, g * BG:(g + 1) * BG], ALU.add))
                    tsc(comb[g][:], comb[g][:], 0.0, None, ALU.max).then_inc(S(f"comb_ready{g}"), 1)
                if begin:
                    dve.wait_ge(S(f"logits_ready{g}"), t + 1)
                    own(tt(logit[g], psL[g], one(XL, t)[g * BG:(g + 1) * BG], ALU.add))
                    dve.tensor_reduce(nmax[g], logit[g], AX_X, ALU.max, negate=True)\
                        .then_inc(S(f"max_ready{g}"), 1)
                    dve.wait_ge(S(f"exp_ready{g}"), t + 1)
                    own(dve.reciprocal(rsum[g], esum[g]))
                    stt(spread[g], expd[g].unsqueeze(1).to_broadcast([BG, 2, NS]), rsum[g],
                        parity[g * BG:(g + 1) * BG], ALU.mult, ALU.mult).then_inc(S(f"spread_ready{g}"), 1)
                    dve.wait_ge(S(f"turned{g}"), t + 1)
                    own(dve.tensor_copy(awb[g][:, :, 0], psT[g]))
                    tt(awb[g][:, :, 1], psT[g], awb[g][:, :, 0], ALU.subtract).then_inc(S(f"placed{g}"), 1)
                next(background[0], None)

            def loop(turn):
                per = 10 + 7
                with dve.Fori(1, NT) as t:
                    own.loop(t - 1, per)
                    background[0] = exact_quotient(t)
                    turn(t)
                    own.end(NT - 1, per)
                own(dve.tensor_copy(acc4[:], c4[:, 0]))
                per = 10 + 1
                with dve.Fori(NT, NS - 1) as t:
                    own.loop(t - NT, per)
                    background[0] = add_run(t - (NT - 1))
                    turn(t)
                    own.end(NS - 1 - NT, per)
                background[0] = iter(())
            for _ in exact_quotient(0):
                pass
            scan(half, lambda g, t: None, loop)
            sum4(tc)
            tsc(stopped, tc, 0.0, None, ALU.is_equal).then_inc(S("flags_ready"), 1)
            dve.wait_ge(S("flags_summed"), 1)
            own.do(tsc(keep, bank[0][:, 0:NT], 0.0, None, ALU.is_equal))
            phase_end(dve, 2)
            dve_rest(dve, own)

        @block.scalar
        def _(act):
            own = Chain(act, s_act)
            act.preload_act_table(ACT.Sqrt)
            act.wait_ge(s_dve, VAR_AT)
            act.activation(std, var, ACT.Sqrt).then_inc(S("root_ready"), 1)
            for n in range(NG):
                act.wait_ge(S("ew_ready"), n + 1)
                js = slice(n * TPG, (n + 1) * TPG)
                ps = bank[n % 4][:].rearrange("p (j c) -> p j c", j=TPG)
                own.do(act.activation(EWf[:, js], ps, ACT.Copy))
                own.do(act.activation(EWp[0][:, js], ps, ACT.Copy))
            for n in range(NG):
                act.wait_ge(S("xt_ready"), n + 1)
                own.do(act.activation(xhT[:, :, n * 8:(n + 1) * 8].rearrange("p t b -> p b t"),
                                      bank[4 + n % 4][:].rearrange("p (b t) -> p b t", t=NS), ACT.Copy))
            for n in range(NG):
                act.wait_ge(S("xc_ready"), n + 1)
                own.do(act.activation(XC[:, n * 8:(n + 1) * 8].rearrange("p t b -> p (t b)"), bank[2 + n % 2][:],
                                      ACT.Identity, bias=COL["b_comb"]))
            phase_end(act, 1)
            act.preload_act_table(ACT.Exp)

            def half(g, t, end, begin):
                if end:
                    act.wait_ge(S(f"hidden_ready{g}"), t)
                    if not (isinstance(t, int) and t == 1):
                        act.wait_ge(S(f"h_kept{g}"), t - 1)
                    act.activation(h[g][:], psH[g], ACT.Tanh, bias=b_h[:]).then_inc(S(f"h_ready{g}"), 1)
                if begin:
                    act.wait_ge(S(f"max_ready{g}"), t + 1)
                    act.activation(expd[g], logit[g], ACT.Exp, bias=nmax[g], accum_out=esum[g])\
                        .then_inc(S(f"exp_ready{g}"), 1)

            def loop(turn):
                with act.Fori(1, NS - 1) as t:
                    turn(t)
            scan(half, lambda g, t: None, loop)
            phase_end(act, 2)
            act_rest(act, own)

        @block.tensor
        def _(pe):
            mm = pe.matmul
            own = Chain(pe, s_pe)
            pe.wait_ge(s_const, 1)
            pe.wait_ge(s_ctx, 16)
            pe.wait_ge(s_w, 16 * 8)
            for n in range(NG):
                if n >= 4:
                    pe.wait_ge(s_act, 2 * (n - 3))
                for q in range(TPG):
                    j = n * TPG + q
                    last = mm(bank[n % 4][:, q * C:(q + 1) * C], ctxT[:, j * P:(j + 1) * P], W["WcaT"],
                              start=True, stop=True)
                last.then_inc(S("ew_ready"), 1)
            for n in range(NG):
                pe.wait_ge(S("xhat_ready"), n + 1)
                if n >= 4:
                    pe.wait_ge(s_act, 2 * NG + n - 3)
                for q in range(TPG):
                    last = pe.transpose(bank[4 + n % 4][:, q * C:(q + 1) * C], xhat[:, n * TPG + q, :], ident[:])
                last.then_inc(S("xt_ready"), 1)
            pe.wait_ge(s_act, 3 * NG)
            for n in range(NG):
                if n >= 2:
                    pe.wait_ge(S("xl_taken"), n - 1)
                for i in range(8):
                    last = mm(bank[n % 2][0:NB, i * NS:(i + 1) * NS], xhT[:, n * 8 + i, :], wat[:, 0, :],
                              start=True, stop=True)
                last.then_inc(S("xl_ready"), 1)
                if n >= 2:
                    pe.wait_ge(s_act, 3 * NG + n - 1)
                mm(bank[2 + n % 2][:], W["WcxT"], xhT[:, n * 8:(n + 1) * 8].rearrange("p t b -> p (t b)"),
                   start=True, stop=True).then_inc(S("xc_ready"), 1)
            phase_end(pe, 1)

            def finish(g, t):
                pe.wait_ge(S(f"comb_ready{g}"), t)
                mm(psH[g], W["WihT"], comb[g][:], start=False, stop=True, skip_group_check=True)\
                    .then_inc(S(f"hidden_ready{g}"), 1)

            def start(g, t):
                pe.wait_ge(S(f"h_ready{g}"), t + 1)
                mm(psL[g], h[g][:], wat[:, 1, :], start=True, stop=True).then_inc(S(f"logits_ready{g}"), 1)
                mm(psH[g], W["WhhT"], h[g][:], start=True, stop=False, skip_group_check=True)

            def turn_weights(g, t):
                pe.wait_ge(S(f"spread_ready{g}"), t + 1)
                mm(psT[g], spread[g].rearrange("b a l -> b (a l)"),
                   ident[g * BG:(g + 1) * BG, g * BG:(g + 1) * BG], start=True, stop=True).then_inc(S(f"turned{g}"), 1)

            def attention(g, t, pairs):
                if pairs[0] == 0:
                    pe.wait_ge(S(f"placed{g}"), t + 1)
                for p in pairs:
                    for i in range(3):
                        last = mm(psC[g][:, 4 * p:4 * p + 4], EWp[i][:, g * (BG // 2) + p, :],
                                  awb[g][:, 2 * p:2 * p + 2, :].rearrange("p b k -> p (b k)"),
                                  start=(i == 0), stop=(i == 2), skip_group_check=True)
                if pairs[-1] == BG // 2 - 1:
                    last.then_inc(S(f"attended{g}"), 1)

            def both(ga, ta_, g, t, end, begin):
                attention(ga, ta_, range(0, 5))
                if end:
                    finish(g, t)
                attention(ga, ta_, range(5, 9))
                if begin:
                    start(g, t)
                attention(ga, ta_, range(9, BG // 2))
                if begin:
                    turn_weights(g, t)

            def turn(t, first=False, last=False):
                both(0, t, 1, t, not first, True)
                both(1, t, 0, t + 1, True, not last)
            start(0, 0)
            turn_weights(0, 0)
            turn(0, first=True)
            with pe.Fori(1, NS - 1) as t:
                turn(t)
            turn(NS - 1, last=True)
            finish(1, NS)
            pe.wait_ge(S("flags_ready"), 1)
            mm(bank[0][:, 0:NT], tri[:], stopped, start=True, stop=True).then_inc(S("flags_summed"), 1)
            phase_end(pe, 2)
            pe_rest(pe, own)


def kernel(**inputs):
    import numpy as np
    import concourse.bacc as bacc
    from concourse.bass_utils import run_bass_kernel_spmd as run

    a = {k: np.asarray(v) for k, v in inputs.items()}

    def tiles(t):
        return t.reshape(NT, P, C).transpose(1, 0, 2)

    r = "L0_xcond_"
    s = "L1_xcond_"
    Wa, Wc = a[r + "W_attn"], a[r + "W_comb"]
    squares = {"WcxT": Wc[:, :C].T, "WcaT": Wc[:, C:].T, "WihT": a[r + "W_ih"].T, "WhhT": a[r + "W_hh"].T,
               "WoT": a[r + "W_out"].T, "wk": a[s + "wk"], "wvT": a[s + "wv"].T, "wu": a[s + "wu"],
               "wq": a[s + "wq"], "w1": a[s + "w1"], "w2": a[s + "w2"]}
    columns = {"b_comb": a[r + "b_comb"], "b_ih": a[r + "b_ih"], "b_hh": a[r + "b_hh"], "kv_g": a[s + "lnkv_g"],
               "kv_b": a[s + "lnkv_b"], "q_g": a[s + "lnq_g"], "q_b": a[s + "lnq_b"], "m_g": a[s + "lnm_g"],
               "m_b": a[s + "lnm_b"], "bk": a[s + "bk"], "bq": a[s + "bq"], "bv": a[s + "bv"], "b1": a[s + "b1"]}
    rowsd = {"b_out": a[r + "b_out"], "q_mu": a[s + "q_mu"], "q_logsig": a[s + "q_logsig"], "p_g": a[s + "lnp_g"],
             "p_b": a[s + "lnp_b"], "b2": a[s + "b2"], "bu": a[s + "bu"]}
    wp = a["L0_ffn_w_proj"]
    arrays = {
        "x": tiles(a["x"]),
        "ctxT": a["ctx_1024"].reshape(NB * NS, C).T,
        "ctx_tok": tiles(a["ctx_1024"]),
        "condb": tiles(np.broadcast_to(a["cond_1024"][:, None, :], (NB, NS, C))),
        "wsq": np.stack([squares[n] for n in SQ], 1),
        "wat": np.stack([Wa[:, :C].T, Wa[:, C:].T], 1),
        "cols": np.stack([columns[n].reshape(C) for n in COLS], 1),
        "rows": np.broadcast_to(np.stack([rowsd[n].reshape(C) for n in ROWS], 0)[None], (P, len(ROWS), C)),
        "battn": np.broadcast_to(a[r + "b_attn"][None], (NB, NS)),
        "h0T": a["cond_1024"].T,
        "wr0": a["L0_ffn_w_router"],
        "wr1": a["L1_ffn_router_w"].T,
        "wgf": np.concatenate([a["L0_ffn_w_gate"], a["L0_ffn_w_fc"]], 2).transpose(1, 0, 2),
        "wpj": wp.reshape(E0 // 2, 2 * H0, C).transpose(1, 0, 2),
        "wgu": np.concatenate([a["L1_ffn_w_gate"], a["L1_ffn_w_up"]], 1).transpose(2, 0, 1),
        "wdn": a["L1_ffn_w_down"].reshape(E1, C, FC, P).transpose(3, 0, 2, 1).reshape(P, E1 * FC, C),
    }
    nc = bacc.Bacc("TRN2", target_bir_lowering=False, num_devices=1)
    given, d = {}, {}
    for name, v in arrays.items():
        v = np.ascontiguousarray(v)
        given[f"{name}_dram"] = v
        d[name] = nc.dram_tensor(f"{name}_dram", v.shape, F32, kind="ExternalInput").ap()
    out = nc.dram_tensor("out_dram", (P, NT, C), F32, kind="ExternalOutput").ap()
    program(nc, d, out)
    res = run(nc, [given], core_ids=[0])
    return res.results[0]["out_dram"].transpose(1, 0, 2).reshape(NB, NS, C)
```

```python
from contextlib import ExitStack

import concourse.bass as bass
from concourse import mybir

F32 = mybir.dt.float32
BF16 = mybir.dt.bfloat16
F16 = mybir.dt.float16
U32 = mybir.dt.uint32
F32R = mybir.dt.float32r
ALU = mybir.AluOpType
ACT = mybir.ActivationFunctionType
AX_X = mybir.AxisListType.X

NB, NS, C = 64, 64, 128
P = 128
NT = NB * NS // P
TPG = 4
NG = NT // TPG
BG = NB // 2
E0, H0, CAP = 16, 64, 8
E1, F1 = 8, 256
FC = F1 // P
NSLOT = E0 * CAP
EPS = 1e-5
EPS_ATTN = 1e-8
ITERS = 3
VAR_AT = 50
HIGH12 = 0xFFFFF000

SQ = ["WcxT", "WcaT", "WihT", "WhhT", "WoT", "wk", "wvT", "wu", "wq", "w1", "w2"]
COLS = ["b_comb", "b_ih", "b_hh", "kv_g", "kv_b", "q_g", "q_b", "m_g", "m_b", "bk", "bq", "bv", "b1"]
ROWS = ["b_out", "q_mu", "q_logsig", "p_g", "p_b", "b2", "bu"]


def wait_apart(eng, sem, value):
    if not isinstance(value, int):
        value = eng.to_reg(value)
        eng.wait_ge(ALWAYS[0], 1)
    eng.wait_ge(sem, value)


ALWAYS = []


class Chain:

    def __init__(self, eng, sem):
        self.eng, self.sem, self.done, self.n, self.at = eng, sem, 0, 0, 0

    def do(self, ins):
        ins.then_inc(self.sem, 1)
        self.n += 1
        return ins

    def sync(self):
        self.eng.wait_ge(self.sem, self.at + self.n if isinstance(self.at, int) else self.at + self.n)

    def sync_apart(self):
        wait_apart(self.eng, self.sem, self.at + self.n)

    def apart(self, ins):
        self.do(ins)
        self.sync_apart()

    def __call__(self, ins):
        self.do(ins)
        self.sync()

    def loop(self, turn, per_turn):
        self.outer = (self.at, self.n)
        base = self.n + (self.at if isinstance(self.at, int) else 0)
        self.at = turn * per_turn + base if isinstance(self.at, int) else self.at + turn * per_turn + self.n
        self.n = 0

    def end(self, turns, per_turn):
        assert self.n == per_turn, (self.n, per_turn)
        self.at, n = self.outer
        self.n = n + turns * per_turn


def program(nc, d, out):
    ctx = ExitStack()
    with ctx:
        def sb(name, shape, dt=F32):
            return ctx.enter_context(nc.sbuf_tensor(name, shape, dt))

        def under(name, shape, dt):
            with nc.sbuf_tensor(name, shape, dt) as t:
                return t

        def sem(name):
            return ctx.enter_context(nc.semaphore(name))

        bank = [ctx.enter_context(nc.psum_tensor(f"bank{i}", [P, 512], F32)) for i in range(8)]

        X = sb("X", [P, NT, C])
        zT2_0 = under("zT_high_", [P, NT * C], F32R)
        R1 = sb("R1", [P, NT * C])
        R23 = sb("R23", [P, 2 * NT * C])
        wgu2_ = under("weights_halves", [P, 2, E1, 2 * F1], F32R)
        R45 = sb("R45", [P, 2 * NT * C])
        zT2_1 = under("zT_low", [P, NT * C], F32R)
        R6 = sb("R6", [P, NT * C])
        R7 = sb("R7", [P, NT * C + NT])
        W1B = sb("W1B", [P, E1 * 2 * F1 + E1 * FC * C])
        cen = R1[:, :].rearrange("p (j c) -> p j c", j=NT)
        xhat = R23[:, 0:NT * C].rearrange("p (j c) -> p j c", j=NT)
        cenh = R23[:, NT * C:].rearrange("p (j c) -> p j c", j=NT)
        xhT = R45[:, 0:NT * C].rearrange("p (t b) -> p t b", t=NS)
        EWf = R45[:, NT * C:].rearrange("p (j c) -> p j c", j=NT)
        XL = R45[:, NT * C:].rearrange("p (t l) -> p t l", t=NS)
        EWp = [W1B[:, i * NT * C // 2:(i + 1) * NT * C // 2].bitcast(BF16).rearrange("p (j c) -> p j c", j=NT)
               for i in range(3)]
        HT = R6[:, :].rearrange("p (b t) -> p b t", t=NS)
        ctxT = R7[:, 0:NT * C]
        xh16 = R7[:, 0:NT * C].bitcast(F16).rearrange("p (t b k) -> p t b k", t=NS, k=2)
        sq = R45[:, 0:NT * C].rearrange("p (j c) -> p j c", j=NT)
        BT = R23[:, :].rearrange("p (e b s) -> p e b s", e=E0, b=NB)
        OT = R45[:, :].rearrange("p (e b s) -> p e b s", e=E0, b=NB)
        kT = R1[:, :]
        V = R7[:, :].rearrange("p (j c) -> p j c", j=NT)
        slots = R23[:, 0:NT * C].rearrange("p (j c) -> p j c", j=NT)
        condb = R23[:, NT * C:].rearrange("p (j c) -> p j c", j=NT)
        ctxk = R6[:, :].rearrange("p (j c) -> p j c", j=NT)
        wgu = W1B[:, 0:E1 * 2 * F1].rearrange("p (e f) -> p e f", e=E1)
        zT2 = [zT2_0[:], zT2_1[:]]
        wgu2 = [wgu2_[:, i] for i in range(2)]
        wdn = W1B[:, E1 * 2 * F1:].rearrange("p (e c) -> p e c", e=E1 * FC)

        wgf = W1B[:, 0:E0 * 2 * H0].rearrange("p (e f) -> p e f", e=E0)
        wpj = W1B[:, E0 * 2 * H0:E0 * 2 * H0 + E0 // 2 * C].rearrange("p (e c) -> p e c", e=E0 // 2)
        wsq = sb("wsq", [P, len(SQ), C])
        wat = sb("wat", [P, 2, NS])
        wr0 = sb("wr0", [P, E0])
        wr1 = sb("wr1", [P, E1])
        cols = sb("cols", [P, len(COLS)])
        rows = sb("rows", [P, len(ROWS), C])
        battn = sb("battn", [NB, NS])
        h0T = sb("h0T", [P, NB])
        W = {n: wsq[:, i, :] for i, n in enumerate(SQ)}
        COL = {n: cols[:, i:i + 1] for i, n in enumerate(COLS)}
        ROW = {n: rows[:, i, :] for i, n in enumerate(ROWS)}

        ident = sb("ident", [P, P])
        tri = sb("tri", [P, P])
        blk = sb("blk", [P, P])
        ones = sb("ones", [P, P])
        iota = sb("iota", [P, NSLOT])
        iotaE = sb("iotaE", [P, E0])
        mhalf = sb("mhalf", [P, TPG])
        parity = sb("parity", [BG, 2, NS])
        b_h = sb("b_h", [P, 1])
        wvu = sb("wvu", [P, C])
        bvu = sb("bvu", [P, C])
        bvb = sb("bvb", [P, P])
        qsig = sb("qsig", [P, C])

        a16 = sb("a16", [P, NT, 16])
        a8 = sb("a8", [P, NT, 8])
        a4 = sb("a4", [P, NT, 4])
        a2 = sb("a2", [P, NT, 2])
        acc4 = sb("acc4", [P, NT, 4])
        tok = sb("tok", [P, 20, NT])
        (mean, var, std, rstd, rh, rl, rlo, ta, tb, tc, td, te, tf, stopped, keep, inv, sh, sl) = (
            tok[:, i, :] for i in range(18))
        cl = sb("cl", [P, C])
        er = sb("er", [P, C])
        pr = sb("pr", [P, C])
        pr2 = sb("pr2", [P, C])

        h = [sb(f"h{g}", [P, BG]) for g in range(2)]
        h16 = [sb(f"h16{g}", [P, 2, BG], F16) for g in range(2)]
        WP = {n: sb(n + "_parts", [P, 3, C], BF16) for n in ("WcxT", "WhhT")}
        comb = [sb(f"comb{g}", [P, BG]) for g in range(2)]
        awb = [sb(f"awb{g}", [P, BG, 2], F16) for g in range(2)]
        expd, spread, nmax, esum, rsum = (
            [sb(f"{n}{g}", [BG] + more) for g in range(2)] for n, more in (
                ("expd", [NS]), ("spread", [2, NS]), ("nmax", [1]), ("esum", [1]), ("rsum", [1])))

        ring = [[sb(f"ring{i}{u}", [P, 512]) for u in range(2)] for i in range(5)]
        vst = [sb(f"vst{u}", [P, TPG, C + 1]) for u in range(2)]
        zero4 = sb("zero4", [P, TPG])
        bn6, mv, ve, rs, nm = (
            [[sb(f"{n}{w}{u}", [P, TPG] + more) for u in range(2)] for w in range(2)]
            for n, more in (("bn6", [6]), ("mv", [2]), ("ve", []), ("rs", []), ("nm", [])))
        ta4, tb4, tc4 = ([sb(f"{n}{u}", [P, TPG]) for u in range(2)] for n in ("attn_top", "attn_inv", "upd_inv"))
        mx = [sb(f"mx{u}", [P, TPG]) for u in range(2)]
        sm = [sb(f"sm{u}", [P, TPG]) for u in range(2)]
        rsa = sb("rsa", [P, NT])
        nma = sb("nma", [P, NT])

        lg, pb, oh1, oh2, tmpE = (R7[:, i * NT * E0:(i + 1) * NT * E0].rearrange("p (j e) -> p j e", e=E0)
                                  for i in range(5))
        cw = R7[:, 5 * NT * E0:5 * NT * E0 + NT * E1].rearrange("p (j e) -> p j e", e=E1)
        rt = sb("rt", [P, 12, NT])
        (m1, m2, i1, i2, sd1, sd2, sc1, sc2, ra, rb, rc, rd) = (rt[:, i, :] for i in range(12))

        s_x, s_ctx, s_w, s_l0, s_l1, s_cond, s_ctxk, s_out = (
            sem(n) for n in ("x_loaded", "ctx_loaded", "weights_loaded", "l0_loaded", "l1_loaded",
                             "cond_loaded", "ctxk_loaded", "out_stored"))
        s_phase = sem("phase_ended")
        s_dve, s_pool, s_act, s_pe = (sem(n) for n in ("dve_own", "pool_own", "act_own", "pe_own"))
        s_const = sem("consts_ready")
        ALWAYS[:] = [s_const]
        names = {}

        def S(name):
            if name not in names:
                names[name] = sem(name)
            return names[name]

        def ds(start, size):
            return slice(start, start + size) if isinstance(start, int) else bass.ds(start, size)

        def one(buf, j):
            return buf[:, j, :] if isinstance(j, int) else buf[:, bass.ds(j, 1), :].rearrange("p a c -> p (a c)")

        def bc(ap, n):
            return ap.unsqueeze(2).to_broadcast([ap.shape[0], ap.shape[1], n])

        def phase_end(eng, k):
            eng.drain().then_inc(s_phase, 1)
            eng.wait_ge(s_phase, 4 * k)

        block = ctx.enter_context(nc.Block())
        LAST = 17
        SCALE = C ** 0.5

        def outs(u, i):
            return R1[:, (2 * u + i) * 512:(2 * u + i + 1) * 512]

        def upd_ps(q):
            return bank[6 + q // 2][:, q % 2 * (C + 1):(q % 2 + 1) * (C + 1)]

        def prime(eng, *counts, lead=2):
            for name in counts:
                eng.drain().then_inc(S(name), lead)

        def after(eng, name, k, lead=2):
            wait_apart(eng, S(name), k + 1 + lead)

        def steps(eng, own, stages, marks, peel=2):
            def step(n):
                for fn, lag in stages:
                    if 0 <= n - lag < NG:
                        fn(n - lag, (n - lag) % 2)
            for n in range(peel):
                step(n)
            first = peel // 2
            with eng.Fori(first, NG // 2) as t:
                own.loop(t - first, marks)
                for u in range(2):
                    for fn, lag in stages:
                        fn(t * 2 + (u - lag), (u - lag) % 2)
                own.end(NG // 2 - first, marks)
            for n in range(NG, NG + peel):
                step(n)

        def group(buf, n):
            return buf[:, ds(n * TPG, TPG)]

        def tile4(i, u):
            return ring[i][u][:].rearrange("p (q c) -> p q c", q=TPG)

        def bank4(i):
            return bank[i][:].rearrange("p (q c) -> p q c", q=TPG)

        def beside(row, n=TPG):
            return row.unsqueeze(1).to_broadcast([P, n, row.shape[1]])

        def ln_stats(dve, own, mark, w, k, n, u, src):
            for q in range(TPG):
                own.do(dve.bn_stats(bn6[w][u][:, q], one(src, n * TPG + q)))
            own.sync_apart()
            after(dve, mark + "_rstd", k - 2)
            for q in range(TPG):
                last = dve.bn_aggr(mv[w][u][:, q], bn6[w][u][:, q])
            last.then_inc(S(mark + "_stats"), 1)

        def ln_rstd(pool, own, mark, w, k, n, u):
            after(pool, mark + "_stats", k)
            own(pool.tensor_scalar(ve[w][u][:], mv[w][u][:, :, 1], EPS, None, ALU.add))
            own(pool.tensor_tensor(rs[w][u][:], ve[w][u][:], mhalf[:], ALU.pow))
            own(pool.tensor_tensor(nm[w][u][:], mv[w][u][:, :, 0], rs[w][u][:], ALU.mult))
            own(pool.tensor_copy(group(rsa, n), rs[w][u][:]))
            pool.tensor_tensor(group(nma, n), zero4[:], nm[w][u][:], ALU.subtract).then_inc(S(mark + "_rstd"), 1)

        def ln_scale(act, mark, k, n, u, src, dst):
            after(act, mark + "_rstd", k)
            after(act, mark + "_turned", k - 2)
            for q in range(TPG):
                j = n * TPG + q
                last = act.activation(dst[:, q * C:(q + 1) * C], one(src, j), ACT.Identity,
                                      bias=nma[:, ds(j, 1)], scale=rsa[:, ds(j, 1)])
            last.then_inc(S(mark + "_z"), 1)

        def ln_turn(pe, mark, k, n, u, src, ps):
            after(pe, mark + "_z", k)
            after(pe, mark + "_zT", k - 2)
            for q in range(TPG):
                last = pe.transpose(ps[:, q * C:(q + 1) * C], src[:, q * C:(q + 1) * C], ident[:])
            last.then_inc(S(mark + "_turned"), 1)

        def pool_rest(pool, own):
            prime(pool, "a_rstd", "hidden_staged")

            def stage_hidden(n, u):
                after(pool, "y", n - 2)
                pool.tensor_copy(ring[0][u][:].rearrange("p (b t) -> p b t", t=NS), HT[:, ds(n * 8, 8), :])\
                    .then_inc(S("hidden_staged"), 1)
            steps(pool, own, [(stage_hidden, 0), (lambda n, u: ln_rstd(pool, own, "a", 0, n, n, u), 1)], 8)
            phase_end(pool, 3)
            phase_end(pool, 4)
            phase_end(pool, 5)
            phase_end(pool, 6)

            prime(pool, "outs_staged")

            def stage_outs(n, u):
                after(pool, "outs_turned", n - 2)
                pool.tensor_copy(ring[3][u][:].rearrange("p (b e s) -> p e b s", b=4, e=E0),
                                 OT[:, :, ds(n * 8, 4), :]).then_inc(S("outs_staged"), 1)
            steps(pool, own, [(stage_outs, 0)], 0)
            phase_end(pool, 7)

            prime(pool, "kv_rstd")
            steps(pool, own, [(lambda n, u: ln_rstd(pool, own, "kv", 0, n, n, u), 0)], 8)
            own(pool.memset(V[:, :, C:C + 1], 1.0))
            phase_end(pool, 8)

            prime(pool, "noise_rstd")
            pool.wait_ge(s_cond, 16)

            def condition(n, u):
                pool.tensor_tensor(group(condb, n), group(condb, n), beside(ROW["b2"]), ALU.add)
            steps(pool, own, [(lambda n, u: ln_rstd(pool, own, "noise", 0, n, n, u), 0), (condition, 0)], 8)
            phase_end(pool, 9)

            prime(pool, "q_rstd", "k_staged", "v_staged", "m_rstd", "p_rstd", "sums_staged")
            for it in range(ITERS):
                def k_of(n, it=it):
                    return n + it * NG

                def stage_k(n, u):
                    after(pool, "attn_logits", k_of(n - 2))
                    pool.tensor_copy(ring[3][u][:], kT[:, ds(n * 512, 512)]).then_inc(S("k_staged"), 1)

                def stage_v(n, u):
                    after(pool, "updated", k_of(n - 2))
                    pool.tensor_copy(vst[u][:], group(V, n)).then_inc(S("v_staged"), 1)
                steps(pool, own, [(lambda n, u: ln_rstd(pool, own, "q", 0, k_of(n), n, u), 0), (stage_k, 1),
                                  (stage_v, 2)], 8, peel=4)
                phase_end(pool, 10 + 2 * it)

                def stage_sums(n, u):
                    after(pool, "mlp_added", k_of(n - 2))
                    pool.tensor_tensor(tile4(3, u), group(slots, n), group(condb, n), ALU.add)\
                        .then_inc(S("sums_staged"), 1)
                steps(pool, own, [(lambda n, u: ln_rstd(pool, own, "m", 0, k_of(n), n, u), 0), (stage_sums, 1),
                                  (lambda n, u: ln_rstd(pool, own, "p", 1, k_of(n), n, u), 3)], 16, peel=4)
                phase_end(pool, 11 + 2 * it)

            prime(pool, "f_rstd", "zT_kept")

            def low_zT(n, u):
                after(pool, "zT_high", n)
                pool.tensor_tensor(zT2[1][:, ds(n * 512, 512)], ring[2][u][:], ring[1][u][:], ALU.subtract)\
                    .then_inc(S("zT_kept"), 1)
            steps(pool, own, [(lambda n, u: ln_rstd(pool, own, "f", 0, n, n, u), 0), (low_zT, 1)], 8)
            phase_end(pool, 16)
            phase_end(pool, 17)

        def route(dve, own, e, pos):
            tt, tsc, stt = dve.tensor_tensor, dve.tensor_scalar, dve.scalar_tensor_tensor
            L, pr_, h1_, h2_, t_ = (b[:, :, 0:e] for b in (lg, pb, oh1, oh2, tmpE))
            idx = iotaE[:, 0:e].unsqueeze(1).to_broadcast([P, NT, e])
            own(dve.tensor_reduce(ra, L, AX_X, ALU.max))
            tt(pr_, L, bc(ra, e), ALU.subtract).then_inc(S("route_shifted"), 1)
            dve.wait_ge(S("route_exp"), 1 if pos else 2)
            own(dve.tensor_reduce(rb, pr_, AX_X, ALU.add))
            own(dve.reciprocal(rc, rb))
            own(tt(pr_, pr_, bc(rc, e), ALU.mult))
            for m, i, oh, src in ((m1, i1, h1_, pr_), (m2, i2, h2_, t_)):
                own(dve.tensor_reduce(m, src, AX_X, ALU.max))
                own(tt(oh, src, bc(m, e), ALU.is_equal))
                own(tt(oh, oh, idx, ALU.mult))
                own(dve.tensor_reduce(i, oh, AX_X, ALU.min))
                own(tt(oh, idx, bc(i, e), ALU.is_equal))
                if m is m1:
                    own(stt(t_, oh, -4.0, pr_, ALU.mult, ALU.add))

        def dve_rest(dve, own):
            tt, tsc, stt = dve.tensor_tensor, dve.tensor_scalar, dve.scalar_tensor_tensor
            prime(dve, "a_stats", "logits_kept")

            def add_output(n, u):
                after(dve, "y", n)
                for q in range(TPG):
                    j = n * TPG + q
                    own.do(stt(one(X, j), bank[u][:, q * C:(q + 1) * C], keep[:, ds(j, 1)], one(X, j),
                               ALU.mult, ALU.add))
                own.sync_apart()
                ln_stats(dve, own, "a", 0, n, n, u, X)

            def keep_logits(k, n, u, e):
                after(dve, "router", k)
                dve.tensor_copy(group(lg, n)[:, :, 0:e], bank[4 + u][:, 0:TPG * e].rearrange("p (q e) -> p q e", e=e))\
                    .then_inc(S("logits_kept"), 1)
            steps(dve, own, [(add_output, 0), (lambda n, u: keep_logits(n, n, u, E0), 2)], 16)
            phase_end(dve, 3)

            route(dve, own, E0, True)
            dve.nop().then_inc(S("picked"), 1)
            for k, (oh, i, sd, sc) in enumerate(((oh1, i1, sd1, sc1), (oh2, i2, sd2, sc2))):
                ps = bank[k][:].rearrange("p (j e) -> p j e", e=E0)
                dve.wait_ge(S("counted"), k + 1)
                own(tt(tmpE, ps, oh, ALU.mult))
                own(dve.tensor_reduce(ra, tmpE, AX_X, ALU.add))
                own(tsc(ra, ra, -1.0, None, ALU.add))
                own.do(tsc(rb, ra, float(CAP), None, ALU.is_lt))
                own(tsc(rc, ra, float(CAP - 1), None, ALU.min))
                own(stt(sc, i, float(CAP), rc, ALU.mult, ALU.add))
                own(tsc(sc, sc, 100.0 * CAP, None, ALU.add))
                own(stt(sd, sc, 1.0, rb, ALU.add, ALU.mult))
                own(tsc(sd, sd, -1.0, None, ALU.add))
            phase_end(dve, 4)

            prime(dve, "places", "placed_hi")

            def places(n, u):
                after(dve, "dispatched", n - 2)
                for q in range(TPG):
                    j = n * TPG + q
                    own.do(tsc(ring[2][u][:, q * C:(q + 1) * C], iota[:], sd1[:, ds(j, 1)], None, ALU.is_equal))
                own.sync()
                for q in range(TPG):
                    j = n * TPG + q
                    cs = slice(q * C, (q + 1) * C)
                    last = stt(ring[1][u][:, cs], iota[:], sd2[:, ds(j, 1)], ring[2][u][:, cs], ALU.is_equal, ALU.add)
                last.then_inc(S("places"), 1)

            def keep_hi(n, u):
                after(dve, "dispatched", n)
                dve.tensor_copy(BT[:, :, ds(n * 8 + 4, 4), :],
                                bank[2 * u + 1][:].rearrange("p (b e s) -> p e b s", b=4, e=E0))\
                    .then_inc(S("placed_hi"), 1)
            steps(dve, own, [(places, 0), (keep_hi, 1)], 8)
            phase_end(dve, 5)

            for p in range(E0 // 2):
                u = p % 2
                dve.wait_ge(S("fc"), p + 1)
                dve.wait_ge(S("silu"), p + 1)
                if p >= 2:
                    dve.wait_ge(S("down"), 2 * (p - 1))
                tt(ring[1][u][:], ring[0][u][:], bank[2 + u][:], ALU.mult).then_inc(S("gated"), 1)
                dve.wait_ge(S("down"), 2 * p + 1)
                dve.tensor_copy(OT[:, 2 * p], bank[4 + 2 * u][:].rearrange("p (b s) -> p b s", s=CAP))\
                    .then_inc(S("out_even"), 1)
            phase_end(dve, 6)

            prime(dve, "weights", "x_added")

            def weights(n, u):
                after(dve, "weights_turned", n - 2)
                for q in range(TPG):
                    j = n * TPG + q
                    cs = slice(q * C, (q + 1) * C)
                    own.do(tsc(ring[0][u][:, cs], iota[:], sc1[:, ds(j, 1)], m1[:, ds(j, 1)], ALU.is_equal, ALU.mult))
                    own.do(tsc(ring[1][u][:, cs], iota[:], sc2[:, ds(j, 1)], m2[:, ds(j, 1)], ALU.is_equal, ALU.mult))
                own.sync()
                tt(ring[0][u][:], ring[0][u][:], ring[1][u][:], ALU.add).then_inc(S("weights"), 1)

            def add_collected(n, u):
                after(dve, "collected", n)
                tt(group(X, n), group(X, n), bank4(6 + u), ALU.add).then_inc(S("x_added"), 1)
            steps(dve, own, [(weights, 0), (add_collected, 2)], 16)
            phase_end(dve, 7)

            prime(dve, "kv_stats", "v_kept")
            for i, (sem_, dst, bk) in enumerate((("wvu", wvu[:], bank[6][:, 0:C]), ("bvu", bvu[:], bank[7][:, 0:C]))):
                dve.wait_ge(S("folded"), i + 1)
                if i == 0:
                    dve.tensor_copy(dst, bk).then_inc(S("folded_kept"), 1)
                else:
                    tt(dst, bk, ROW["bu"], ALU.add).then_inc(S("folded_kept"), 1)
            dve.wait_ge(s_ctxk, 16)

            def keep_v(n, u):
                after(dve, "v", n)
                tt(group(V, n)[:, :, 0:C], bank4(4 + u), beside(bvu[:]), ALU.add).then_inc(S("v_kept"), 1)
            steps(dve, own, [(lambda n, u: ln_stats(dve, own, "kv", 0, n, n, u, ctxk), 0), (keep_v, 2)], 8)
            phase_end(dve, 8)

            prime(dve, "noise_stats", "noise_turned")

            def begin_slots(n, u):
                after(dve, "noise_z", n)
                own(tt(tile4(0, u), tile4(0, u), beside(qsig[:]), ALU.mult))
                tt(group(slots, n), tile4(0, u), beside(ROW["q_mu"]), ALU.add).then_inc(S("noise_turned"), 1)
            dve.wait_ge(s_l1, 32)

            def split_weights(n, u):
                w = W1B[:, ds(n * 512, 512)]
                hi, lo = (wgu2[i][:, ds(n, 1)].rearrange("p a f -> p (a f)") for i in range(2))
                own(tsc(ring[1][u][:].bitcast(U32), w.bitcast(U32), HIGH12, None, ALU.bitwise_and))
                own.do(dve.tensor_copy(hi, ring[1][u][:]))
                own.do(tt(lo, w, ring[1][u][:], ALU.subtract))
            steps(dve, own, [(lambda n, u: ln_stats(dve, own, "noise", 0, n, n, u, X), 0), (split_weights, 0),
                             (begin_slots, 1)], 16)
            phase_end(dve, 9)

            prime(dve, "q_stats", "attn_max", "attn", "updated_kept", "m_stats", "mlp_added", "p_stats", "p_turned")
            for it in range(ITERS):
                def k_of(n, it=it):
                    return n + it * NG

                def attn_max(n, u):
                    after(dve, "attn_logits", k_of(n))
                    own(dve.tensor_reduce(ta4[u][:], bank[4 + u][:, 0:TPG * NS].rearrange("p (q s) -> p q s", s=NS),
                                          AX_X, ALU.max))
                    tsc(mx[u][:], ta4[u][:], -SCALE, None, ALU.mult).then_inc(S("attn_max"), 1)

                def attn(n, u):
                    after(dve, "attn_exp", k_of(n))
                    own(dve.reciprocal(tb4[u][:], sm[u][:]))
                    for q in range(TPG):
                        cs = slice(q * NS, (q + 1) * NS)
                        last = tsc(ring[4][u][:, cs], ring[4][u][:, cs], tb4[u][:, q:q + 1], EPS_ATTN, ALU.mult, ALU.add)
                    last.then_inc(S("attn"), 1)

                def update(n, u):
                    after(dve, "updated", k_of(n))
                    for q in range(TPG):
                        own.do(dve.reciprocal(tc4[u][:, q:q + 1], upd_ps(q)[:, C:C + 1]))
                    own.sync()
                    for q in range(TPG):
                        s_ = one(slots, n * TPG + q)
                        last = own.do(stt(s_, upd_ps(q)[:, 0:C], tc4[u][:, q:q + 1], s_, ALU.mult, ALU.add))
                    own.sync()
                    dve.nop().then_inc(S("updated_kept"), 1)
                steps(dve, own, [(lambda n, u: ln_stats(dve, own, "q", 0, k_of(n), n, u, slots), 0),
                                 (update, 4), (attn_max, 2), (attn, 3)], 28, peel=4)
                phase_end(dve, 10 + 2 * it)

                def add_mlp(n, u):
                    after(dve, "mlp", k_of(n))
                    after(dve, "sums_staged", k_of(n))
                    tt(group(slots, n), bank4(4 + u), tile4(3, u), ALU.add).then_inc(S("mlp_added"), 1)
                    after(dve, "mlp_added", k_of(n))
                    ln_stats(dve, own, "p", 1, k_of(n), n, u, slots)

                def affine(n, u):
                    after(dve, "p_z", k_of(n))
                    own(tt(tile4(4, u), tile4(4, u), beside(ROW["p_g"]), ALU.mult))
                    tt(group(slots, n), tile4(4, u), beside(ROW["p_b"]), ALU.add).then_inc(S("p_turned"), 1)
                steps(dve, own, [(lambda n, u: ln_stats(dve, own, "m", 0, k_of(n), n, u, slots), 0),
                                 (add_mlp, 3), (affine, 4)], 18, peel=4)
                phase_end(dve, 11 + 2 * it)

            prime(dve, "f_stats", "zT_high")

            def add_slots(n, u):
                own.do(tt(group(X, n), group(X, n), group(slots, n), ALU.add))
                own.sync_apart()
                ln_stats(dve, own, "f", 0, n, n, u, X)

            def high_zT(n, u):
                after(dve, "f_zT", n)
                after(dve, "zT_kept", n - 2)
                own(tsc(ring[1][u][:].bitcast(U32), ring[2][u][:].bitcast(U32), HIGH12, None, ALU.bitwise_and))
                dve.tensor_copy(zT2[0][:, ds(n * 512, 512)], ring[1][u][:]).then_inc(S("zT_high"), 1)
            steps(dve, own, [(add_slots, 0), (high_zT, 1), (lambda n, u: keep_logits(n + NG, n, u, E1), 2)], 12)
            dve.wait_ge(S("logits_kept"), 2 + 2 * NG)
            route(dve, own, E1, False)
            own(tt(ra, m1, m2, ALU.add))
            own(dve.reciprocal(rb, ra))
            own.do(tt(m1, m1, rb, ALU.mult))
            own(tt(m2, m2, rb, ALU.mult))
            own.do(tt(oh1[:, :, 0:E1], oh1[:, :, 0:E1], bc(m1, E1), ALU.mult))
            own(tt(oh2[:, :, 0:E1], oh2[:, :, 0:E1], bc(m2, E1), ALU.mult))
            own(tt(cw, oh1[:, :, 0:E1], oh2[:, :, 0:E1], ALU.add))
            phase_end(dve, 16)

            prime(dve, "y_added")
            prime(dve, "prod", lead=2 * FC)
            units = E1 * FC

            def add_expert(n, e):
                after(dve, "ffn_y", n * E1 + e)
                own.sync()
                for q in range(TPG):
                    j = n * TPG + q
                    own.do(stt(one(X, j), bank[6 + e % 2][:, q * C:(q + 1) * C], one(cw, j)[:, e:e + 1], one(X, j),
                               ALU.mult, ALU.add))
                own.sync()
                dve.nop().then_inc(S("y_added"), 1)
            with dve.Fori(0, NG) as n:
                own.loop(n, E1 * TPG)
                for e in range(E1):
                    for f in range(FC):
                        k = e * FC + f
                        after(dve, "ffn_up", n * units + k)
                        after(dve, "ffn_silu", n * units + k)
                        after(dve, "ffn_y", n * E1 + (e - 2))
                        tt(ring[2 + f][e % 2][:], ring[f][e % 2][:], bank[2 + f][:], ALU.mult).then_inc(S("prod"), 1)
                    if e > 0:
                        add_expert(n, e - 1)
                add_expert(n, E1 - 1)
                own.end(NG, E1 * TPG)
            phase_end(dve, 17)

        def act_rest(act, own):
            prime(act, "a_z", "a_zT")

            def keep_zT(mark, k, n, u, src, dst, g=None, b=None, free=None):
                after(act, mark + "_turned", k)
                after(act, free, k - 2)
                if g is None:
                    act.activation(dst, src, ACT.Copy).then_inc(S(mark + "_zT"), 1)
                else:
                    act.activation(dst, src, ACT.Identity, bias=b, scale=g).then_inc(S(mark + "_zT"), 1)
            steps(act, own, [(lambda n, u: keep_zT("a", n, n, u, bank[2 + u][:], ring[2][u][:], free="router"), 2),
                             (lambda n, u: ln_scale(act, "a", n, n, u, X, ring[1][u]), 1)], 0)
            phase_end(act, 3)
            act.wait_ge(S("route_shifted"), 1)
            act.activation(pb, pb, ACT.Exp).then_inc(S("route_exp"), 1)
            phase_end(act, 4)

            prime(act, "rows_scaled", "placed_lo")

            def scale_rows(n, u):
                after(act, "dispatched", n - 2)
                for q in range(TPG):
                    j = n * TPG + q
                    last = act.activation(ring[0][u][:, q * C:(q + 1) * C], one(X, j), ACT.Identity,
                                          bias=nma[:, ds(j, 1)], scale=rsa[:, ds(j, 1)])
                last.then_inc(S("rows_scaled"), 1)

            def keep_lo(n, u):
                after(act, "dispatched", n)
                act.activation(BT[:, :, ds(n * 8, 4), :], bank[2 * u][:].rearrange("p (b e s) -> p e b s", b=4, e=E0),
                               ACT.Copy).then_inc(S("placed_lo"), 1)
            steps(act, own, [(scale_rows, 0), (keep_lo, 1)], 0)
            act.preload_act_table(ACT.Silu)
            phase_end(act, 5)

            for p in range(E0 // 2):
                u = p % 2
                act.wait_ge(S("gate"), p + 1)
                if p >= 2:
                    act.wait_ge(S("gated"), p - 1)
                act.activation(ring[0][u][:], bank[u][:], ACT.Silu).then_inc(S("silu"), 1)
                act.wait_ge(S("down"), 2 * p + 2)
                act.activation(OT[:, 2 * p + 1], bank[5 + 2 * u][:].rearrange("p (b s) -> p b s", s=CAP), ACT.Copy)\
                    .then_inc(S("out_odd"), 1)
            phase_end(act, 6)

            prime(act, "weights_T", "outs_lo", "outs_hi", "outs_staged_hi")

            def weights_T(n, u):
                after(act, "weights_turned", n)
                after(act, "collected", n - 2)
                act.activation(ring[2][u][:], bank[u][:], ACT.Copy).then_inc(S("weights_T"), 1)

            def outs_kept(n, u):
                after(act, "outs_turned", n)
                act.activation(outs(u, 0), bank[2 + u][:], ACT.Copy).then_inc(S("outs_lo"), 1)
                act.activation(outs(u, 1), bank[4 + u][:], ACT.Copy).then_inc(S("outs_hi"), 1)

            def stage_hi(n, u):
                after(act, "outs_turned", n - 2)
                act.activation(ring[4][u][:].rearrange("p (b e s) -> p e b s", b=4, e=E0),
                               OT[:, :, ds(n * 8 + 4, 4), :], ACT.Copy).then_inc(S("outs_staged_hi"), 1)
            steps(act, own, [(stage_hi, 0), (weights_T, 1), (outs_kept, 1)], 0)
            act.preload_act_table(ACT.Exp)
            act.activation(qsig[:], ROW["q_logsig"], ACT.Exp)
            act.activation(bvb[:], COL["bv"].to_broadcast([P, P]), ACT.Copy)
            phase_end(act, 7)

            prime(act, "kv_z", "kv_zT", "k_kept")

            def keep_k(n, u):
                after(act, "k", n)
                act.activation(kT[:, ds(n * 512, 512)], bank[2 + u][:], ACT.Identity, bias=COL["bk"])\
                    .then_inc(S("k_kept"), 1)
            steps(act, own, [(keep_k, 2),
                             (lambda n, u: keep_zT("kv", n, n, u, bank[u][:], ring[1][u][:], COL["kv_g"], COL["kv_b"],
                                                   free="v"), 1),
                             (lambda n, u: ln_scale(act, "kv", n, n, u, ctxk, ring[0][u]), 0)], 0)
            phase_end(act, 8)

            prime(act, "noise_z")
            steps(act, own, [(lambda n, u: ln_scale(act, "noise", n, n, u, X, ring[0][u]), 0)], 0)
            phase_end(act, 9)

            prime(act, "q_z", "q_zT", "q_kept", "attn_exp", "m_z", "m_zT", "gelu", "p_z")
            for it in range(ITERS):
                def k_of(n, it=it):
                    return n + it * NG

                def keep_q(n, u):
                    after(act, "q", k_of(n))
                    after(act, "attn_logits", k_of(n - 2))
                    act.activation(ring[2][u][:], bank[2 + u][:], ACT.Identity, bias=COL["bq"]).then_inc(S("q_kept"), 1)

                def attn_exp(n, u):
                    after(act, "attn_max", k_of(n))
                    after(act, "updated", k_of(n - 2))
                    for q in range(TPG):
                        cs = slice(q * NS, (q + 1) * NS)
                        last = act.activation(ring[4][u][:, cs], bank[4 + u][:, cs], ACT.Exp, bias=mx[u][:, q:q + 1],
                                              scale=SCALE, accum_out=sm[u][:, q:q + 1])
                    last.then_inc(S("attn_exp"), 1)
                steps(act, own, [(keep_q, 2),
                                 (lambda n, u: keep_zT("q", k_of(n), n, u, bank[u][:], ring[1][u][:], COL["q_g"],
                                                       COL["q_b"], free="q"), 1),
                                 (attn_exp, 3),
                                 (lambda n, u: ln_scale(act, "q", k_of(n), n, u, slots, ring[0][u]), 0)],
                      0, peel=4)
                act.preload_act_table(ACT.Gelu)
                phase_end(act, 10 + 2 * it)

                def gelu(n, u):
                    after(act, "mlp_hidden", k_of(n))
                    after(act, "mlp", k_of(n - 2))
                    act.activation(ring[2][u][:], bank[2 + u][:], ACT.Gelu, bias=COL["b1"]).then_inc(S("gelu"), 1)
                steps(act, own, [(gelu, 2),
                                 (lambda n, u: keep_zT("m", k_of(n), n, u, bank[u][:], ring[1][u][:], COL["m_g"],
                                                       COL["m_b"], free="mlp_hidden"), 1),
                                 (lambda n, u: ln_scale(act, "m", k_of(n), n, u, slots, ring[0][u]), 0),
                                 (lambda n, u: ln_scale(act, "p", k_of(n), n, u, slots, ring[4][u]), 3)], 0, peel=4)
                act.preload_act_table(ACT.Exp)
                phase_end(act, 11 + 2 * it)

            prime(act, "f_z", "f_zT")

            def keep_zT_f(n, u):
                after(act, "zT_kept", n - 2)
                keep_zT("f", n, n, u, bank[u][:], ring[2][u][:], free="f_router")
            steps(act, own, [(keep_zT_f, 1), (lambda n, u: ln_scale(act, "f", n, n, u, X, ring[0][u]), 0)], 0)
            act.wait_ge(S("route_shifted"), 2)
            act.activation(pb[:, :, 0:E1], pb[:, :, 0:E1], ACT.Exp).then_inc(S("route_exp"), 1)
            act.preload_act_table(ACT.Silu)
            phase_end(act, 16)

            prime(act, "ffn_silu")
            units = E1 * FC
            with act.Fori(0, NG) as n:
                for e in range(E1):
                    for f in range(FC):
                        k = n * units + e * FC + f
                        after(act, "ffn_gate", k)
                        after(act, "prod", k - 2 * FC, 2 * FC)
                        act.activation(ring[f][e % 2][:], bank[f][:], ACT.Silu).then_inc(S("ffn_silu"), 1)
            phase_end(act, 17)

        def pe_rest(pe, own):
            mm = pe.matmul
            prime(pe, "y", "a_turned", "router")

            def hidden_out(n, u):
                after(pe, "hidden_staged", n)
                after(pe, "a_stats", n - 2)
                for q in range(TPG):
                    ps = bank[u][:, q * C:(q + 1) * C]
                    mm(ps, ring[0][u][:, q * C:(q + 1) * C], W["WoT"], start=True, stop=False)
                    last = mm(ps, ones[0:1, :], ROW["b_out"][0:1, :], start=False, stop=True)
                last.then_inc(S("y"), 1)

            def router(mark, k, n, u, w, e, zT):
                after(pe, mark + "_zT", n)
                after(pe, "logits_kept", k - 2)
                for q in range(TPG):
                    last = mm(bank[4 + u][:, q * e:(q + 1) * e], zT[:, q * C:(q + 1) * C], w[:], start=True, stop=True)
                last.then_inc(S("router"), 1)
            steps(pe, own, [(hidden_out, 0), (lambda n, u: router("a", n, n, u, wr0, E0, ring[2][u]), 2),
                            (lambda n, u: ln_turn(pe, "a", n, n, u, ring[1][u], bank[2 + u]), 1)], 0)
            phase_end(pe, 3)

            pe.wait_ge(S("picked"), 1)
            rows1, rows2 = (b.rearrange("p j e -> p (j e)") for b in (oh1, oh2))
            mm(bank[0][:], tri[:], rows1, start=True, stop=True).then_inc(S("counted"), 1)
            mm(bank[1][:], tri[:], rows2, start=True, stop=False)
            mm(bank[1][:], blk[:], rows1, start=False, stop=True).then_inc(S("counted"), 1)
            phase_end(pe, 4)

            prime(pe, "dispatched")

            def dispatch(n, u):
                after(pe, "rows_scaled", n)
                after(pe, "places", n)
                after(pe, "placed_lo", n - 2)
                after(pe, "placed_hi", n - 2)
                for q in range(TPG):
                    for b in range(2):
                        r = slice(b * NS, (b + 1) * NS)
                        last = mm(bank[2 * u + b][:, q * C:(q + 1) * C], ring[0][u][r, q * C:(q + 1) * C],
                                  ring[1][u][r, q * C:(q + 1) * C], start=True, stop=True)
                last.then_inc(S("dispatched"), 1)
            steps(pe, own, [(dispatch, 0)], 0)
            phase_end(pe, 5)

            pe.wait_ge(s_l0, 32)

            def down(p):
                u = p % 2
                pe.wait_ge(S("gated"), p + 1)
                for i, kept in ((0, "out_even"), (1, "out_odd")):
                    if p >= 2:
                        pe.wait_ge(S(kept), p - 1)
                    r = slice(i * H0, (i + 1) * H0)
                    mm(bank[4 + 2 * u + i][:], wpj[r, p, :], ring[1][u][r, :], start=True, stop=True)\
                        .then_inc(S("down"), 1)
            for p in range(E0 // 2):
                u = p % 2
                for bk, cs, name, free in ((u, slice(0, H0), "gate", "silu"), (2 + u, slice(H0, 2 * H0), "fc", "gated")):
                    if p >= 2:
                        pe.wait_ge(S(free), p - 1)
                    for i in range(2):
                        last = mm(bank[bk][i * H0:(i + 1) * H0, :], wgf[:, 2 * p + i, cs],
                                  BT[:, 2 * p + i].rearrange("p b s -> p (b s)"), start=True, stop=True)
                    last.then_inc(S(name), 1)
                if p:
                    down(p - 1)
            down(E0 // 2 - 1)
            phase_end(pe, 6)

            prime(pe, "weights_turned", "outs_turned", "collected")

            def turn_collect(n, u):
                after(pe, "weights", n)
                after(pe, "weights_T", n - 2)
                for q in range(TPG):
                    last = pe.transpose(bank[u][:, q * C:(q + 1) * C], ring[0][u][:, q * C:(q + 1) * C], ident[:])
                last.then_inc(S("weights_turned"), 1)
                after(pe, "outs_staged", n)
                after(pe, "outs_staged_hi", n)
                after(pe, "outs_lo", n - 2)
                after(pe, "outs_hi", n - 2)
                for i in range(2):
                    for q in range(TPG):
                        last = pe.transpose(bank[2 + 2 * i + u][:, q * C:(q + 1) * C],
                                            ring[3 + i][u][:, q * C:(q + 1) * C], ident[:])
                last.then_inc(S("outs_turned"), 1)

            def collect(n, u):
                after(pe, "weights_T", n)
                after(pe, "outs_lo", n)
                after(pe, "outs_hi", n)
                after(pe, "x_added", n - 2)
                for b in range(2 * TPG):
                    q, r = b // 2, b % 2
                    last = mm(bank[6 + u][r * NS:(r + 1) * NS, q * C:(q + 1) * C], ring[2][u][:, b * NS:(b + 1) * NS],
                              outs(u, r)[:, q * C:(q + 1) * C], start=True, stop=True)
                last.then_inc(S("collected"), 1)
            steps(pe, own, [(turn_collect, 0), (collect, 1)], 0)
            phase_end(pe, 7)

            mm(bank[6][:, 0:C], W["wvT"], W["wu"], start=True, stop=True).then_inc(S("folded"), 1)
            mm(bank[7][:, 0:C], bvb[:], W["wu"], start=True, stop=True).then_inc(S("folded"), 1)
            pe.wait_ge(S("folded_kept"), 2)
            prime(pe, "kv_turned", "k", "v")

            def keys_values(n, u):
                after(pe, "kv_zT", n)
                after(pe, "k_kept", n - 2)
                mm(bank[2 + u][:], W["wk"], ring[1][u][:], start=True, stop=True).then_inc(S("k"), 1)
                after(pe, "v_kept", n - 2)
                for q in range(TPG):
                    last = mm(bank[4 + u][:, q * C:(q + 1) * C], ring[1][u][:, q * C:(q + 1) * C], wvu[:],
                              start=True, stop=True)
                last.then_inc(S("v"), 1)
            steps(pe, own, [(keys_values, 1), (lambda n, u: ln_turn(pe, "kv", n, n, u, ring[0][u], bank[u]), 0)], 0)
            phase_end(pe, 8)
            phase_end(pe, 9)

            prime(pe, "q_turned", "q", "attn_logits", "updated", "m_turned", "mlp_hidden", "mlp")
            for it in range(ITERS):
                def k_of(n, it=it):
                    return n + it * NG

                def queries(n, u):
                    after(pe, "q_zT", k_of(n))
                    after(pe, "q_kept", k_of(n - 2))
                    mm(bank[2 + u][:], W["wq"], ring[1][u][:], start=True, stop=True).then_inc(S("q"), 1)

                def attn_logits(n, u):
                    after(pe, "q_kept", k_of(n))
                    after(pe, "k_staged", k_of(n))
                    after(pe, "attn_exp", k_of(n - 2))
                    for b in range(2 * TPG):
                        q, r = b // 2, b % 2
                        cs = slice(b * NS, (b + 1) * NS)
                        last = mm(bank[4 + u][r * NS:(r + 1) * NS, q * NS:(q + 1) * NS], ring[3][u][:, cs],
                                  ring[2][u][:, cs], start=True, stop=True)
                    last.then_inc(S("attn_logits"), 1)

                def updates(n, u):
                    after(pe, "attn", k_of(n))
                    after(pe, "v_staged", k_of(n))
                    after(pe, "updated_kept", k_of(n - 1))
                    for b in range(2 * TPG):
                        q, r = b // 2, b % 2
                        rs_ = slice(r * NS, (r + 1) * NS)
                        last = mm(upd_ps(q)[rs_, :], ring[4][u][rs_, q * NS:(q + 1) * NS], vst[u][rs_, q, :],
                                  start=True, stop=True)
                    last.then_inc(S("updated"), 1)
                steps(pe, own, [(attn_logits, 2), (queries, 1), (updates, 3),
                                (lambda n, u: ln_turn(pe, "q", k_of(n), n, u, ring[0][u], bank[u]), 0)],
                      0, peel=4)
                phase_end(pe, 10 + 2 * it)

                def mlp_hidden(n, u):
                    after(pe, "m_zT", k_of(n))
                    after(pe, "gelu", k_of(n - 2))
                    mm(bank[2 + u][:], W["w1"], ring[1][u][:], start=True, stop=True).then_inc(S("mlp_hidden"), 1)

                def mlp(n, u):
                    after(pe, "gelu", k_of(n))
                    after(pe, "mlp_added", k_of(n - 2))
                    for q in range(TPG):
                        last = mm(bank[4 + u][:, q * C:(q + 1) * C], ring[2][u][:, q * C:(q + 1) * C], W["w2"],
                                  start=True, stop=True)
                    last.then_inc(S("mlp"), 1)
                steps(pe, own, [(mlp, 2), (mlp_hidden, 1),
                                (lambda n, u: ln_turn(pe, "m", k_of(n), n, u, ring[0][u], bank[u]), 0)], 0, peel=4)
                phase_end(pe, 11 + 2 * it)

            prime(pe, "f_turned", "f_router")

            def router_f(n, u):
                router("f", n + NG, n, u, wr1, E1, ring[2][u])
                pe.nop().then_inc(S("f_router"), 1)
            steps(pe, own, [(router_f, 1), (lambda n, u: ln_turn(pe, "f", n, n, u, ring[0][u], bank[u]), 0)], 0)
            phase_end(pe, 16)

            pe.wait_ge(s_l1, 32)
            prime(pe, "ffn_gate", "ffn_up", "ffn_y")
            units = E1 * FC

            def down(n, e):
                after(pe, "prod", n * units + (e * FC + FC - 1), 2 * FC)
                after(pe, "y_added", n * E1 + (e - 2))
                for q in range(TPG):
                    for f in range(FC):
                        last = mm(bank[6 + e % 2][:, q * C:(q + 1) * C], ring[2 + f][e % 2][:, q * C:(q + 1) * C],
                                  wdn[:, e * FC + f, :], start=(f == 0), stop=(f == FC - 1))
                last.then_inc(S("ffn_y"), 1)

            def product(ps, e, at, n, name):
                for i, (w_, z_) in enumerate(((0, 0), (1, 0), (0, 1))):
                    last = mm(ps, wgu2[w_][:, e, at:at + P], zT2[z_][:, ds(n * 512, 512)],
                              start=(i == 0), stop=(i == 2))
                last.then_inc(S(name), 1)
            with pe.Fori(0, NG) as n:
                for e in range(E1):
                    for f in range(FC):
                        k = n * units + e * FC + f
                        after(pe, "ffn_silu", k - FC)
                        product(bank[f][:], e, f * P, n, "ffn_gate")
                        after(pe, "prod", k - FC, 2 * FC)
                        product(bank[2 + f][:], e, F1 + f * P, n, "ffn_up")
                    if e > 0:
                        down(n, e - 1)
                down(n, E1 - 1)
            phase_end(pe, 17)

        @block.sync
        def _(sp):
            sp.dma_start(X[:], d["x"]).then_inc(s_x, 16)
            sp.dma_start(ctxT, d["ctxT"]).then_inc(s_ctx, 16)
            for buf, name in ((wsq, "wsq"), (wat, "wat"), (cols, "cols"), (rows, "rows"), (battn, "battn"),
                              (h0T, "h0T"), (wr0, "wr0"), (wr1, "wr1")):
                sp.dma_start(buf[:], d[name]).then_inc(s_w, 16)
            sp.wait_ge(s_phase, 4 * 2)
            sp.dma_start(wgf, d["wgf"]).then_inc(s_l0, 16)
            sp.dma_start(wpj, d["wpj"]).then_inc(s_l0, 16)
            sp.wait_ge(s_phase, 4 * 3)
            sp.dma_start(ctxk, d["ctx_tok"]).then_inc(s_ctxk, 16)
            sp.wait_ge(s_phase, 4 * 6)
            sp.dma_start(condb, d["condb"]).then_inc(s_cond, 16)
            sp.wait_ge(s_l0, 32)
            sp.dma_start(wgu, d["wgu"]).then_inc(s_l1, 16)
            sp.dma_start(wdn, d["wdn"]).then_inc(s_l1, 16)
            sp.wait_ge(s_phase, 4 * LAST)
            sp.dma_start(out, X[:]).then_inc(s_out, 16)
            sp.wait_ge(s_out, 16)

        psL = [bank[g][0:BG, 0:NS] for g in range(2)]
        psT = [bank[2 + g][:, 0:BG] for g in range(2)]
        psC = [bank[4 + g][:, 0:2 * BG] for g in range(2)]
        psH = [bank[6 + g][:, 0:BG] for g in range(2)]

        def scan(eng, pair):
            pair(0, 0, None, None, False, True)
            pair(1, 0, 0, 0, False, True)
            with eng.Fori(1, NS) as t:
                pair(0, t, 1, t - 1, True, True)
                pair(1, t, 0, t, True, True)
            pair(0, NS, 1, NS - 1, True, False)
            pair(1, NS, None, None, True, False)

        @block.gpsimd
        def _(pool):
            own = Chain(pool, s_pool)
            for buf in (ident, tri, blk):
                own(pool.memset(buf[:], 0.0))
            own(pool.memset(ones[:], 1.0))
            own(pool.memset(mhalf[:], -0.5))
            own(pool.memset(zero4[:], 0.0))
            own(pool.affine_select(out=ident[:], in_=ident[:], compare_op=ALU.not_equal, fill=1.0, base=0,
                                      pattern=[[-1, P]], channel_multiplier=1))
            for b in range(2):
                own(pool.memset(blk[b * NS:(b + 1) * NS, b * NS:(b + 1) * NS], 1.0))
            own(pool.iota(iota[:], [[1, NSLOT]], base=0, channel_multiplier=0,
                             allow_small_or_imprecise_dtypes=True))
            own(pool.iota(iotaE[:], [[1, E0]], base=-100, channel_multiplier=0,
                             allow_small_or_imprecise_dtypes=True))
            own(pool.affine_select(out=tri[:], in_=blk[:], compare_op=ALU.is_ge, fill=0.0, base=0,
                                   pattern=[[1, P]], channel_multiplier=-1))
            own(pool.memset(parity[:], 0.0))
            for k in range(BG // 2 + 1):
                own(pool.affine_select(out=parity[:], in_=parity[:], compare_op=ALU.not_equal, fill=1.0,
                                       base=-2 * k, pattern=[[-1, 2], [0, NS]], channel_multiplier=1))
            pool.nop().then_inc(s_const, 1)
            pool.wait_ge(s_w, 16 * 8)
            for name in ("WcxT", "WhhT"):
                part = WP[name]
                own(pool.tensor_copy(part[:, 0], W[name]))
                own(pool.tensor_tensor(pr[:], W[name], part[:, 0], ALU.subtract))
                own(pool.tensor_copy(part[:, 1], pr[:]))
                own(pool.tensor_tensor(part[:, 2], pr[:], part[:, 1], ALU.subtract))
            for n in range(NG):
                js = slice(n * TPG, (n + 1) * TPG)
                pool.wait_ge(s_act, 2 * (n + 1))
                own(pool.tensor_tensor(EWf[:, js], EWf[:, js], EWp[0][:, js], ALU.subtract))
                own(pool.tensor_copy(EWp[1][:, js], EWf[:, js]))
                own(pool.tensor_tensor(EWp[2][:, js], EWf[:, js], EWp[1][:, js], ALU.subtract))
            pool.nop().then_inc(S("ew_split"), 1)
            phase_end(pool, 1)

            for g in range(2):
                pool.tensor_copy(h[g][:], h0T[:, g * BG:(g + 1) * BG]).then_inc(S(f"h_ready{g}"), 1)


            with pool.Fori(0, NT) as j:
                own.loop(j, 12)
                c, q, ch = one(cen, j), one(xhat, j), one(cenh, j)
                rh_, rl_, rlo_ = (v[:, ds(j, 1)].to_broadcast([P, C]) for v in (rh, rl, rlo))
                own.do(pool.tensor_tensor(cl[:], c, ch, ALU.subtract))
                own.apart(pool.tensor_tensor(er[:], ch, rh_, ALU.mult))
                own.do(pool.tensor_tensor(er[:], er[:], q, ALU.subtract))
                own.apart(pool.tensor_tensor(pr[:], ch, rl_, ALU.mult))
                own.do(pool.tensor_tensor(er[:], er[:], pr[:], ALU.add))
                own.apart(pool.tensor_tensor(pr2[:], cl[:], rh_, ALU.mult))
                own.do(pool.tensor_tensor(er[:], er[:], pr2[:], ALU.add))
                own.apart(pool.tensor_tensor(pr[:], cl[:], rl_, ALU.mult))
                own.do(pool.tensor_tensor(er[:], er[:], pr[:], ALU.add))
                own.apart(pool.tensor_tensor(pr2[:], c, rlo_, ALU.mult))
                own.apart(pool.tensor_tensor(er[:], er[:], pr2[:], ALU.add))
                own.apart(pool.tensor_tensor(c, q, er[:], ALU.add))
                own.end(NT, 12)
            c4 = cen.rearrange("p j (k i) -> p i j k", k=4)
            own.apart(pool.tensor_tensor(acc4[:], c4[:, 0], c4[:, 1], ALU.add))
            with pool.Fori(2, C // 4) as i:
                own.loop(i - 2, 1)
                own.apart(pool.tensor_tensor(acc4[:], acc4[:], c4[:, bass.ds(i, 1)].rearrange("p a j k -> p (a j) k"),
                                       ALU.add))
                own.end(C // 4 - 2, 1)
            own(pool.tensor_tensor(ta, acc4[:, :, 0], acc4[:, :, 1], ALU.add))
            own(pool.tensor_tensor(tb, ta, acc4[:, :, 2], ALU.add))
            own(pool.tensor_tensor(tc, tb, acc4[:, :, 3], ALU.add))
            pool.nop().then_inc(S("quotients_summed"), 1)
            phase_end(pool, 2)
            pool_rest(pool, own)

        @block.vector
        def _(dve):
            own = Chain(dve, s_dve)
            tt, tsc, stt = dve.tensor_tensor, dve.tensor_scalar, dve.scalar_tensor_tensor
            x16 = X[:].rearrange("p j (i l) -> p i j l", l=16)

            dve.wait_ge(s_x, 16)
            own(tt(a16[:], x16[:, 0], x16[:, 1], ALU.add))
            for i in range(2, 8):
                own(tt(a16[:], a16[:], x16[:, i], ALU.add))
            r4 = a16[:].rearrange("p j (r k) -> p j r k", r=4)
            r2 = a8[:].rearrange("p j (r k) -> p j r k", r=2)
            own(tt(r2, r4[:, :, 0::2, :], r4[:, :, 1::2, :], ALU.add))
            own(tt(a4[:], r2[:, :, 0, :], r2[:, :, 1, :], ALU.add))
            own(tt(a2[:], a4[:, :, 0::2], a4[:, :, 1::2], ALU.add))
            own(tt(ta, a2[:, :, 0], a2[:, :, 1], ALU.add))
            own(tsc(mean, ta, 1.0 / C, None, ALU.mult))
            own(tt(cen, X[:], bc(mean, C), ALU.subtract))
            own.do(tt(sq, cen, cen, ALU.mult))
            own(tsc(cenh.bitcast(U32), cen.bitcast(U32), HIGH12, None, ALU.bitwise_and))
            q4 = sq.rearrange("p j (k i) -> p i j k", k=4)
            own(tt(acc4[:], q4[:, 0], q4[:, 1], ALU.add))
            for i in range(2, 32):
                own(tt(acc4[:], acc4[:], q4[:, i], ALU.add))

            def sum4(dst):
                own(tt(ta, acc4[:, :, 0], acc4[:, :, 1], ALU.add))
                own(tt(tb, ta, acc4[:, :, 2], ALU.add))
                own(tt(dst, tb, acc4[:, :, 3], ALU.add))
            sum4(tc)
            own.do(tsc(var, tc, 1.0 / C, EPS, ALU.mult, ALU.add))
            own.sync()
            assert own.n == VAR_AT, own.n
            dve.wait_ge(S("root_ready"), 1)

            def split(hi, lo, a):
                own(tsc(hi.bitcast(U32), a.bitcast(U32), HIGH12, None, ALU.bitwise_and))
                own(tt(lo, a, hi, ALU.subtract))

            def product_error(ah, al, bh, bl, prod, err, t):
                own(tt(err, ah, bh, ALU.mult))
                own(tt(err, err, prod, ALU.subtract))
                for u_, v_ in ((ah, bl), (al, bh), (al, bl)):
                    own(tt(t, u_, v_, ALU.mult))
                    own(tt(err, err, t, ALU.add))
            for _ in range(2):
                own(dve.reciprocal(inv, std))
                split(sh, sl, std)
                own(tt(td, std, std, ALU.mult))
                product_error(sh, sl, sh, sl, td, te, tf)
                own(tt(ta, var, td, ALU.subtract))
                own(tt(ta, ta, te, ALU.subtract))
                own(tt(ta, ta, inv, ALU.mult))
                own(stt(std, ta, 0.5, std, ALU.mult, ALU.add))
            own(dve.reciprocal(rstd, std))
            split(sh, sl, std)
            split(rh, rl, rstd)
            own(tt(td, std, rstd, ALU.mult))
            product_error(sh, sl, rh, rl, td, te, tf)
            own(tsc(ta, td, -1.0, 1.0, ALU.mult, ALU.add))
            own(tt(ta, ta, te, ALU.subtract))
            own(tt(rlo, rstd, ta, ALU.mult))
            for j in range(0, NT, TPG):
                tt(xhat[:, j:j + TPG], cen[:, j:j + TPG], bc(rstd[:, j:j + TPG], C), ALU.mult)\
                    .then_inc(S("xhat_ready"), 1)
            dve.wait_ge(s_w, 16 * 8)
            own.do(tt(b_h[:], COL["b_ih"], COL["b_hh"], ALU.add))
            for n in range(NG):
                dve.wait_ge(s_act, 2 * NG + n + 1)
                hi, lo = (xh16[:, :, n * 8:(n + 1) * 8, k] for k in range(2))
                tt(lo, xhT[:, :, n * 8:(n + 1) * 8], hi, ALU.subtract)
            dve.wait_ge(S("ew_split"), 1)
            own.do(dve.memset(XL[NB:P], 0.0))
            for n in range(NG):
                dve.wait_ge(S("xl_ready"), n + 1)
                tt(XL[0:NB, n * 8:(n + 1) * 8, :], bank[n % 2][0:NB, :].rearrange("b (t l) -> b t l", l=NS),
                   battn[:].unsqueeze(1).to_broadcast([NB, 8, NS]), ALU.add).then_inc(S("xl_taken"), 1)
            phase_end(dve, 1)

            def pair(a, ta_, b, tb_, end, begin):
                if b is not None:
                    dve.wait_ge(S(f"exp_ready{b}"), tb_ + 1)
                    own(dve.reciprocal(rsum[b][:], esum[b][:]))
                    stt(spread[b][:], expd[b][:].unsqueeze(1).to_broadcast([BG, 2, NS]), rsum[b][:],
                        parity[:], ALU.mult, ALU.mult).then_inc(S(f"spread_ready{b}"), 1)
                if end:
                    dve.wait_ge(S(f"attended{a}"), ta_)
                    own(dve.tensor_reduce(comb[a][:], psC[a].rearrange("p (b k) -> p b k", k=2), AX_X, ALU.add))
                    tsc(comb[a][:], comb[a][:], COL["b_comb"], 0.0, ALU.add, ALU.max)\
                        .then_inc(S(f"comb_ready{a}"), 1)
                if b is not None:
                    dve.wait_ge(S(f"turned{b}"), tb_ + 1)
                    own(dve.tensor_copy(awb[b][:, :, 0], psT[b]))
                    tt(awb[b][:, :, 1], psT[b], awb[b][:, :, 0], ALU.subtract).then_inc(S(f"placed{b}"), 1)
                if begin:
                    dve.wait_ge(S(f"logits_ready{a}"), ta_ + 1)
                    dve.tensor_reduce(nmax[a][:], psL[a], AX_X, ALU.max, negate=True)\
                        .then_inc(S(f"max_ready{a}"), 1)
                if begin and end:
                    dve.wait_ge(S(f"h_kept{a}"), ta_)
                    tt(h16[a][:, 1], h[a][:], h16[a][:, 0], ALU.subtract).then_inc(S(f"h_split{a}"), 1)
            pair(0, 0, None, None, False, True)
            pair(1, 0, 0, 0, False, True)
            with dve.Fori(1, NS) as t:
                own.loop(t - 1, 6)
                pair(0, t, 1, t - 1, True, True)
                pair(1, t, 0, t, True, True)
                own.end(NS - 1, 6)
            pair(0, NS, 1, NS - 1, True, False)
            pair(1, NS, None, None, True, False)
            dve.wait_ge(S("quotients_summed"), 1)
            tsc(stopped, tc, 0.0, None, ALU.is_equal).then_inc(S("flags_ready"), 1)
            dve.wait_ge(S("flags_summed"), 1)
            own.do(tsc(keep, bank[0][:, 0:NT], 0.0, None, ALU.is_equal))
            phase_end(dve, 2)
            dve_rest(dve, own)

        @block.scalar
        def _(act):
            own = Chain(act, s_act)
            act.preload_act_table(ACT.Sqrt)
            act.wait_ge(s_dve, VAR_AT)
            act.activation(std, var, ACT.Sqrt).then_inc(S("root_ready"), 1)
            for n in range(NG):
                act.wait_ge(S("ew_ready"), n + 1)
                js = slice(n * TPG, (n + 1) * TPG)
                ps = bank[n % 4][:].rearrange("p (j c) -> p j c", j=TPG)
                own.do(act.activation(EWf[:, js], ps, ACT.Copy))
                own.do(act.activation(EWp[0][:, js], ps, ACT.Copy))
            for n in range(NG):
                act.wait_ge(S("xt_ready"), n + 1)
                act.activation(xh16[:, :, n * 8:(n + 1) * 8, 0].rearrange("p t b -> p b t"),
                               bank[4 + n % 4][:].rearrange("p (b t) -> p b t", t=NS), ACT.Copy)
                own.do(act.activation(xhT[:, :, n * 8:(n + 1) * 8].rearrange("p t b -> p b t"),
                                      bank[4 + n % 4][:].rearrange("p (b t) -> p b t", t=NS), ACT.Copy))
            phase_end(act, 1)
            act.preload_act_table(ACT.Exp)

            def pair(a, ta_, b, tb_, end, begin):
                if b is not None:
                    act.wait_ge(S(f"max_ready{b}"), tb_ + 1)
                    act.activation(expd[b][:], psL[b], ACT.Exp, bias=nmax[b][:], accum_out=esum[b][:])\
                        .then_inc(S(f"exp_ready{b}"), 1)
                if end:
                    act.wait_ge(S(f"hidden_ready{a}"), ta_)
                    act.activation(h[a][:], psH[a], ACT.Tanh, bias=b_h[:]).then_inc(S(f"h_ready{a}"), 1)
                    to = HT[:, a * BG:(a + 1) * BG, ds(ta_ - 1, 1)].rearrange("p b a -> p (b a)")
                    act.activation(h16[a][:, 0], psH[a], ACT.Tanh, bias=b_h[:])
                    act.activation(to, psH[a], ACT.Tanh, bias=b_h[:]).then_inc(S(f"h_kept{a}"), 1)
            scan(act, pair)
            phase_end(act, 2)
            act_rest(act, own)

        @block.tensor
        def _(pe):
            mm = pe.matmul
            own = Chain(pe, s_pe)
            pe.wait_ge(s_const, 1)
            pe.wait_ge(s_ctx, 16)
            pe.wait_ge(s_w, 16 * 8)
            for n in range(NG):
                if n >= 4:
                    pe.wait_ge(s_act, 2 * (n - 3))
                for q in range(TPG):
                    j = n * TPG + q
                    last = mm(bank[n % 4][:, q * C:(q + 1) * C], ctxT[:, j * P:(j + 1) * P], W["WcaT"],
                              start=True, stop=True)
                last.then_inc(S("ew_ready"), 1)
            for n in range(NG):
                pe.wait_ge(S("xhat_ready"), n + 1)
                if n >= 4:
                    pe.wait_ge(s_act, 2 * NG + n - 3)
                for q in range(TPG):
                    last = pe.transpose(bank[4 + n % 4][:, q * C:(q + 1) * C], xhat[:, n * TPG + q, :], ident[:])
                last.then_inc(S("xt_ready"), 1)
            pe.wait_ge(s_act, 3 * NG)
            for n in range(NG):
                if n >= 2:
                    pe.wait_ge(S("xl_taken"), n - 1)
                for i in range(8):
                    last = mm(bank[n % 2][0:NB, i * NS:(i + 1) * NS], xhT[:, n * 8 + i, :], wat[:, 0, :],
                              start=True, stop=True)
                last.then_inc(S("xl_ready"), 1)
            phase_end(pe, 1)

            def attention(g, t, pairs):
                if pairs[0] == 0:
                    pe.wait_ge(S(f"placed{g}"), t + 1)
                for p in pairs:
                    for i in range(3):
                        last = mm(psC[g][:, 4 * p:4 * p + 4], EWp[i][:, g * (BG // 2) + p, :],
                                  awb[g][:, 2 * p:2 * p + 2, :].rearrange("p b k -> p (b k)"),
                                  start=False, stop=(i == 2), skip_group_check=True)
                if pairs[-1] == BG // 2 - 1:
                    last.then_inc(S(f"attended{g}"), 1)

            def pair(a, ta_, b, tb_, end, begin):
                if b is not None:
                    wait_apart(pe, S(f"spread_ready{b}"), tb_ + 1)
                    pe.transpose(psT[b], spread[b][:].rearrange("b a l -> b (a l)"),
                                 ident[0:BG, 0:BG]).then_inc(S(f"turned{b}"), 1)
                if end:
                    pe.wait_ge(S(f"comb_ready{a}"), ta_)
                    mm(psH[a], W["WihT"], comb[a][:], start=False, stop=True, skip_group_check=True)\
                        .then_inc(S(f"hidden_ready{a}"), 1)
                if begin:
                    mm(psL[a], ident[:, a * BG:(a + 1) * BG], one(XL, ta_), start=True, stop=False)
                if b is not None:
                    attention(b, tb_, range(0, 5))
                if begin:
                    pe.wait_ge(S(f"h_ready{a}"), ta_ + 1)
                    mm(psL[a], h[a][:], wat[:, 1, :], start=False, stop=True).then_inc(S(f"logits_ready{a}"), 1)
                if b is not None:
                    attention(b, tb_, range(5, BG // 2))
                if begin:
                    if end:
                        pe.wait_ge(S(f"h_split{a}"), ta_)
                        for i in range(3):
                            for k in range(2):
                                mm(psH[a], WP["WhhT"][:, i], h16[a][:, k], start=(i + k == 0), stop=False,
                                   skip_group_check=True)
                    else:
                        mm(psH[a], W["WhhT"], h[a][:], start=True, stop=False, skip_group_check=True)
                    x_t = xh16[:, ds(ta_, 1), a * BG:(a + 1) * BG].rearrange("p t b k -> p (t b k)")
                    for i in range(3):
                        mm(psC[a], WP["WcxT"][:, i], x_t, start=(i == 0), stop=False, skip_group_check=True)
            scan(pe, pair)
            pe.wait_ge(S("flags_ready"), 1)
            mm(bank[0][:, 0:NT], tri[:], stopped, start=True, stop=True).then_inc(S("flags_summed"), 1)
            phase_end(pe, 2)
            pe_rest(pe, own)


def kernel(**inputs):
    import numpy as np
    import concourse.bacc as bacc
    from concourse.bass_utils import run_bass_kernel_spmd as run

    a = {k: np.asarray(v) for k, v in inputs.items()}

    def tiles(t):
        return t.reshape(NT, P, C).transpose(1, 0, 2)

    r = "L0_xcond_"
    s = "L1_xcond_"
    Wa, Wc = a[r + "W_attn"], a[r + "W_comb"]
    squares = {"WcxT": Wc[:, :C].T, "WcaT": Wc[:, C:].T, "WihT": a[r + "W_ih"].T, "WhhT": a[r + "W_hh"].T,
               "WoT": a[r + "W_out"].T, "wk": a[s + "wk"], "wvT": a[s + "wv"].T, "wu": a[s + "wu"],
               "wq": a[s + "wq"], "w1": a[s + "w1"], "w2": a[s + "w2"]}
    columns = {"b_comb": a[r + "b_comb"], "b_ih": a[r + "b_ih"], "b_hh": a[r + "b_hh"], "kv_g": a[s + "lnkv_g"],
               "kv_b": a[s + "lnkv_b"], "q_g": a[s + "lnq_g"], "q_b": a[s + "lnq_b"], "m_g": a[s + "lnm_g"],
               "m_b": a[s + "lnm_b"], "bk": a[s + "bk"], "bq": a[s + "bq"], "bv": a[s + "bv"], "b1": a[s + "b1"]}
    rowsd = {"b_out": a[r + "b_out"], "q_mu": a[s + "q_mu"], "q_logsig": a[s + "q_logsig"], "p_g": a[s + "lnp_g"],
             "p_b": a[s + "lnp_b"], "b2": a[s + "b2"], "bu": a[s + "bu"]}
    wp = a["L0_ffn_w_proj"]
    arrays = {
        "x": tiles(a["x"]),
        "ctxT": a["ctx_1024"].reshape(NB * NS, C).T,
        "ctx_tok": tiles(a["ctx_1024"]),
        "condb": tiles(np.broadcast_to(a["cond_1024"][:, None, :], (NB, NS, C))),
        "wsq": np.stack([squares[n] for n in SQ], 1),
        "wat": np.stack([Wa[:, :C].T, Wa[:, C:].T], 1),
        "cols": np.stack([columns[n].reshape(C) for n in COLS], 1),
        "rows": np.broadcast_to(np.stack([rowsd[n].reshape(C) for n in ROWS], 0)[None], (P, len(ROWS), C)),
        "battn": np.broadcast_to(a[r + "b_attn"][None], (NB, NS)),
        "h0T": a["cond_1024"].T,
        "wr0": a["L0_ffn_w_router"],
        "wr1": a["L1_ffn_router_w"].T,
        "wgf": np.concatenate([a["L0_ffn_w_gate"], a["L0_ffn_w_fc"]], 2).transpose(1, 0, 2),
        "wpj": wp.reshape(E0 // 2, 2 * H0, C).transpose(1, 0, 2),
        "wgu": np.concatenate([a["L1_ffn_w_gate"], a["L1_ffn_w_up"]], 1).transpose(2, 0, 1),
        "wdn": a["L1_ffn_w_down"].reshape(E1, C, FC, P).transpose(3, 0, 2, 1).reshape(P, E1 * FC, C),
    }
    nc = bacc.Bacc("TRN2", target_bir_lowering=False, num_devices=1)
    given, d = {}, {}
    for name, v in arrays.items():
        v = np.ascontiguousarray(v)
        given[f"{name}_dram"] = v
        d[name] = nc.dram_tensor(f"{name}_dram", v.shape, F32, kind="ExternalInput").ap()
    out = nc.dram_tensor("out_dram", (P, NT, C), F32, kind="ExternalOutput").ap()
    program(nc, d, out)
    res = run(nc, [given], core_ids=[0])
    return res.results[0]["out_dram"].transpose(1, 0, 2).reshape(NB, NS, C)
```

```python
from contextlib import ExitStack

import concourse.bass as bass
from concourse import mybir

F32 = mybir.dt.float32
BF16 = mybir.dt.bfloat16
F16 = mybir.dt.float16
U32 = mybir.dt.uint32
F32R = mybir.dt.float32r
ALU = mybir.AluOpType
ACT = mybir.ActivationFunctionType
AX_X = mybir.AxisListType.X

NB, NS, C = 64, 64, 128
P = 128
NT = NB * NS // P
TPG = 4
NG = NT // TPG
BG = NB // 2
E0, H0, CAP = 16, 64, 8
E1, F1 = 8, 256
FC = F1 // P
NSLOT = E0 * CAP
EPS = 1e-5
EPS_ATTN = 1e-8
ITERS = 3
HIGH12 = 0xFFFFF000

SQ = ["WcxT", "WcaT", "WihT", "WhhT", "WoT", "wk", "wvT", "wu", "wqT", "w1", "w2"]
COLS = ["b_comb", "b_ih", "b_hh", "kv_g", "kv_b", "q_g", "q_b", "m_g", "m_b", "bk", "bq", "bv", "b1"]
ROWS = ["b_out", "q_mu", "q_logsig", "p_g", "p_b", "b2", "bu"]


class Chain:

    def __init__(self, eng, sem, wait_apart):
        self.wait_apart = wait_apart
        self.eng, self.sem, self.done, self.n, self.at = eng, sem, 0, 0, 0

    def do(self, ins):
        ins.then_inc(self.sem, 1)
        self.n += 1
        return ins

    def sync(self):
        self.eng.wait_ge(self.sem, self.at + self.n if isinstance(self.at, int) else self.at + self.n)

    def sync_apart(self):
        self.wait_apart(self.eng, self.sem, self.at + self.n)

    def apart(self, ins):
        self.do(ins)
        self.sync_apart()

    def __call__(self, ins):
        self.do(ins)
        self.sync()

    def loop(self, turn, per_turn):
        self.outer = (self.at, self.n)
        base = self.n + (self.at if isinstance(self.at, int) else 0)
        self.at = turn * per_turn + base if isinstance(self.at, int) else self.at + turn * per_turn + self.n
        self.n = 0

    def end(self, turns, per_turn):
        assert self.n == per_turn, (self.n, per_turn)
        self.at, n = self.outer
        self.n = n + turns * per_turn


def program(nc, d, out):
    ctx = ExitStack()
    with ctx:
        def sb(name, shape, dt=F32):
            return ctx.enter_context(nc.sbuf_tensor(name, shape, dt))

        def under(name, shape, dt):
            with nc.sbuf_tensor(name, shape, dt) as t:
                return t

        def sem(name):
            return ctx.enter_context(nc.semaphore(name))

        bank = [ctx.enter_context(nc.psum_tensor(f"bank{i}", [P, 512], F32)) for i in range(8)]

        X = sb("X", [P, NT, C])
        zT2_0 = under("zT_high_", [P, NT * C], F32R)
        R1 = sb("R1", [P, NT * C])
        R23 = sb("R23", [P, 2 * NT * C])
        wgu2_ = under("weights_halves", [P, 2, E1, 2 * F1], F32R)
        R45 = sb("R45", [P, 2 * NT * C])
        zT2_1 = under("zT_low", [P, NT * C], F32R)
        R6 = sb("R6", [P, NT * C])
        R7 = sb("R7", [P, NT * C + NT])
        W1B = sb("W1B", [P, E1 * 2 * F1 + E1 * FC * C])
        cen = R1[:, :].rearrange("p (j c) -> p j c", j=NT)
        xhat = R23[:, 0:NT * C].rearrange("p (j c) -> p j c", j=NT)
        cenh = R23[:, NT * C:].rearrange("p (j c) -> p j c", j=NT)
        xhT = R45[:, 0:NT * C].rearrange("p (t b) -> p t b", t=NS)
        EWf = R6[:, :].rearrange("p (j c) -> p j c", j=NT)
        XL = R45[:, NT * C:].rearrange("p (t l) -> p t l", t=NS)
        EWp = [W1B[:, i * NT * C // 2:(i + 1) * NT * C // 2].bitcast(BF16).rearrange("p (j c) -> p j c", j=NT)
               for i in range(3)]
        HT = R6[:, :].rearrange("p (b t) -> p b t", t=NS)
        ctxT = R7[:, 0:NT * C]
        xh16 = R7[:, 0:NT * C].bitcast(F16).rearrange("p (t b k) -> p t b k", t=NS, k=2)
        sq = R45[:, 0:NT * C].rearrange("p (j c) -> p j c", j=NT)
        BT = R23[:, :].rearrange("p (e b s) -> p e b s", e=E0, b=NB)
        OT = R45[:, :].rearrange("p (e b s) -> p e b s", e=E0, b=NB)
        kqT = R1[:, :]
        V = R7[:, :].rearrange("p (j c) -> p j c", j=NT)
        slots = R23[:, 0:NT * C].rearrange("p (j c) -> p j c", j=NT)
        condb = R23[:, NT * C:].rearrange("p (j c) -> p j c", j=NT)
        ctxk = R6[:, :].rearrange("p (j c) -> p j c", j=NT)
        wgu = W1B[:, 0:E1 * 2 * F1].rearrange("p (e f) -> p e f", e=E1)
        zT2 = [zT2_0[:], zT2_1[:]]
        wgu2 = [wgu2_[:, i] for i in range(2)]
        wdn = W1B[:, E1 * 2 * F1:].rearrange("p (e c) -> p e c", e=E1 * FC)

        wgf = W1B[:, 0:E0 * 2 * H0].rearrange("p (e f) -> p e f", e=E0)
        wpj = W1B[:, E0 * 2 * H0:E0 * 2 * H0 + E0 // 2 * C].rearrange("p (e c) -> p e c", e=E0 // 2)
        wsq = sb("wsq", [P, len(SQ), C])
        wat = sb("wat", [P, 2, NS])
        wr0 = sb("wr0", [P, E0])
        wr1 = sb("wr1", [P, E1])
        cols = sb("cols", [P, len(COLS)])
        rows = sb("rows", [P, len(ROWS), C])
        battn = sb("battn", [NB, NS])
        h0T = sb("h0T", [P, NB])
        W = {n: wsq[:, i, :] for i, n in enumerate(SQ)}
        COL = {n: cols[:, i:i + 1] for i, n in enumerate(COLS)}
        ROW = {n: rows[:, i, :] for i, n in enumerate(ROWS)}

        ident = sb("ident", [P, P])
        tri = sb("tri", [P, P])
        blk = sb("blk", [P, P])
        iota = sb("iota", [P, NSLOT])
        iotaE = sb("iotaE", [P, E0])
        mhalf = sb("mhalf", [P, TPG])
        parity = sb("parity", [BG, 2, NS])
        b_h = sb("b_h", [P, 1])
        wvu = sb("wvu", [P, C])
        bvu = sb("bvu", [P, C])
        bvb = sb("bvb", [P, P])
        qsig = sb("qsig", [P, C])

        a16 = sb("a16", [P, NT, 16])
        a8 = sb("a8", [P, NT, 8])
        a4 = sb("a4", [P, NT, 4])
        a2 = sb("a2", [P, NT, 2])
        acc4 = sb("acc4", [P, NT, 4])
        tok = sb("tok", [P, 20, NT])
        (mean, var, std, rstd, rh, rl, rlo, ta, tb, tc, td, te, tf, stopped, keep, inv, sh, sl) = (
            tok[:, i, :] for i in range(18))
        cl = sb("cl", [P, C])
        er = sb("er", [P, C])
        pr = sb("pr", [P, C])
        pr2 = sb("pr2", [P, C])

        h = [sb(f"h{g}", [P, BG]) for g in range(2)]
        h16 = [sb(f"h16{g}", [P, 2, BG], F16) for g in range(2)]
        WP = {n: sb(n + "_parts", [P, 3, C], BF16) for n in ("WcxT", "WhhT")}
        comb = [sb(f"comb{g}", [P, BG]) for g in range(2)]
        awb = [sb(f"awb{g}", [P, BG, 2], F16) for g in range(2)]
        expd, spread, nmax, esum, rsum = (
            [sb(f"{n}{g}", [BG] + more) for g in range(2)] for n, more in (
                ("expd", [NS]), ("spread", [2, NS]), ("nmax", [1]), ("esum", [1]), ("rsum", [1])))

        ring = [[sb(f"ring{i}{u}", [P, 512]) for u in range(2)] for i in range(5)]
        vst = [sb(f"vst{u}", [P, TPG, C + 1]) for u in range(2)]
        bn6, mv, ve, rs, nm = (
            [[sb(f"{n}{w}{u}", [P, TPG] + more) for u in range(2)] for w in range(2)]
            for n, more in (("bn6", [6]), ("mv", [2]), ("ve", []), ("rs", []), ("nm", [])))
        ta4, tb4, tc4 = ([sb(f"{n}{u}", [P, TPG]) for u in range(2)] for n in ("attn_top", "attn_inv", "upd_inv"))
        mx = [sb(f"mx{u}", [P, TPG]) for u in range(2)]
        sm = [sb(f"sm{u}", [P, TPG]) for u in range(2)]
        rsa = sb("rsa", [P, NT])
        kb = sb("kb", [P, NT])
        nma = sb("nma", [P, NT])

        lg, pb, oh1, oh2, tmpE = (R7[:, i * NT * E0:(i + 1) * NT * E0].rearrange("p (j e) -> p j e", e=E0)
                                  for i in range(5))
        cw = R7[:, 5 * NT * E0:5 * NT * E0 + NT * E1].rearrange("p (j e) -> p j e", e=E1)
        rt = sb("rt", [P, 12, NT])
        (m1, m2, i1, i2, sd1, sd2, sc1, sc2, ra, rb, rc, rd) = (rt[:, i, :] for i in range(12))

        s_x, s_ctx, s_w, s_l0, s_l1, s_cond, s_ctxk, s_out = (
            sem(n) for n in ("x_loaded", "ctx_loaded", "weights_loaded", "l0_loaded", "l1_loaded",
                             "cond_loaded", "ctxk_loaded", "out_stored"))
        s_phase = sem("phase_ended")
        s_dve, s_pool, s_act, s_pe = (sem(n) for n in ("dve_own", "pool_own", "act_own", "pe_own"))
        s_const = sem("consts_ready")
        names = {}

        def S(name):
            if name not in names:
                names[name] = sem(name)
            return names[name]

        def wait_apart(eng, sem, value):
            if not isinstance(value, int):
                value = eng.to_reg(value)
                eng.wait_ge(s_const, 1)
            eng.wait_ge(sem, value)

        def ds(start, size):
            return slice(start, start + size) if isinstance(start, int) else bass.ds(start, size)

        def one(buf, j):
            return buf[:, j, :] if isinstance(j, int) else buf[:, bass.ds(j, 1), :].rearrange("p a c -> p (a c)")

        def bc(ap, n):
            return ap.unsqueeze(2).to_broadcast([ap.shape[0], ap.shape[1], n])

        def phase_end(eng, k):
            eng.drain().then_inc(s_phase, 1)
            eng.wait_ge(s_phase, 4 * k)

        block = ctx.enter_context(nc.Block())
        LAST = 16
        SCALE = C ** 0.5

        def outs(u, i):
            return R1[:, (2 * u + i) * 512:(2 * u + i + 1) * 512]

        def upd_ps(q):
            return bank[6 + q // 2][:, q % 2 * (C + 1):(q % 2 + 1) * (C + 1)]

        def prime(eng, *counts, lead=2):
            for name in counts:
                eng.drain().then_inc(S(name), lead)

        def after(eng, name, k, lead=2):
            wait_apart(eng, S(name), k + 1 + lead)

        def steps(eng, own, stages, marks, peel=2):
            def step(n):
                for fn, lag in stages:
                    if 0 <= n - lag < NG:
                        fn(n - lag, (n - lag) % 2)
            for n in range(peel):
                step(n)
            first = peel // 2
            with eng.Fori(first, NG // 2) as t:
                own.loop(t - first, marks)
                for u in range(2):
                    for fn, lag in stages:
                        fn(t * 2 + (u - lag), (u - lag) % 2)
                own.end(NG // 2 - first, marks)
            for n in range(NG, NG + peel):
                step(n)

        def group(buf, n):
            return buf[:, ds(n * TPG, TPG)]

        def tile4(i, u):
            return ring[i][u][:].rearrange("p (q c) -> p q c", q=TPG)

        def bank4(i):
            return bank[i][:].rearrange("p (q c) -> p q c", q=TPG)

        def beside(row, n=TPG):
            return row.unsqueeze(1).to_broadcast([P, n, row.shape[1]])

        def ln_stats(dve, own, mark, w, k, n, u, src):
            for q in range(TPG):
                own.do(dve.bn_stats(bn6[w][u][:, q], one(src, n * TPG + q)))
            own.sync_apart()
            after(dve, mark + "_rstd", k - 2)
            for q in range(TPG):
                last = dve.bn_aggr(mv[w][u][:, q], bn6[w][u][:, q])
            last.then_inc(S(mark + "_stats"), 1)

        def ln_rstd(pool, own, mark, w, k, n, u):
            after(pool, mark + "_z", k - 2)
            after(pool, mark + "_stats", k)
            own.do(pool.tensor_scalar(nm[w][u][:], mv[w][u][:, :, 0], -1.0, None, ALU.mult))
            own(pool.tensor_scalar(ve[w][u][:], mv[w][u][:, :, 1], EPS, None, ALU.add))
            own(pool.tensor_tensor(rs[w][u][:], ve[w][u][:], mhalf[:], ALU.pow))
            last = pool.tensor_tensor(nm[w][u][:], nm[w][u][:], rs[w][u][:], ALU.mult)
            if mark == "a":
                own(last)
                pool.tensor_copy(group(rsa, n), rs[w][u][:])
                last = pool.tensor_copy(group(nma, n), nm[w][u][:])
            last.then_inc(S(mark + "_rstd"), 1)

        def ln_scale(act, mark, w, k, n, u, src, dst):
            after(act, mark + "_rstd", k)
            after(act, mark + "_turned", k - 2)
            for q in range(TPG):
                j = n * TPG + q
                last = act.activation(dst[:, q * C:(q + 1) * C], one(src, j), ACT.Identity,
                                      bias=nm[w][u][:, q:q + 1], scale=rs[w][u][:, q:q + 1])
            last.then_inc(S(mark + "_z"), 1)

        def ln_turn(pe, mark, k, n, u, src, ps):
            after(pe, mark + "_z", k)
            after(pe, mark + "_zT", k - 2)
            for q in range(TPG):
                last = pe.transpose(ps[:, q * C:(q + 1) * C], src[:, q * C:(q + 1) * C], ident[:])
            last.then_inc(S(mark + "_turned"), 1)

        def pool_rest(pool, own):
            prime(pool, "a_rstd")

            steps(pool, own, [(lambda n, u: ln_rstd(pool, own, "a", 0, n, n, u), 0)], 8)
            phase_end(pool, 3)
            phase_end(pool, 4)
            phase_end(pool, 5)
            phase_end(pool, 6)

            prime(pool, "outs_staged")

            def stage_outs(n, u):
                after(pool, "outs_turned", n - 2)
                pool.tensor_copy(ring[3][u][:].rearrange("p (b e s) -> p e b s", b=4, e=E0),
                                 OT[:, :, ds(n * 8, 4), :]).then_inc(S("outs_staged"), 1)
            steps(pool, own, [(stage_outs, 0)], 0)
            phase_end(pool, 7)

            prime(pool, "kv_rstd", "noise_rstd", "w_low_kept")
            own(pool.memset(V[:, :, C:C + 1], 1.0))
            pool.wait_ge(s_cond, 16)

            def condition(n, u):
                pool.tensor_tensor(group(condb, n), group(condb, n), beside(ROW["b2"]), ALU.add)
            def w_low(n, u):
                after(pool, "w_high", n)
                pool.tensor_tensor(wgu2[1][:, ds(n, 1)].rearrange("p a f -> p (a f)"), W1B[:, ds(n * 512, 512)],
                                   ring[3][u][:], ALU.subtract).then_inc(S("w_low_kept"), 1)
            steps(pool, own, [(w_low, 1), (lambda n, u: ln_rstd(pool, own, "kv", 0, n, n, u), 0),
                              (lambda n, u: ln_rstd(pool, own, "noise", 1, n, n, u), 0), (condition, 0)], 12)
            phase_end(pool, 8)

            prime(pool, "k_staged", "q_rstd", "m_rstd", "p_rstd", "sums_staged")
            for it in range(ITERS):
                def k_of(n, it=it):
                    return n + it * NG

                def stage_k(n, u):
                    after(pool, "attn_logits", k_of(n - 2))
                    pool.tensor_copy(ring[3][u][:], kqT[:, ds(n * 512, 512)]).then_inc(S("k_staged"), 1)
                steps(pool, own, [(stage_k, 1), (lambda n, u: ln_rstd(pool, own, "q", 0, k_of(n), n, u), 0)],
                      6, peel=4)
                phase_end(pool, 9 + 2 * it)

                def stage_sums(n, u):
                    after(pool, "mlp_added", k_of(n - 2))
                    pool.tensor_tensor(tile4(3, u), group(slots, n), group(condb, n), ALU.add)\
                        .then_inc(S("sums_staged"), 1)
                steps(pool, own, [(lambda n, u: ln_rstd(pool, own, "m", 0, k_of(n), n, u), 0), (stage_sums, 1),
                                  (lambda n, u: ln_rstd(pool, own, "p", 1, k_of(n), n, u), 3)], 12, peel=4)
                phase_end(pool, 10 + 2 * it)

            prime(pool, "f_rstd", "zT_kept")

            def low_zT(n, u):
                after(pool, "zT_high", n)
                pool.tensor_tensor(zT2[1][:, ds(n * 512, 512)], ring[2][u][:], ring[1][u][:], ALU.subtract)\
                    .then_inc(S("zT_kept"), 1)
            steps(pool, own, [(lambda n, u: ln_rstd(pool, own, "f", 0, n, n, u), 0), (low_zT, 1)], 6)
            phase_end(pool, 15)
            phase_end(pool, 16)

        def route(dve, own, e, pos):
            tt, tsc, stt = dve.tensor_tensor, dve.tensor_scalar, dve.scalar_tensor_tensor
            L, pr_, h1_, h2_, t_ = (b[:, :, 0:e] for b in (lg, pb, oh1, oh2, tmpE))
            idx = iotaE[:, 0:e].unsqueeze(1).to_broadcast([P, NT, e])
            own(dve.tensor_reduce(ra, L, AX_X, ALU.max))
            tt(pr_, L, bc(ra, e), ALU.subtract).then_inc(S("route_shifted"), 1)
            dve.wait_ge(S("route_exp"), 1 if pos else 2)
            own(dve.tensor_reduce(rb, pr_, AX_X, ALU.add))
            own(dve.reciprocal(rc, rb))
            own(tt(pr_, pr_, bc(rc, e), ALU.mult))
            for m, i, oh, src in ((m1, i1, h1_, pr_), (m2, i2, h2_, t_)):
                own(dve.tensor_reduce(m, src, AX_X, ALU.max))
                own(tt(oh, src, bc(m, e), ALU.is_equal))
                own(tt(oh, oh, idx, ALU.mult))
                own(dve.tensor_reduce(i, oh, AX_X, ALU.min))
                own(tt(oh, idx, bc(i, e), ALU.is_equal))
                if m is m1:
                    own(stt(t_, oh, -4.0, pr_, ALU.mult, ALU.add))

        def dve_rest(dve, own):
            tt, tsc, stt = dve.tensor_tensor, dve.tensor_scalar, dve.scalar_tensor_tensor
            prime(dve, "a_stats", "logits_kept")

            def add_output(n, u):
                for q in range(TPG):
                    j = n * TPG + q
                    own.do(stt(one(X, j), ROW["b_out"], keep[:, ds(j, 1)], one(X, j), ALU.mult, ALU.add))
                own.sync()
                after(dve, "y", n)
                for q in range(TPG):
                    j = n * TPG + q
                    own.do(stt(one(X, j), bank[u][:, q * C:(q + 1) * C], keep[:, ds(j, 1)], one(X, j),
                               ALU.mult, ALU.add))
                own.sync_apart()
                ln_stats(dve, own, "a", 0, n, n, u, X)

            def keep_logits(k, n, u, e):
                after(dve, "router", k)
                dve.tensor_copy(group(lg, n)[:, :, 0:e], bank[4 + u][:, 0:TPG * e].rearrange("p (q e) -> p q e", e=e))\
                    .then_inc(S("logits_kept"), 1)
            steps(dve, own, [(add_output, 0), (lambda n, u: keep_logits(n, n, u, E0), 2)], 24)
            phase_end(dve, 3)

            route(dve, own, E0, True)
            dve.nop().then_inc(S("picked"), 1)
            for k, (oh, i, sd, sc) in enumerate(((oh1, i1, sd1, sc1), (oh2, i2, sd2, sc2))):
                ps = bank[k][:].rearrange("p (j e) -> p j e", e=E0)
                dve.wait_ge(S("counted"), k + 1)
                own(tt(tmpE, ps, oh, ALU.mult))
                own(dve.tensor_reduce(ra, tmpE, AX_X, ALU.add))
                own(tsc(ra, ra, -1.0, None, ALU.add))
                own.do(tsc(rb, ra, float(CAP), None, ALU.is_lt))
                own(tsc(rc, ra, float(CAP - 1), None, ALU.min))
                own(stt(sc, i, float(CAP), rc, ALU.mult, ALU.add))
                own(tsc(sc, sc, 100.0 * CAP, None, ALU.add))
                own(stt(sd, sc, 1.0, rb, ALU.add, ALU.mult))
                own(tsc(sd, sd, -1.0, None, ALU.add))
            phase_end(dve, 4)

            prime(dve, "places", "placed_hi")

            def places(n, u):
                after(dve, "dispatched", n - 2)
                for q in range(TPG):
                    j = n * TPG + q
                    own.do(tsc(ring[2][u][:, q * C:(q + 1) * C], iota[:], sd1[:, ds(j, 1)], None, ALU.is_equal))
                own.sync()
                for q in range(TPG):
                    j = n * TPG + q
                    cs = slice(q * C, (q + 1) * C)
                    last = stt(ring[1][u][:, cs], iota[:], sd2[:, ds(j, 1)], ring[2][u][:, cs], ALU.is_equal, ALU.add)
                last.then_inc(S("places"), 1)

            def keep_hi(n, u):
                after(dve, "dispatched", n)
                dve.tensor_copy(BT[:, :, ds(n * 8 + 4, 4), :],
                                bank[2 * u + 1][:].rearrange("p (b e s) -> p e b s", b=4, e=E0))\
                    .then_inc(S("placed_hi"), 1)
            steps(dve, own, [(places, 0), (keep_hi, 1)], 8)
            phase_end(dve, 5)

            for p in range(E0 // 2):
                u = p % 2
                dve.wait_ge(S("fc"), p + 1)
                dve.wait_ge(S("silu"), p + 1)
                if p >= 2:
                    dve.wait_ge(S("down"), 2 * (p - 1))
                tt(ring[1][u][:], ring[0][u][:], bank[2 + u][:], ALU.mult).then_inc(S("gated"), 1)
                dve.wait_ge(S("down"), 2 * p + 1)
                dve.tensor_copy(OT[:, 2 * p], bank[4 + 2 * u][:].rearrange("p (b s) -> p b s", s=CAP))\
                    .then_inc(S("out_even"), 1)
            phase_end(dve, 6)

            prime(dve, "weights", "x_added")

            def weights(n, u):
                after(dve, "weights_turned", n - 2)
                for q in range(TPG):
                    j = n * TPG + q
                    cs = slice(q * C, (q + 1) * C)
                    own.do(tsc(ring[0][u][:, cs], iota[:], sc1[:, ds(j, 1)], m1[:, ds(j, 1)], ALU.is_equal, ALU.mult))
                    own.do(tsc(ring[1][u][:, cs], iota[:], sc2[:, ds(j, 1)], m2[:, ds(j, 1)], ALU.is_equal, ALU.mult))
                own.sync()
                tt(ring[0][u][:], ring[0][u][:], ring[1][u][:], ALU.add).then_inc(S("weights"), 1)

            def add_collected(n, u):
                after(dve, "collected", n)
                tt(group(X, n), group(X, n), bank4(6 + u), ALU.add).then_inc(S("x_added"), 1)
            steps(dve, own, [(weights, 0), (add_collected, 2)], 16)
            phase_end(dve, 7)

            prime(dve, "kv_stats", "v_kept", "kb_kept", "noise_stats", "noise_turned", "w_high")
            for i, (sem_, dst, bk) in enumerate((("wvu", wvu[:], bank[6][:, 0:C]), ("bvu", bvu[:], bank[7][:, 0:C]))):
                dve.wait_ge(S("folded"), i + 1)
                if i == 0:
                    dve.tensor_copy(dst, bk).then_inc(S("folded_kept"), 1)
                else:
                    tt(dst, bk, ROW["bu"], ALU.add).then_inc(S("folded_kept"), 1)
            dve.wait_ge(s_ctxk, 16)

            def keep_v(n, u):
                after(dve, "v", n)
                tt(group(V, n)[:, :, 0:C], bank4(4 + u), beside(bvu[:]), ALU.add).then_inc(S("v_kept"), 1)

            def keep_kb(n, u):
                after(dve, "kb", n)
                tsc(group(kb, n), bank[2 + u][:, 0:TPG], SCALE, None, ALU.mult).then_inc(S("kb_kept"), 1)

            def begin_slots(n, u):
                after(dve, "noise_z", n)
                own(tt(tile4(2, u), tile4(2, u), beside(qsig[:]), ALU.mult))
                tt(group(slots, n), tile4(2, u), beside(ROW["q_mu"]), ALU.add).then_inc(S("noise_turned"), 1)
            dve.wait_ge(s_l1, 32)

            def split_weights(n, u):
                after(dve, "w_high_kept", n - 2)
                after(dve, "w_low_kept", n - 2)
                tsc(ring[3][u][:].bitcast(U32), W1B[:, ds(n * 512, 512)].bitcast(U32), HIGH12, None, ALU.bitwise_and)\
                    .then_inc(S("w_high"), 1)
            steps(dve, own, [(lambda n, u: ln_stats(dve, own, "kv", 0, n, n, u, ctxk), 0),
                             (lambda n, u: ln_stats(dve, own, "noise", 1, n, n, u, X), 0),
                             (split_weights, 0), (keep_v, 2), (keep_kb, 2), (begin_slots, 1)], 18)
            phase_end(dve, 8)

            prime(dve, "q_stats", "attn_max", "attn", "updated_kept", "m_stats", "mlp_added", "p_stats", "p_turned")
            for it in range(ITERS):
                def k_of(n, it=it):
                    return n + it * NG

                def attn_max(n, u):
                    after(dve, "attn_logits", k_of(n))
                    own(dve.tensor_reduce(ta4[u][:], bank[4 + u][:, 0:TPG * NS].rearrange("p (q s) -> p q s", s=NS),
                                          AX_X, ALU.max))
                    own(stt(ta4[u][:], ta4[u][:], SCALE, group(kb, n), ALU.mult, ALU.add))
                    tt(mx[u][:], group(kb, n), ta4[u][:], ALU.subtract).then_inc(S("attn_max"), 1)

                def attn(n, u):
                    after(dve, "attn_exp", k_of(n))
                    own(dve.reciprocal(tb4[u][:], sm[u][:]))
                    for q in range(TPG):
                        cs = slice(q * NS, (q + 1) * NS)
                        last = tsc(ring[4][u][:, cs], ring[4][u][:, cs], tb4[u][:, q:q + 1], EPS_ATTN,
                                   ALU.mult, ALU.add)
                    last.then_inc(S("attn"), 1)

                def update(n, u):
                    after(dve, "updated", k_of(n))
                    for q in range(TPG):
                        own.do(dve.reciprocal(tc4[u][:, q:q + 1], upd_ps(q)[:, C:C + 1]))
                    own.sync()
                    for q in range(TPG):
                        s_ = one(slots, n * TPG + q)
                        last = own.do(stt(s_, upd_ps(q)[:, 0:C], tc4[u][:, q:q + 1], s_, ALU.mult, ALU.add))
                    own.sync()
                    dve.nop().then_inc(S("updated_kept"), 1)
                steps(dve, own, [(attn, 3), (update, 4), (attn_max, 2),
                                 (lambda n, u: ln_stats(dve, own, "q", 0, k_of(n), n, u, slots), 0)], 30, peel=4)
                phase_end(dve, 9 + 2 * it)

                def add_mlp(n, u):
                    after(dve, "mlp", k_of(n))
                    after(dve, "sums_staged", k_of(n))
                    tt(group(slots, n), bank4(4 + u), tile4(3, u), ALU.add).then_inc(S("mlp_added"), 1)
                    after(dve, "mlp_added", k_of(n))
                    ln_stats(dve, own, "p", 1, k_of(n), n, u, slots)

                def affine(n, u):
                    after(dve, "p_z", k_of(n))
                    own(tt(tile4(4, u), tile4(4, u), beside(ROW["p_g"]), ALU.mult))
                    tt(group(slots, n), tile4(4, u), beside(ROW["p_b"]), ALU.add).then_inc(S("p_turned"), 1)
                steps(dve, own, [(lambda n, u: ln_stats(dve, own, "m", 0, k_of(n), n, u, slots), 0),
                                 (add_mlp, 3), (affine, 4)], 18, peel=4)
                phase_end(dve, 10 + 2 * it)

            prime(dve, "f_stats", "zT_high")

            def add_slots(n, u):
                own.do(tt(group(X, n), group(X, n), group(slots, n), ALU.add))
                own.sync_apart()
                ln_stats(dve, own, "f", 0, n, n, u, X)

            def high_zT(n, u):
                after(dve, "f_zT", n)
                after(dve, "zT_kept", n - 2)
                after(dve, "zT_high_kept", n - 2)
                tsc(ring[1][u][:].bitcast(U32), ring[2][u][:].bitcast(U32), HIGH12, None, ALU.bitwise_and)\
                    .then_inc(S("zT_high"), 1)
            steps(dve, own, [(add_slots, 0), (high_zT, 1), (lambda n, u: keep_logits(n + NG, n, u, E1), 2)], 10)
            dve.wait_ge(S("logits_kept"), 2 + 2 * NG)
            route(dve, own, E1, False)
            own(tt(ra, m1, m2, ALU.add))
            own(dve.reciprocal(rb, ra))
            own.do(tt(m1, m1, rb, ALU.mult))
            own(tt(m2, m2, rb, ALU.mult))
            own.do(tt(oh1[:, :, 0:E1], oh1[:, :, 0:E1], bc(m1, E1), ALU.mult))
            own(tt(oh2[:, :, 0:E1], oh2[:, :, 0:E1], bc(m2, E1), ALU.mult))
            own(tt(cw, oh1[:, :, 0:E1], oh2[:, :, 0:E1], ALU.add))
            phase_end(dve, 15)

            prime(dve, "y_added")
            prime(dve, "prod", lead=2 * FC)
            units = E1 * FC

            def add_expert(n, e):
                after(dve, "ffn_y", n * E1 + e)
                own.sync()
                for q in range(TPG):
                    j = n * TPG + q
                    own.do(stt(one(X, j), bank[6 + e % 2][:, q * C:(q + 1) * C], one(cw, j)[:, e:e + 1], one(X, j),
                               ALU.mult, ALU.add))
                own.sync()
                dve.nop().then_inc(S("y_added"), 1)
            with dve.Fori(0, NG) as n:
                own.loop(n, E1 * TPG)
                for e in range(E1):
                    for f in range(FC):
                        k = e * FC + f
                        after(dve, "ffn_up", n * units + k)
                        after(dve, "ffn_silu", n * units + k)
                        after(dve, "ffn_y", n * E1 + (e - 2))
                        tt(ring[2 + f][e % 2][:], ring[f][e % 2][:], bank[2 + f][:], ALU.mult).then_inc(S("prod"), 1)
                    if e > 0:
                        add_expert(n, e - 1)
                add_expert(n, E1 - 1)
                own.end(NG, E1 * TPG)
            phase_end(dve, 16)

        def act_rest(act, own):
            prime(act, "a_z", "a_zT", "hidden_staged")

            def stage_hidden(n, u):
                after(act, "y", n - 2)
                act.activation(ring[0][u][:].rearrange("p (b t) -> p b t", t=NS), HT[:, ds(n * 8, 8), :], ACT.Copy)\
                    .then_inc(S("hidden_staged"), 1)

            def keep_zT(mark, k, n, u, src, dst, g=None, b=None, free=None):
                after(act, mark + "_turned", k)
                after(act, free, k - 2)
                if g is None:
                    act.activation(dst, src, ACT.Copy).then_inc(S(mark + "_zT"), 1)
                else:
                    act.activation(dst, src, ACT.Identity, bias=b, scale=g).then_inc(S(mark + "_zT"), 1)
            steps(act, own, [(stage_hidden, 0),
                             (lambda n, u: keep_zT("a", n, n, u, bank[2 + u][:], ring[2][u][:], free="router"), 2),
                             (lambda n, u: ln_scale(act, "a", 0, n, n, u, X, ring[1][u]), 1)], 0)
            phase_end(act, 3)
            act.wait_ge(S("route_shifted"), 1)
            act.activation(pb, pb, ACT.Exp).then_inc(S("route_exp"), 1)
            phase_end(act, 4)

            prime(act, "rows_scaled", "placed_lo")

            def scale_rows(n, u):
                after(act, "dispatched", n - 2)
                for q in range(TPG):
                    j = n * TPG + q
                    last = act.activation(ring[0][u][:, q * C:(q + 1) * C], one(X, j), ACT.Identity,
                                          bias=nma[:, ds(j, 1)], scale=rsa[:, ds(j, 1)])
                last.then_inc(S("rows_scaled"), 1)

            def keep_lo(n, u):
                after(act, "dispatched", n)
                act.activation(BT[:, :, ds(n * 8, 4), :], bank[2 * u][:].rearrange("p (b e s) -> p e b s", b=4, e=E0),
                               ACT.Copy).then_inc(S("placed_lo"), 1)
            steps(act, own, [(scale_rows, 0), (keep_lo, 1)], 0)
            act.preload_act_table(ACT.Silu)
            phase_end(act, 5)

            for p in range(E0 // 2):
                u = p % 2
                act.wait_ge(S("gate"), p + 1)
                if p >= 2:
                    act.wait_ge(S("gated"), p - 1)
                act.activation(ring[0][u][:], bank[u][:], ACT.Silu).then_inc(S("silu"), 1)
                act.wait_ge(S("down"), 2 * p + 2)
                act.activation(OT[:, 2 * p + 1], bank[5 + 2 * u][:].rearrange("p (b s) -> p b s", s=CAP), ACT.Copy)\
                    .then_inc(S("out_odd"), 1)
            phase_end(act, 6)

            prime(act, "weights_T", "outs_lo", "outs_hi", "outs_staged_hi")

            def weights_T(n, u):
                after(act, "weights_turned", n)
                after(act, "collected", n - 2)
                act.activation(ring[2][u][:], bank[u][:], ACT.Copy).then_inc(S("weights_T"), 1)

            def outs_kept(n, u):
                after(act, "outs_turned", n)
                act.activation(outs(u, 0), bank[2 + u][:], ACT.Copy).then_inc(S("outs_lo"), 1)
                act.activation(outs(u, 1), bank[4 + u][:], ACT.Copy).then_inc(S("outs_hi"), 1)

            def stage_hi(n, u):
                after(act, "outs_turned", n - 2)
                act.activation(ring[4][u][:].rearrange("p (b e s) -> p e b s", b=4, e=E0),
                               OT[:, :, ds(n * 8 + 4, 4), :], ACT.Copy).then_inc(S("outs_staged_hi"), 1)
            steps(act, own, [(stage_hi, 0), (weights_T, 1), (outs_kept, 1)], 0)
            act.preload_act_table(ACT.Exp)
            act.activation(qsig[:], ROW["q_logsig"], ACT.Exp)
            act.activation(bvb[:], COL["bv"].to_broadcast([P, P]), ACT.Copy)
            phase_end(act, 7)

            prime(act, "kv_z", "kv_zT", "k_kept", "kq_kept", "noise_z", "w_high_kept")

            def keep_k(n, u):
                after(act, "k", n)
                after(act, "kq", n - 2)
                act.activation(ring[4][u][:], bank[2 + u][:], ACT.Identity, bias=COL["bk"]).then_inc(S("k_kept"), 1)

            def keep_kq(n, u):
                after(act, "kq", n)
                act.activation(kqT[:, ds(n * 512, 512)], bank[6 + u][:], ACT.Copy).then_inc(S("kq_kept"), 1)
            def keep_w_high(n, u):
                after(act, "w_high", n)
                act.activation(wgu2[0][:, ds(n, 1)].rearrange("p a f -> p (a f)"), ring[3][u][:], ACT.Copy)\
                    .then_inc(S("w_high_kept"), 1)
            steps(act, own, [(keep_kq, 3), (keep_k, 2), (keep_w_high, 1),
                             (lambda n, u: keep_zT("kv", n, n, u, bank[u][:], ring[1][u][:], COL["kv_g"], COL["kv_b"],
                                                   free="v"), 1),
                             (lambda n, u: ln_scale(act, "kv", 0, n, n, u, ctxk, ring[0][u]), 0),
                             (lambda n, u: ln_scale(act, "noise", 1, n, n, u, X, ring[2][u]), 0)], 0, peel=4)
            phase_end(act, 8)

            prime(act, "v_staged", "q_z", "q_zT", "attn_exp", "m_z", "m_zT", "gelu", "p_z")
            for it in range(ITERS):
                def k_of(n, it=it):
                    return n + it * NG

                def attn_exp(n, u):
                    after(act, "attn_max", k_of(n))
                    after(act, "updated", k_of(n - 2))
                    for q in range(TPG):
                        cs = slice(q * NS, (q + 1) * NS)
                        last = act.activation(ring[4][u][:, cs], bank[4 + u][:, cs], ACT.Exp, bias=mx[u][:, q:q + 1],
                                              scale=SCALE, accum_out=sm[u][:, q:q + 1])
                    last.then_inc(S("attn_exp"), 1)
                def stage_v(n, u):
                    after(act, "updated", k_of(n - 2))
                    act.activation(vst[u][:], group(V, n), ACT.Copy).then_inc(S("v_staged"), 1)
                steps(act, own, [(attn_exp, 3),
                                 (lambda n, u: keep_zT("q", k_of(n), n, u, bank[u][:], ring[1][u][:], COL["q_g"],
                                                       COL["q_b"], free="attn_logits"), 2),
                                 (stage_v, 2),
                                 (lambda n, u: ln_scale(act, "q", 0, k_of(n), n, u, slots, ring[0][u]), 1)],
                      0, peel=4)
                act.preload_act_table(ACT.Gelu)
                phase_end(act, 9 + 2 * it)

                def gelu(n, u):
                    after(act, "mlp_hidden", k_of(n))
                    after(act, "mlp", k_of(n - 2))
                    act.activation(ring[2][u][:], bank[2 + u][:], ACT.Gelu, bias=COL["b1"]).then_inc(S("gelu"), 1)
                steps(act, own, [(gelu, 2),
                                 (lambda n, u: keep_zT("m", k_of(n), n, u, bank[u][:], ring[1][u][:], COL["m_g"],
                                                       COL["m_b"], free="mlp_hidden"), 1),
                                 (lambda n, u: ln_scale(act, "m", 0, k_of(n), n, u, slots, ring[0][u]), 0),
                                 (lambda n, u: ln_scale(act, "p", 1, k_of(n), n, u, slots, ring[4][u]), 3)], 0, peel=4)
                act.preload_act_table(ACT.Exp)
                phase_end(act, 10 + 2 * it)

            prime(act, "f_z", "f_zT", "zT_high_kept")

            def keep_zT_high(n, u):
                after(act, "zT_high", n)
                act.activation(zT2[0][:, ds(n * 512, 512)], ring[1][u][:], ACT.Copy).then_inc(S("zT_high_kept"), 1)

            def keep_zT_f(n, u):
                after(act, "zT_kept", n - 2)
                keep_zT("f", n, n, u, bank[u][:], ring[2][u][:], free="f_router")
            steps(act, own, [(keep_zT_high, 2), (keep_zT_f, 1),
                             (lambda n, u: ln_scale(act, "f", 0, n, n, u, X, ring[0][u]), 0)], 0)
            act.wait_ge(S("route_shifted"), 2)
            act.activation(pb[:, :, 0:E1], pb[:, :, 0:E1], ACT.Exp).then_inc(S("route_exp"), 1)
            act.preload_act_table(ACT.Silu)
            phase_end(act, 15)

            prime(act, "ffn_silu")
            units = E1 * FC
            with act.Fori(0, NG) as n:
                for e in range(E1):
                    for f in range(FC):
                        k = n * units + e * FC + f
                        after(act, "ffn_gate", k)
                        after(act, "prod", k - 2 * FC, 2 * FC)
                        act.activation(ring[f][e % 2][:], bank[f][:], ACT.Silu).then_inc(S("ffn_silu"), 1)
            phase_end(act, 16)

        def pe_rest(pe, own):
            mm = pe.matmul
            prime(pe, "y", "a_turned", "router")

            def hidden_out(n, u):
                after(pe, "hidden_staged", n)
                after(pe, "a_stats", n - 2)
                for q in range(TPG):
                    last = mm(bank[u][:, q * C:(q + 1) * C], ring[0][u][:, q * C:(q + 1) * C], W["WoT"],
                              start=True, stop=True)
                last.then_inc(S("y"), 1)

            def router(mark, k, n, u, w, e, zT):
                after(pe, mark + "_zT", n)
                after(pe, "logits_kept", k - 2)
                for q in range(TPG):
                    last = mm(bank[4 + u][:, q * e:(q + 1) * e], zT[:, q * C:(q + 1) * C], w[:], start=True, stop=True)
                last.then_inc(S("router"), 1)
            steps(pe, own, [(hidden_out, 0), (lambda n, u: router("a", n, n, u, wr0, E0, ring[2][u]), 2),
                            (lambda n, u: ln_turn(pe, "a", n, n, u, ring[1][u], bank[2 + u]), 1)], 0)
            phase_end(pe, 3)

            pe.wait_ge(S("picked"), 1)
            rows1, rows2 = (b.rearrange("p j e -> p (j e)") for b in (oh1, oh2))
            mm(bank[0][:], tri[:], rows1, start=True, stop=True).then_inc(S("counted"), 1)
            mm(bank[1][:], tri[:], rows2, start=True, stop=False)
            mm(bank[1][:], blk[:], rows1, start=False, stop=True).then_inc(S("counted"), 1)
            phase_end(pe, 4)

            prime(pe, "dispatched")

            def dispatch(n, u):
                after(pe, "rows_scaled", n)
                after(pe, "places", n)
                after(pe, "placed_lo", n - 2)
                after(pe, "placed_hi", n - 2)
                for q in range(TPG):
                    for b in range(2):
                        r = slice(b * NS, (b + 1) * NS)
                        last = mm(bank[2 * u + b][:, q * C:(q + 1) * C], ring[0][u][r, q * C:(q + 1) * C],
                                  ring[1][u][r, q * C:(q + 1) * C], start=True, stop=True)
                last.then_inc(S("dispatched"), 1)
            steps(pe, own, [(dispatch, 0)], 0)
            phase_end(pe, 5)

            pe.wait_ge(s_l0, 32)

            def down(p):
                u = p % 2
                pe.wait_ge(S("gated"), p + 1)
                for i, kept in ((0, "out_even"), (1, "out_odd")):
                    if p >= 2:
                        pe.wait_ge(S(kept), p - 1)
                    r = slice(i * H0, (i + 1) * H0)
                    mm(bank[4 + 2 * u + i][:], wpj[r, p, :], ring[1][u][r, :], start=True, stop=True)\
                        .then_inc(S("down"), 1)
            for p in range(E0 // 2):
                u = p % 2
                for bk, cs, name, free in ((u, slice(0, H0), "gate", "silu"),
                                           (2 + u, slice(H0, 2 * H0), "fc", "gated")):
                    if p >= 2:
                        pe.wait_ge(S(free), p - 1)
                    for i in range(2):
                        last = mm(bank[bk][i * H0:(i + 1) * H0, :], wgf[:, 2 * p + i, cs],
                                  BT[:, 2 * p + i].rearrange("p b s -> p (b s)"), start=True, stop=True)
                    last.then_inc(S(name), 1)
                if p:
                    down(p - 1)
            down(E0 // 2 - 1)
            phase_end(pe, 6)

            prime(pe, "weights_turned", "outs_turned", "collected")

            def turn_collect(n, u):
                after(pe, "weights", n)
                after(pe, "weights_T", n - 2)
                for q in range(TPG):
                    last = pe.transpose(bank[u][:, q * C:(q + 1) * C], ring[0][u][:, q * C:(q + 1) * C], ident[:])
                last.then_inc(S("weights_turned"), 1)
                after(pe, "outs_staged", n)
                after(pe, "outs_staged_hi", n)
                after(pe, "outs_lo", n - 2)
                after(pe, "outs_hi", n - 2)
                for i in range(2):
                    for q in range(TPG):
                        last = pe.transpose(bank[2 + 2 * i + u][:, q * C:(q + 1) * C],
                                            ring[3 + i][u][:, q * C:(q + 1) * C], ident[:])
                last.then_inc(S("outs_turned"), 1)

            def collect(n, u):
                after(pe, "weights_T", n)
                after(pe, "outs_lo", n)
                after(pe, "outs_hi", n)
                after(pe, "x_added", n - 2)
                for b in range(2 * TPG):
                    q, r = b // 2, b % 2
                    last = mm(bank[6 + u][r * NS:(r + 1) * NS, q * C:(q + 1) * C], ring[2][u][:, b * NS:(b + 1) * NS],
                              outs(u, r)[:, q * C:(q + 1) * C], start=True, stop=True)
                last.then_inc(S("collected"), 1)
            steps(pe, own, [(turn_collect, 0), (collect, 1)], 0)
            phase_end(pe, 7)

            mm(bank[6][:, 0:C], W["wvT"], W["wu"], start=True, stop=True).then_inc(S("folded"), 1)
            mm(bank[7][:, 0:C], bvb[:], W["wu"], start=True, stop=True).then_inc(S("folded"), 1)
            pe.wait_ge(S("folded_kept"), 2)
            prime(pe, "kv_turned", "k", "v", "kb", "kq")

            def keys_values(n, u):
                after(pe, "kv_zT", n)
                after(pe, "kb_kept", n - 2)
                mm(bank[2 + u][:], W["wk"], ring[1][u][:], start=True, stop=True).then_inc(S("k"), 1)
                after(pe, "v_kept", n - 2)
                for q in range(TPG):
                    last = mm(bank[4 + u][:, q * C:(q + 1) * C], ring[1][u][:, q * C:(q + 1) * C], wvu[:],
                              start=True, stop=True)
                last.then_inc(S("v"), 1)
            def keys_of_queries(n, u):
                after(pe, "k_kept", n)
                after(pe, "kq_kept", n - 2)
                for q in range(TPG):
                    last = mm(bank[2 + u][:, q:q + 1], ring[4][u][:, q * C:(q + 1) * C], COL["bq"],
                              start=True, stop=True)
                last.then_inc(S("kb"), 1)
                mm(bank[6 + u][:], W["wqT"], ring[4][u][:], start=True, stop=True).then_inc(S("kq"), 1)
            steps(pe, own, [(keys_of_queries, 2), (keys_values, 1),
                            (lambda n, u: ln_turn(pe, "kv", n, n, u, ring[0][u], bank[u]), 0)], 0)
            phase_end(pe, 8)

            prime(pe, "q_turned", "attn_logits", "updated", "m_turned", "mlp_hidden", "mlp")
            for it in range(ITERS):
                def k_of(n, it=it):
                    return n + it * NG

                def attn_logits(n, u):
                    after(pe, "q_zT", k_of(n))
                    after(pe, "k_staged", k_of(n))
                    after(pe, "attn_exp", k_of(n - 2))
                    for b in range(2 * TPG):
                        q, r = b // 2, b % 2
                        cs = slice(b * NS, (b + 1) * NS)
                        last = mm(bank[4 + u][r * NS:(r + 1) * NS, q * NS:(q + 1) * NS], ring[3][u][:, cs],
                                  ring[1][u][:, cs], start=True, stop=True)
                    last.then_inc(S("attn_logits"), 1)

                def updates(n, u):
                    after(pe, "attn", k_of(n))
                    after(pe, "v_staged", k_of(n))
                    after(pe, "updated_kept", k_of(n - 1))
                    for b in range(2 * TPG):
                        q, r = b // 2, b % 2
                        rs_ = slice(r * NS, (r + 1) * NS)
                        last = mm(upd_ps(q)[rs_, :], ring[4][u][rs_, q * NS:(q + 1) * NS], vst[u][rs_, q, :],
                                  start=True, stop=True)
                    last.then_inc(S("updated"), 1)
                steps(pe, own, [(attn_logits, 2), (updates, 3),
                                (lambda n, u: ln_turn(pe, "q", k_of(n), n, u, ring[0][u], bank[u]), 1)],
                      0, peel=4)
                phase_end(pe, 9 + 2 * it)

                def mlp_hidden(n, u):
                    after(pe, "m_zT", k_of(n))
                    after(pe, "gelu", k_of(n - 2))
                    mm(bank[2 + u][:], W["w1"], ring[1][u][:], start=True, stop=True).then_inc(S("mlp_hidden"), 1)

                def mlp(n, u):
                    after(pe, "gelu", k_of(n))
                    after(pe, "mlp_added", k_of(n - 2))
                    for q in range(TPG):
                        last = mm(bank[4 + u][:, q * C:(q + 1) * C], ring[2][u][:, q * C:(q + 1) * C], W["w2"],
                                  start=True, stop=True)
                    last.then_inc(S("mlp"), 1)
                steps(pe, own, [(mlp, 2), (mlp_hidden, 1),
                                (lambda n, u: ln_turn(pe, "m", k_of(n), n, u, ring[0][u], bank[u]), 0)], 0, peel=4)
                phase_end(pe, 10 + 2 * it)

            prime(pe, "f_turned", "f_router")

            def router_f(n, u):
                router("f", n + NG, n, u, wr1, E1, ring[2][u])
                pe.nop().then_inc(S("f_router"), 1)
            steps(pe, own, [(router_f, 1), (lambda n, u: ln_turn(pe, "f", n, n, u, ring[0][u], bank[u]), 0)], 0)
            phase_end(pe, 15)

            pe.wait_ge(s_l1, 32)
            prime(pe, "ffn_gate", "ffn_up", "ffn_y")
            units = E1 * FC

            def down(n, e):
                after(pe, "prod", n * units + (e * FC + FC - 1), 2 * FC)
                after(pe, "y_added", n * E1 + (e - 2))
                for q in range(TPG):
                    for f in range(FC):
                        last = mm(bank[6 + e % 2][:, q * C:(q + 1) * C], ring[2 + f][e % 2][:, q * C:(q + 1) * C],
                                  wdn[:, e * FC + f, :], start=(f == 0), stop=(f == FC - 1))
                last.then_inc(S("ffn_y"), 1)

            def product(ps, e, at, n, name):
                for i, (w_, z_) in enumerate(((0, 0), (1, 0), (0, 1))):
                    last = mm(ps, wgu2[w_][:, e, at:at + P], zT2[z_][:, ds(n * 512, 512)],
                              start=(i == 0), stop=(i == 2))
                last.then_inc(S(name), 1)
            with pe.Fori(0, NG) as n:
                for e in range(E1):
                    for f in range(FC):
                        k = n * units + e * FC + f
                        after(pe, "ffn_silu", k - FC)
                        product(bank[f][:], e, f * P, n, "ffn_gate")
                        after(pe, "prod", k - FC, 2 * FC)
                        product(bank[2 + f][:], e, F1 + f * P, n, "ffn_up")
                    if e > 0:
                        down(n, e - 1)
                down(n, E1 - 1)
            phase_end(pe, 16)

        @block.sync
        def _(sp):
            sp.dma_start(X[:], d["x"]).then_inc(s_x, 16)
            sp.dma_start(ctxT, d["ctxT"]).then_inc(s_ctx, 16)
            for buf, name in ((wsq, "wsq"), (wat, "wat"), (cols, "cols"), (rows, "rows"), (battn, "battn"),
                              (h0T, "h0T"), (wr0, "wr0"), (wr1, "wr1")):
                sp.dma_start(buf[:], d[name]).then_inc(s_w, 16)
            sp.wait_ge(s_phase, 4 * 2)
            sp.dma_start(wgf, d["wgf"]).then_inc(s_l0, 16)
            sp.dma_start(wpj, d["wpj"]).then_inc(s_l0, 16)
            sp.wait_ge(s_phase, 4 * 3)
            sp.dma_start(ctxk, d["ctx_tok"]).then_inc(s_ctxk, 16)
            sp.wait_ge(s_phase, 4 * 6)
            sp.dma_start(condb, d["condb"]).then_inc(s_cond, 16)
            sp.wait_ge(s_l0, 32)
            sp.dma_start(wgu, d["wgu"]).then_inc(s_l1, 16)
            sp.dma_start(wdn, d["wdn"]).then_inc(s_l1, 16)
            sp.wait_ge(s_phase, 4 * LAST)
            sp.dma_start(out, X[:]).then_inc(s_out, 16)
            sp.wait_ge(s_out, 16)

        psL = [bank[g][0:BG, 0:NS] for g in range(2)]
        psT = [bank[2 + g][:, 0:BG] for g in range(2)]
        psC = [bank[4 + g][:, 0:2 * BG] for g in range(2)]
        psH = [bank[6 + g][:, 0:BG] for g in range(2)]

        def scan(eng, pair):
            pair(0, 0, None, None, False, True)
            pair(1, 0, 0, 0, False, True)
            with eng.Fori(1, NS) as t:
                pair(0, t, 1, t - 1, True, True)
                pair(1, t, 0, t, True, True)
            pair(0, NS, 1, NS - 1, True, False)
            pair(1, NS, None, None, True, False)

        @block.gpsimd
        def _(pool):
            own = Chain(pool, s_pool, wait_apart)
            for buf in (ident, tri, blk):
                own(pool.memset(buf[:], 0.0))
            own(pool.memset(mhalf[:], -0.5))
            own(pool.memset(XL[NB:P], 0.0))
            own(pool.affine_select(out=ident[:], in_=ident[:], compare_op=ALU.not_equal, fill=1.0, base=0,
                                      pattern=[[-1, P]], channel_multiplier=1))
            for b in range(2):
                own(pool.memset(blk[b * NS:(b + 1) * NS, b * NS:(b + 1) * NS], 1.0))
            own(pool.iota(iota[:], [[1, NSLOT]], base=0, channel_multiplier=0,
                             allow_small_or_imprecise_dtypes=True))
            own(pool.iota(iotaE[:], [[1, E0]], base=-100, channel_multiplier=0,
                             allow_small_or_imprecise_dtypes=True))
            own(pool.affine_select(out=tri[:], in_=blk[:], compare_op=ALU.is_ge, fill=0.0, base=0,
                                   pattern=[[1, P]], channel_multiplier=-1))
            own(pool.memset(parity[:], 0.0))
            for k in range(BG // 2 + 1):
                own(pool.affine_select(out=parity[:], in_=parity[:], compare_op=ALU.not_equal, fill=1.0,
                                       base=-2 * k, pattern=[[-1, 2], [0, NS]], channel_multiplier=1))
            pool.nop().then_inc(s_const, 1)
            pool.wait_ge(s_w, 16 * 8)
            for name in ("WcxT", "WhhT"):
                part = WP[name]
                own(pool.tensor_copy(part[:, 0], W[name]))
                own(pool.tensor_tensor(pr[:], W[name], part[:, 0], ALU.subtract))
                own(pool.tensor_copy(part[:, 1], pr[:]))
                own(pool.tensor_tensor(part[:, 2], pr[:], part[:, 1], ALU.subtract))

            def ew_last(n):
                js = slice(n * TPG, (n + 1) * TPG)
                pool.wait_ge(S("ew_second"), n + 1)
                pool.tensor_tensor(EWp[2][:, js], EWf[:, js], EWp[1][:, js], ALU.subtract)
            for n in range(NG):
                js = slice(n * TPG, (n + 1) * TPG)
                pool.wait_ge(s_act, 2 * (n + 1))
                pool.tensor_tensor(EWf[:, js], EWf[:, js], EWp[0][:, js], ALU.subtract).then_inc(S("ew_rest"), 1)
                if n > 0:
                    ew_last(n - 1)
            ew_last(NG - 1)
            phase_end(pool, 1)

            for g in range(2):
                pool.tensor_copy(h[g][:], h0T[:, g * BG:(g + 1) * BG]).then_inc(S(f"h_ready{g}"), 1)


            pool.wait_ge(S("root_exact"), 1)
            with pool.Fori(0, NT) as j:
                own.loop(j, 12)
                c, q, ch = one(cen, j), one(xhat, j), one(cenh, j)
                rh_, rl_, rlo_ = (v[:, ds(j, 1)].to_broadcast([P, C]) for v in (rh, rl, rlo))
                own.do(pool.tensor_tensor(cl[:], c, ch, ALU.subtract))
                own.apart(pool.tensor_tensor(er[:], ch, rh_, ALU.mult))
                own.do(pool.tensor_tensor(er[:], er[:], q, ALU.subtract))
                own.apart(pool.tensor_tensor(pr[:], ch, rl_, ALU.mult))
                own.do(pool.tensor_tensor(er[:], er[:], pr[:], ALU.add))
                own.apart(pool.tensor_tensor(pr2[:], cl[:], rh_, ALU.mult))
                own.do(pool.tensor_tensor(er[:], er[:], pr2[:], ALU.add))
                own.apart(pool.tensor_tensor(pr[:], cl[:], rl_, ALU.mult))
                own.do(pool.tensor_tensor(er[:], er[:], pr[:], ALU.add))
                own.apart(pool.tensor_tensor(pr2[:], c, rlo_, ALU.mult))
                own.apart(pool.tensor_tensor(er[:], er[:], pr2[:], ALU.add))
                own.apart(pool.tensor_tensor(c, q, er[:], ALU.add))
                own.end(NT, 12)
            c4 = cen.rearrange("p j (k i) -> p i j k", k=4)
            own.apart(pool.tensor_tensor(acc4[:], c4[:, 0], c4[:, 1], ALU.add))
            with pool.Fori(2, C // 4) as i:
                own.loop(i - 2, 1)
                own.apart(pool.tensor_tensor(acc4[:], acc4[:], c4[:, bass.ds(i, 1)].rearrange("p a j k -> p (a j) k"),
                                       ALU.add))
                own.end(C // 4 - 2, 1)
            own(pool.tensor_tensor(ta, acc4[:, :, 0], acc4[:, :, 1], ALU.add))
            own(pool.tensor_tensor(tb, ta, acc4[:, :, 2], ALU.add))
            own(pool.tensor_tensor(tc, tb, acc4[:, :, 3], ALU.add))
            pool.nop().then_inc(S("quotients_summed"), 1)
            phase_end(pool, 2)
            pool_rest(pool, own)

        @block.vector
        def _(dve):
            own = Chain(dve, s_dve, wait_apart)
            tt, tsc, stt = dve.tensor_tensor, dve.tensor_scalar, dve.scalar_tensor_tensor
            x16 = X[:].rearrange("p j (i l) -> p i j l", l=16)

            dve.wait_ge(s_x, 16)
            own(tt(a16[:], x16[:, 0], x16[:, 1], ALU.add))
            for i in range(2, 8):
                own(tt(a16[:], a16[:], x16[:, i], ALU.add))
            r4 = a16[:].rearrange("p j (r k) -> p j r k", r=4)
            r2 = a8[:].rearrange("p j (r k) -> p j r k", r=2)
            own(tt(r2, r4[:, :, 0::2, :], r4[:, :, 1::2, :], ALU.add))
            own(tt(a4[:], r2[:, :, 0, :], r2[:, :, 1, :], ALU.add))
            own(tt(a2[:], a4[:, :, 0::2], a4[:, :, 1::2], ALU.add))
            own(tt(ta, a2[:, :, 0], a2[:, :, 1], ALU.add))
            own(tsc(mean, ta, 1.0 / C, None, ALU.mult))
            own(tt(cen, X[:], bc(mean, C), ALU.subtract))
            own.do(tt(sq, cen, cen, ALU.mult))
            own.sync()
            q4 = sq.rearrange("p j (k i) -> p i j k", k=4)
            own(tt(acc4[:], q4[:, 0], q4[:, 1], ALU.add))
            for i in range(2, 32):
                own(tt(acc4[:], acc4[:], q4[:, i], ALU.add))

            def sum4(dst):
                own(tt(ta, acc4[:, :, 0], acc4[:, :, 1], ALU.add))
                own(tt(tb, ta, acc4[:, :, 2], ALU.add))
                own(tt(dst, tb, acc4[:, :, 3], ALU.add))
            sum4(tc)
            own.do(tsc(var, tc, 1.0 / C, EPS, ALU.mult, ALU.add))
            own.sync()
            dve.nop().then_inc(S("var_ready"), 1)
            dve.wait_ge(S("root_ready"), 1)
            own(dve.reciprocal(rstd, std))
            for j in range(0, NT, TPG):
                tt(xhat[:, j:j + TPG], cen[:, j:j + TPG], bc(rstd[:, j:j + TPG], C), ALU.mult)\
                    .then_inc(S("xhat_ready"), 1)

            dve.wait_ge(s_w, 16 * 8)
            own.do(tt(b_h[:], COL["b_ih"], COL["b_hh"], ALU.add))

            def split(hi, lo, a):
                own(tsc(hi.bitcast(U32), a.bitcast(U32), HIGH12, None, ALU.bitwise_and))
                own(tt(lo, a, hi, ALU.subtract))

            def product_error(ah, al, bh, bl, prod, err, t):
                own(tt(err, ah, bh, ALU.mult))
                own(tt(err, err, prod, ALU.subtract))
                for u_, v_ in ((ah, bl), (al, bh), (al, bl)):
                    own(tt(t, u_, v_, ALU.mult))
                    own(tt(err, err, t, ALU.add))

            def exact_root():
                for _ in range(2):
                    own(dve.reciprocal(inv, std))
                    split(sh, sl, std)
                    own(tt(td, std, std, ALU.mult))
                    yield
                    product_error(sh, sl, sh, sl, td, te, tf)
                    yield
                    own(tt(ta, var, td, ALU.subtract))
                    own(tt(ta, ta, te, ALU.subtract))
                    own(tt(ta, ta, inv, ALU.mult))
                    own(stt(std, ta, 0.5, std, ALU.mult, ALU.add))
                yield
                own(dve.reciprocal(rstd, std))
                split(sh, sl, std)
                split(rh, rl, rstd)
                yield
                own(tt(td, std, rstd, ALU.mult))
                product_error(sh, sl, rh, rl, td, te, tf)
                yield
                own(tsc(ta, td, -1.0, 1.0, ALU.mult, ALU.add))
                own(tt(ta, ta, te, ALU.subtract))
                own(tt(rlo, rstd, ta, ALU.mult))
                own.do(tsc(cenh.bitcast(U32), cen.bitcast(U32), HIGH12, None, ALU.bitwise_and))
                own.sync()
                dve.nop().then_inc(S("root_exact"), 1)

            root = exact_root()
            for n in range(NG):
                dve.wait_ge(s_act, 2 * NG + n + 1)
                hi, lo = (xh16[:, :, n * 8:(n + 1) * 8, k] for k in range(2))
                tt(lo, xhT[:, :, n * 8:(n + 1) * 8], hi, ALU.subtract)
            for n in range(NG):
                dve.wait_ge(S("xl_ready"), n + 1)
                tt(XL[0:NB, n * 8:(n + 1) * 8, :], bank[n % 4][0:NB, :].rearrange("b (t l) -> b t l", l=NS),
                   battn[:].unsqueeze(1).to_broadcast([NB, 8, NS]), ALU.add).then_inc(S("xl_taken"), 1)
                next(root, None)
            for _ in root:
                pass
            phase_end(dve, 1)

            def pair(a, ta_, b, tb_, end, begin):
                if b is not None:
                    dve.wait_ge(S(f"exp_ready{b}"), tb_ + 1)
                    own(dve.reciprocal(rsum[b][:], esum[b][:]))
                    stt(spread[b][:], expd[b][:].unsqueeze(1).to_broadcast([BG, 2, NS]), rsum[b][:],
                        parity[:], ALU.mult, ALU.mult).then_inc(S(f"spread_ready{b}"), 1)
                if end:
                    dve.wait_ge(S(f"attended{a}"), ta_)
                    own(dve.tensor_reduce(comb[a][:], psC[a].rearrange("p (b k) -> p b k", k=2), AX_X, ALU.add))
                    tsc(comb[a][:], comb[a][:], COL["b_comb"], 0.0, ALU.add, ALU.max)\
                        .then_inc(S(f"comb_ready{a}"), 1)
                if b is not None:
                    dve.wait_ge(S(f"turned{b}"), tb_ + 1)
                    own(dve.tensor_copy(awb[b][:, :, 0], psT[b]))
                    tt(awb[b][:, :, 1], psT[b], awb[b][:, :, 0], ALU.subtract).then_inc(S(f"placed{b}"), 1)
                if begin:
                    dve.wait_ge(S(f"logits_ready{a}"), ta_ + 1)
                    dve.tensor_reduce(nmax[a][:], psL[a], AX_X, ALU.max, negate=True)\
                        .then_inc(S(f"max_ready{a}"), 1)
                if begin and end:
                    dve.wait_ge(S(f"h_kept{a}"), ta_)
                    tt(h16[a][:, 1], h[a][:], h16[a][:, 0], ALU.subtract).then_inc(S(f"h_split{a}"), 1)
            pair(0, 0, None, None, False, True)
            pair(1, 0, 0, 0, False, True)
            with dve.Fori(1, NS) as t:
                own.loop(t - 1, 6)
                pair(0, t, 1, t - 1, True, True)
                pair(1, t, 0, t, True, True)
                own.end(NS - 1, 6)
            pair(0, NS, 1, NS - 1, True, False)
            pair(1, NS, None, None, True, False)
            dve.wait_ge(S("quotients_summed"), 1)
            tsc(stopped, tc, 0.0, None, ALU.is_equal).then_inc(S("flags_ready"), 1)
            dve.wait_ge(S("flags_summed"), 1)
            own.do(tsc(keep, bank[0][:, 0:NT], 0.0, None, ALU.is_equal))
            phase_end(dve, 2)
            dve_rest(dve, own)

        @block.scalar
        def _(act):
            own = Chain(act, s_act, wait_apart)
            act.preload_act_table(ACT.Sqrt)

            def ew_second(n):
                js = slice(n * TPG, (n + 1) * TPG)
                act.wait_ge(S("ew_rest"), n + 1)
                act.activation(EWp[1][:, js], EWf[:, js], ACT.Copy).then_inc(S("ew_second"), 1)
            for n in range(NG):
                act.wait_ge(S("ew_ready"), n + 1)
                js = slice(n * TPG, (n + 1) * TPG)
                ps = bank[n % 4][:].rearrange("p (j c) -> p j c", j=TPG)
                own.do(act.activation(EWf[:, js], ps, ACT.Copy))
                own.do(act.activation(EWp[0][:, js], ps, ACT.Copy))
                if n >= 2:
                    ew_second(n - 2)
            for n in range(NG - 2, NG):
                ew_second(n)
            act.wait_ge(S("var_ready"), 1)
            act.activation(std, var, ACT.Sqrt).then_inc(S("root_ready"), 1)
            for n in range(NG):
                act.wait_ge(S("xt_ready"), n + 1)
                act.activation(xh16[:, :, n * 8:(n + 1) * 8, 0].rearrange("p t b -> p b t"),
                               bank[4 + n % 4][:].rearrange("p (b t) -> p b t", t=NS), ACT.Copy)
                own.do(act.activation(xhT[:, :, n * 8:(n + 1) * 8].rearrange("p t b -> p b t"),
                                      bank[4 + n % 4][:].rearrange("p (b t) -> p b t", t=NS), ACT.Copy))
            phase_end(act, 1)
            act.preload_act_table(ACT.Exp)

            def pair(a, ta_, b, tb_, end, begin):
                if b is not None:
                    act.wait_ge(S(f"max_ready{b}"), tb_ + 1)
                    act.activation(expd[b][:], psL[b], ACT.Exp, bias=nmax[b][:], accum_out=esum[b][:])\
                        .then_inc(S(f"exp_ready{b}"), 1)
                if end:
                    act.wait_ge(S(f"hidden_ready{a}"), ta_)
                    act.activation(h[a][:], psH[a], ACT.Tanh, bias=b_h[:]).then_inc(S(f"h_ready{a}"), 1)
                    to = HT[:, a * BG:(a + 1) * BG, ds(ta_ - 1, 1)].rearrange("p b a -> p (b a)")
                    act.activation(h16[a][:, 0], psH[a], ACT.Tanh, bias=b_h[:])
                    act.activation(to, psH[a], ACT.Tanh, bias=b_h[:]).then_inc(S(f"h_kept{a}"), 1)
            scan(act, pair)
            phase_end(act, 2)
            act_rest(act, own)

        @block.tensor
        def _(pe):
            mm = pe.matmul
            own = Chain(pe, s_pe, wait_apart)
            pe.wait_ge(s_const, 1)
            pe.wait_ge(s_ctx, 16)
            pe.wait_ge(s_w, 16 * 8)
            for n in range(NG):
                if n >= 4:
                    pe.wait_ge(s_act, 2 * (n - 3))
                for q in range(TPG):
                    j = n * TPG + q
                    last = mm(bank[n % 4][:, q * C:(q + 1) * C], ctxT[:, j * P:(j + 1) * P], W["WcaT"],
                              start=True, stop=True)
                last.then_inc(S("ew_ready"), 1)
            for n in range(NG):
                pe.wait_ge(S("xhat_ready"), n + 1)
                if n >= 4:
                    pe.wait_ge(s_act, 2 * NG + n - 3)
                for q in range(TPG):
                    last = pe.transpose(bank[4 + n % 4][:, q * C:(q + 1) * C], xhat[:, n * TPG + q, :], ident[:])
                last.then_inc(S("xt_ready"), 1)
            pe.wait_ge(s_act, 3 * NG)
            for n in range(NG):
                if n >= 4:
                    pe.wait_ge(S("xl_taken"), n - 3)
                for i in range(8):
                    last = mm(bank[n % 4][0:NB, i * NS:(i + 1) * NS], xhT[:, n * 8 + i, :], wat[:, 0, :],
                              start=True, stop=True)
                last.then_inc(S("xl_ready"), 1)
            phase_end(pe, 1)

            def attention(g, t, pairs):
                if pairs[0] == 0:
                    pe.wait_ge(S(f"placed{g}"), t + 1)
                for p in pairs:
                    for i in range(3):
                        last = mm(psC[g][:, 4 * p:4 * p + 4], EWp[i][:, g * (BG // 2) + p, :],
                                  awb[g][:, 2 * p:2 * p + 2, :].rearrange("p b k -> p (b k)"),
                                  start=False, stop=(i == 2), skip_group_check=True)
                if pairs[-1] == BG // 2 - 1:
                    last.then_inc(S(f"attended{g}"), 1)

            def pair(a, ta_, b, tb_, end, begin):
                if begin:
                    mm(psL[a], ident[:, a * BG:(a + 1) * BG], one(XL, ta_), start=True, stop=False)
                if b is not None:
                    wait_apart(pe, S(f"spread_ready{b}"), tb_ + 1)
                    pe.transpose(psT[b], spread[b][:].rearrange("b a l -> b (a l)"),
                                 ident[0:BG, 0:BG]).then_inc(S(f"turned{b}"), 1)
                if end:
                    pe.wait_ge(S(f"comb_ready{a}"), ta_)
                    mm(psH[a], W["WihT"], comb[a][:], start=False, stop=True, skip_group_check=True)\
                        .then_inc(S(f"hidden_ready{a}"), 1)
                if b is not None:
                    attention(b, tb_, range(0, 5))
                if begin:
                    pe.wait_ge(S(f"h_ready{a}"), ta_ + 1)
                    mm(psL[a], h[a][:], wat[:, 1, :], start=False, stop=True).then_inc(S(f"logits_ready{a}"), 1)
                if b is not None:
                    attention(b, tb_, range(5, BG // 2))
                if begin:
                    if end:
                        pe.wait_ge(S(f"h_split{a}"), ta_)
                        for i in range(3):
                            for k in range(2):
                                mm(psH[a], WP["WhhT"][:, i], h16[a][:, k], start=(i + k == 0), stop=False,
                                   skip_group_check=True)
                    else:
                        mm(psH[a], W["WhhT"], h[a][:], start=True, stop=False, skip_group_check=True)
                    x_t = xh16[:, ds(ta_, 1), a * BG:(a + 1) * BG].rearrange("p t b k -> p (t b k)")
                    for i in range(3):
                        mm(psC[a], WP["WcxT"][:, i], x_t, start=(i == 0), stop=False, skip_group_check=True)
            scan(pe, pair)
            pe.wait_ge(S("flags_ready"), 1)
            mm(bank[0][:, 0:NT], tri[:], stopped, start=True, stop=True).then_inc(S("flags_summed"), 1)
            phase_end(pe, 2)
            pe_rest(pe, own)


def kernel(**inputs):
    import numpy as np
    import concourse.bacc as bacc
    from concourse.bass_utils import run_bass_kernel_spmd as run

    a = {k: np.asarray(v) for k, v in inputs.items()}

    def tiles(t):
        return t.reshape(NT, P, C).transpose(1, 0, 2)

    r = "L0_xcond_"
    s = "L1_xcond_"
    Wa, Wc = a[r + "W_attn"], a[r + "W_comb"]
    squares = {"WcxT": Wc[:, :C].T, "WcaT": Wc[:, C:].T, "WihT": a[r + "W_ih"].T, "WhhT": a[r + "W_hh"].T,
               "WoT": a[r + "W_out"].T, "wk": a[s + "wk"], "wvT": a[s + "wv"].T, "wu": a[s + "wu"],
               "wqT": a[s + "wq"].T, "w1": a[s + "w1"], "w2": a[s + "w2"]}
    columns = {"b_comb": a[r + "b_comb"], "b_ih": a[r + "b_ih"], "b_hh": a[r + "b_hh"], "kv_g": a[s + "lnkv_g"],
               "kv_b": a[s + "lnkv_b"], "q_g": a[s + "lnq_g"], "q_b": a[s + "lnq_b"], "m_g": a[s + "lnm_g"],
               "m_b": a[s + "lnm_b"], "bk": a[s + "bk"], "bq": a[s + "bq"], "bv": a[s + "bv"], "b1": a[s + "b1"]}
    rowsd = {"b_out": a[r + "b_out"], "q_mu": a[s + "q_mu"], "q_logsig": a[s + "q_logsig"], "p_g": a[s + "lnp_g"],
             "p_b": a[s + "lnp_b"], "b2": a[s + "b2"], "bu": a[s + "bu"]}
    wp = a["L0_ffn_w_proj"]
    arrays = {
        "x": tiles(a["x"]),
        "ctxT": a["ctx_1024"].reshape(NB * NS, C).T,
        "ctx_tok": tiles(a["ctx_1024"]),
        "condb": tiles(np.broadcast_to(a["cond_1024"][:, None, :], (NB, NS, C))),
        "wsq": np.stack([squares[n] for n in SQ], 1),
        "wat": np.stack([Wa[:, :C].T, Wa[:, C:].T], 1),
        "cols": np.stack([columns[n].reshape(C) for n in COLS], 1),
        "rows": np.broadcast_to(np.stack([rowsd[n].reshape(C) for n in ROWS], 0)[None], (P, len(ROWS), C)),
        "battn": np.broadcast_to(a[r + "b_attn"][None], (NB, NS)),
        "h0T": a["cond_1024"].T,
        "wr0": a["L0_ffn_w_router"],
        "wr1": a["L1_ffn_router_w"].T,
        "wgf": np.concatenate([a["L0_ffn_w_gate"], a["L0_ffn_w_fc"]], 2).transpose(1, 0, 2),
        "wpj": wp.reshape(E0 // 2, 2 * H0, C).transpose(1, 0, 2),
        "wgu": np.concatenate([a["L1_ffn_w_gate"], a["L1_ffn_w_up"]], 1).transpose(2, 0, 1),
        "wdn": a["L1_ffn_w_down"].reshape(E1, C, FC, P).transpose(3, 0, 2, 1).reshape(P, E1 * FC, C),
    }
    nc = bacc.Bacc("TRN2", target_bir_lowering=False, num_devices=1)
    given, d = {}, {}
    for name, v in arrays.items():
        v = np.ascontiguousarray(v)
        given[f"{name}_dram"] = v
        d[name] = nc.dram_tensor(f"{name}_dram", v.shape, F32, kind="ExternalInput").ap()
    out = nc.dram_tensor("out_dram", (P, NT, C), F32, kind="ExternalOutput").ap()
    program(nc, d, out)
    res = run(nc, [given], core_ids=[0])
    return res.results[0]["out_dram"].transpose(1, 0, 2).reshape(NB, NS, C)
```
